# Optimizing a Trainium2 kernel written in Bass

```python
import numpy as np
import jax
import jax.numpy as jnp

def _softmax(x, axis=-1):
    return jax.nn.softmax(x, axis=axis)

def _gelu(x):
    return jax.nn.gelu(x, approximate=True)

def _silu(x):
    return jax.nn.silu(x)

def _sigmoid(x):
    return jax.nn.sigmoid(x)

def _layernorm(x, axis=-1, eps=1e-05):
    m = jnp.mean(x, axis=axis, keepdims=True)
    v = jnp.var(x, axis=axis, keepdims=True)
    return (x - m) / jnp.sqrt(v + eps)

def _scatter_add(tgt, idx, src, axis=0):
    return tgt.at[idx].add(src)

def _segment_sum(src, seg, n):
    return jax.ops.segment_sum(src, seg, n)
kernel_name = 'mk_decoder_postln_d1_seqx_r4_989347'

def setup_inputs(seed: int=0):
    np.random.seed(seed)
    _w = jnp.asarray

    def _rec_inputs():
        import jax
        import jax.numpy as jnp
        _rk = jax.random.key(seed)
        x = -0.0003929 + 0.9999 * jax.random.normal(jax.random.fold_in(_rk, 1), (32, 256, 256), jnp.float32)
        _lenS = 256 - jax.random.randint(jax.random.fold_in(_rk, 7), (32,), 0, max(1, 256 // 4) + 1, jnp.int32)
        _lenS2 = 120 - jax.random.randint(jax.random.fold_in(_rk, 8), (32,), 0, max(1, 120 // 4) + 1, jnp.int32)
        _ctx_512P = jax.random.normal(jax.random.fold_in(_rk, 11), (32, 16, 128), jnp.float32)
        _ctx_512c = jax.random.dirichlet(jax.random.fold_in(_rk, 511), 0.3 * jnp.ones((16,), jnp.float32), (32, 120))
        _ctx_512t = jnp.einsum('bsk,bkd->bsd', _ctx_512c, _ctx_512P)
        _ctx_512t = _ctx_512t * jax.lax.rsqrt(jnp.mean(jnp.square(_ctx_512t)) + 1e-12) * 0.953939
        ctx_512 = -1.39393e-06 + 0.999914 * (_ctx_512t + 0.3 * jax.random.normal(jax.random.fold_in(_rk, 611), (32, 120, 128), jnp.float32))
        return (x, ctx_512)
    x, ctx_512 = _rec_inputs()

    def _L0_attn_setup():
        import jax, jax.numpy as jnp
        import numpy as np
        B, T, C, H = (2, 512, 256, 16)
        D = C // H
        RW, RA, RG = (64, 64, 128)
        EPS = 1e-05

        def _rwkv7_scan(r, log_w, k, v, a, b):
            Bn, Tn, Hn, Dn = r.shape

            def step(S, xs):
                r_t, w_t, k_t, v_t, a_t, b_t = xs
                sa = jnp.einsum('bhij,bhj->bhi', S, a_t)
                S = S * jnp.exp(w_t)[:, :, None, :] + sa[..., None] * b_t[:, :, None, :] + v_t[..., None] * k_t[:, :, None, :]
                o_t = jnp.einsum('bhij,bhj->bhi', S, r_t)
                return (S, o_t)
            S0 = jnp.zeros((Bn, Hn, Dn, Dn), r.dtype)
            xs = tuple((jnp.swapaxes(x, 0, 1) for x in (r, log_w, k, v, a, b)))
            _, o = jax.lax.scan(step, S0, xs)
            return jnp.swapaxes(o, 0, 1)
        key = jax.random.key(seed)
        ks = iter(jax.random.split(key, 40))
        n = lambda s, sc=0.02: jax.random.normal(next(ks), s, jnp.float32) * sc
        u = lambda s: jax.random.uniform(next(ks), s, jnp.float32)
        return dict(hidden_states=jax.random.normal(next(ks), (B, T, C), jnp.float32), x_r=u((C,)), x_w=u((C,)), x_k=u((C,)), x_v=u((C,)), x_a=u((C,)), x_g=u((C,)), k_k=u((C,)), k_a=u((C,)), r_k=n((H, D), 0.1), W_r=n((C, C)), W_k=n((C, C)), W_v=n((C, C)), W_o=n((C, C)), w_lora_a=n((C, RW)), w_lora_b=n((RW, C)), w_lora_bias=n((C,), 0.1), a_lora_a=n((C, RA)), a_lora_b=n((RA, C)), a_lora_bias=jnp.zeros((C,), jnp.float32), g_lora_a=n((C, RG)), g_lora_b=n((RG, C)), g_lora_bias=jnp.zeros((C,), jnp.float32), gn_weight=jnp.ones((C,), jnp.float32), gn_bias=jnp.zeros((C,), jnp.float32))
    _L0_attn_all = _L0_attn_setup()
    _L0_attn_in = {k: v for k, v in _L0_attn_all.items() if k in ('x_r', 'x_w', 'x_k', 'x_v', 'x_a', 'x_g', 'k_k', 'k_a', 'r_k', 'W_r', 'W_k', 'W_v', 'W_o', 'w_lora_a', 'w_lora_b', 'w_lora_bias', 'a_lora_a', 'a_lora_b', 'a_lora_bias', 'g_lora_a', 'g_lora_b', 'g_lora_bias', 'gn_weight', 'gn_bias')}
    del _L0_attn_all

    def _L0_xattn_setup():
        import jax, jax.numpy as jnp
        import numpy as np
        HEADS = 16
        D_MODEL = 256
        IMG_MODEL = 128
        D_K = D_MODEL // HEADS
        key = jax.random.key(seed)
        ks = jax.random.split(key, 12)
        B, LQ, LKV = (8, 512, 256)
        s_dm = 1.0 / np.sqrt(D_MODEL)
        s_im = 1.0 / np.sqrt(IMG_MODEL)
        return {'q': jax.random.normal(ks[0], (B, LQ, D_MODEL), jnp.float32), 'k': jax.random.normal(ks[1], (B, LKV, IMG_MODEL), jnp.float32), 'v': jax.random.normal(ks[2], (B, LKV, IMG_MODEL), jnp.float32), 'Wq': jax.random.normal(ks[3], (D_MODEL, D_MODEL), jnp.float32) * s_dm, 'bq': jnp.zeros((D_MODEL,), jnp.float32), 'Wk': jax.random.normal(ks[4], (IMG_MODEL, D_MODEL), jnp.float32) * s_im, 'bk': jnp.zeros((D_MODEL,), jnp.float32), 'Wv': jax.random.normal(ks[5], (IMG_MODEL, D_MODEL), jnp.float32) * s_im, 'bv': jnp.zeros((D_MODEL,), jnp.float32), 'Wo': jax.random.normal(ks[6], (D_MODEL, D_MODEL), jnp.float32) * s_dm, 'bo': jnp.zeros((D_MODEL,), jnp.float32)}
    _L0_xattn_all = _L0_xattn_setup()
    _L0_xattn_in = {k: v for k, v in _L0_xattn_all.items() if k in ('Wq', 'bq', 'Wk', 'bk', 'Wv', 'bv', 'Wo', 'bo')}
    del _L0_xattn_all

    def _L0_ffn_setup():
        import jax, jax.numpy as jnp
        import numpy as np
        NUM_EXPERTS = 8
        TOP_K = 2
        MOE_DIM = 512

        def _moe_forward(x, moe_router, moe_w13, moe_w2):
            b, s, d = x.shape
            x_flat = x.reshape(b * s, d)
            router_logits = jnp.einsum('td,de->te', x_flat, moe_router)
            topk_logits, topk_idx = jax.lax.top_k(router_logits, TOP_K)
            topk_weights = jax.nn.softmax(topk_logits, axis=-1).astype(x.dtype)
            tokens = x_flat.shape[0]
            expert_ids = topk_idx.reshape(tokens * TOP_K)
            dispatch_weights = topk_weights.reshape(tokens * TOP_K)
            sort_idx = jnp.argsort(expert_ids, axis=0)
            token_ids = jnp.arange(tokens * TOP_K, dtype=jnp.int32) // TOP_K
            token_ids_sort = token_ids[sort_idx]
            x_sort = x_flat[token_ids_sort]
            w_sort = dispatch_weights[sort_idx].astype(x_flat.dtype)
            group_sizes = jnp.bincount(expert_ids, length=NUM_EXPERTS).astype(jnp.int32)
            w13_out = jax.lax.ragged_dot(x_sort, moe_w13, group_sizes)
            gate, up = jnp.split(w13_out, [MOE_DIM], axis=-1)
            hidden = jax.nn.silu(gate) * up
            out_dispatch = jax.lax.ragged_dot(hidden, moe_w2, group_sizes)
            out_flat = jnp.zeros_like(x_flat).at[token_ids_sort].add(out_dispatch * w_sort[:, None], mode='drop')
            return out_flat.reshape(b, s, d)
        key = jax.random.key(seed)
        k1, k2, k3, k4 = jax.random.split(key, 4)
        B, S, D = (4, 512, 256)
        x = jax.random.normal(k1, (B, S, D), dtype=jnp.float32)
        moe_router = jax.random.normal(k2, (D, NUM_EXPERTS), dtype=jnp.float32) * 0.02
        moe_w13 = jax.random.normal(k3, (NUM_EXPERTS, D, 2 * MOE_DIM), dtype=jnp.float32) * 0.02
        moe_w2 = jax.random.normal(k4, (NUM_EXPERTS, MOE_DIM, D), dtype=jnp.float32) * 0.02
        return {'x': x, 'moe_router': moe_router, 'moe_w13': moe_w13, 'moe_w2': moe_w2}
    _L0_ffn_all = _L0_ffn_setup()
    _L0_ffn_in = {k: v for k, v in _L0_ffn_all.items() if k in ('moe_router', 'moe_w13', 'moe_w2')}
    del _L0_ffn_all
    return {'x': x, 'ctx_512': ctx_512, 'L0_attn_x_r': _L0_attn_in['x_r'], 'L0_attn_x_w': _L0_attn_in['x_w'], 'L0_attn_x_k': _L0_attn_in['x_k'], 'L0_attn_x_v': _L0_attn_in['x_v'], 'L0_attn_x_a': _L0_attn_in['x_a'], 'L0_attn_x_g': _L0_attn_in['x_g'], 'L0_attn_k_k': _L0_attn_in['k_k'], 'L0_attn_k_a': _L0_attn_in['k_a'], 'L0_attn_r_k': _L0_attn_in['r_k'], 'L0_attn_W_r': _L0_attn_in['W_r'], 'L0_attn_W_k': _L0_attn_in['W_k'], 'L0_attn_W_v': _L0_attn_in['W_v'], 'L0_attn_W_o': _L0_attn_in['W_o'], 'L0_attn_w_lora_a': _L0_attn_in['w_lora_a'], 'L0_attn_w_lora_b': _L0_attn_in['w_lora_b'], 'L0_attn_w_lora_bias': _L0_attn_in['w_lora_bias'], 'L0_attn_a_lora_a': _L0_attn_in['a_lora_a'], 'L0_attn_a_lora_b': _L0_attn_in['a_lora_b'], 'L0_attn_a_lora_bias': _L0_attn_in['a_lora_bias'], 'L0_attn_g_lora_a': _L0_attn_in['g_lora_a'], 'L0_attn_g_lora_b': _L0_attn_in['g_lora_b'], 'L0_attn_g_lora_bias': _L0_attn_in['g_lora_bias'], 'L0_attn_gn_weight': _L0_attn_in['gn_weight'], 'L0_attn_gn_bias': _L0_attn_in['gn_bias'], 'L0_xattn_Wq': _L0_xattn_in['Wq'], 'L0_xattn_bq': _L0_xattn_in['bq'], 'L0_xattn_Wk': _L0_xattn_in['Wk'], 'L0_xattn_bk': _L0_xattn_in['bk'], 'L0_xattn_Wv': _L0_xattn_in['Wv'], 'L0_xattn_bv': _L0_xattn_in['bv'], 'L0_xattn_Wo': _L0_xattn_in['Wo'], 'L0_xattn_bo': _L0_xattn_in['bo'], 'L0_ffn_moe_router': _L0_ffn_in['moe_router'], 'L0_ffn_moe_w13': _L0_ffn_in['moe_w13'], 'L0_ffn_moe_w2': _L0_ffn_in['moe_w2']}

def reference(x, ctx_512, L0_attn_x_r, L0_attn_x_w, L0_attn_x_k, L0_attn_x_v, L0_attn_x_a, L0_attn_x_g, L0_attn_k_k, L0_attn_k_a, L0_attn_r_k, L0_attn_W_r, L0_attn_W_k, L0_attn_W_v, L0_attn_W_o, L0_attn_w_lora_a, L0_attn_w_lora_b, L0_attn_w_lora_bias, L0_attn_a_lora_a, L0_attn_a_lora_b, L0_attn_a_lora_bias, L0_attn_g_lora_a, L0_attn_g_lora_b, L0_attn_g_lora_bias, L0_attn_gn_weight, L0_attn_gn_bias, L0_xattn_Wq, L0_xattn_bq, L0_xattn_Wk, L0_xattn_bk, L0_xattn_Wv, L0_xattn_bv, L0_xattn_Wo, L0_xattn_bo, L0_ffn_moe_router, L0_ffn_moe_w13, L0_ffn_moe_w2):
    import jax
    import jax.numpy as jnp

    def _L0_attn_ref(hidden_states, x_r, x_w, x_k, x_v, x_a, x_g, k_k, k_a, r_k, W_r, W_k, W_v, W_o, w_lora_a, w_lora_b, w_lora_bias, a_lora_a, a_lora_b, a_lora_bias, g_lora_a, g_lora_b, g_lora_bias, gn_weight, gn_bias):
        import jax, jax.numpy as jnp
        import numpy as np
        B, T, C, H = (2, 512, 256, 16)
        D = C // H
        RW, RA, RG = (64, 64, 128)
        EPS = 1e-05

        def _rwkv7_scan(r, log_w, k, v, a, b):
            Bn, Tn, Hn, Dn = r.shape

            def step(S, xs):
                r_t, w_t, k_t, v_t, a_t, b_t = xs
                sa = jnp.einsum('bhij,bhj->bhi', S, a_t)
                S = S * jnp.exp(w_t)[:, :, None, :] + sa[..., None] * b_t[:, :, None, :] + v_t[..., None] * k_t[:, :, None, :]
                o_t = jnp.einsum('bhij,bhj->bhi', S, r_t)
                return (S, o_t)
            S0 = jnp.zeros((Bn, Hn, Dn, Dn), r.dtype)
            xs = tuple((jnp.swapaxes(x, 0, 1) for x in (r, log_w, k, v, a, b)))
            _, o = jax.lax.scan(step, S0, xs)
            return jnp.swapaxes(o, 0, 1)
        Bn, Tn, Cn = hidden_states.shape
        shifted = jnp.concatenate([jnp.zeros_like(hidden_states[:, :1]), hidden_states[:, :-1]], axis=1)
        delta = shifted - hidden_states
        xr = hidden_states + delta * x_r
        xw = hidden_states + delta * x_w
        xk = hidden_states + delta * x_k
        xv = hidden_states + delta * x_v
        xa = hidden_states + delta * x_a
        r = xr @ W_r
        log_w = -jax.nn.softplus(-(jnp.tanh(xw @ w_lora_a) @ w_lora_b + w_lora_bias)) - 0.5
        k = xk @ W_k
        v = xv @ W_v
        a = jax.nn.sigmoid(xa @ a_lora_a @ a_lora_b + a_lora_bias)
        g = jax.nn.sigmoid(r @ g_lora_a) @ g_lora_b + g_lora_bias
        kk = (k * k_k).reshape(Bn, Tn, H, D)
        kk = kk / jnp.maximum(jnp.linalg.norm(kk, axis=-1, keepdims=True), 1e-12)
        k = k * (1.0 + (a - 1.0) * k_a)
        rh = r.reshape(Bn, Tn, H, D)
        wh = log_w.reshape(Bn, Tn, H, D)
        kh = k.reshape(Bn, Tn, H, D)
        vh = v.reshape(Bn, Tn, H, D)
        ah = a.reshape(Bn, Tn, H, D)
        o = _rwkv7_scan(rh, wh, kh, vh, -kk, kk * ah)
        mu = o.mean(-1, keepdims=True)
        var = ((o - mu) ** 2).mean(-1, keepdims=True)
        o_flat = ((o - mu) * jax.lax.rsqrt(var + EPS)).reshape(Bn, Tn, C) * gn_weight + gn_bias
        bonus = ((rh * kh * r_k).sum(-1, keepdims=True) * vh).reshape(Bn, Tn, C)
        o_flat = o_flat + bonus
        return o_flat * g @ W_o

    def _L0_xattn_ref(q, k, v, Wq, bq, Wk, bk, Wv, bv, Wo, bo):
        import jax, jax.numpy as jnp
        import numpy as np
        HEADS = 16
        D_MODEL = 256
        IMG_MODEL = 128
        D_K = D_MODEL // HEADS
        B, LQ, _ = q.shape
        LKV = k.shape[1]
        qh = (q @ Wq + bq).reshape(B, LQ, HEADS, D_K).transpose(0, 2, 1, 3)
        kh = (k @ Wk + bk).reshape(B, LKV, HEADS, D_K).transpose(0, 2, 1, 3)
        vh = (v @ Wv + bv).reshape(B, LKV, HEADS, D_K).transpose(0, 2, 1, 3)
        scale = 1.0 / np.sqrt(D_K)
        scores = jnp.einsum('bhqd,bhkd->bhqk', qh, kh) * scale
        attn = jax.nn.softmax(scores, axis=-1)
        out = jnp.einsum('bhqk,bhkd->bhqd', attn, vh)
        concat = out.transpose(0, 2, 1, 3).reshape(B, LQ, D_MODEL)
        return concat @ Wo + bo

    def _L0_ffn_ref(x, moe_router, moe_w13, moe_w2):
        import jax, jax.numpy as jnp
        import numpy as np
        NUM_EXPERTS = 8
        TOP_K = 2
        MOE_DIM = 512

        def _moe_forward(x, moe_router, moe_w13, moe_w2):
            b, s, d = x.shape
            x_flat = x.reshape(b * s, d)
            router_logits = jnp.einsum('td,de->te', x_flat, moe_router)
            topk_logits, topk_idx = jax.lax.top_k(router_logits, TOP_K)
            topk_weights = jax.nn.softmax(topk_logits, axis=-1).astype(x.dtype)
            tokens = x_flat.shape[0]
            expert_ids = topk_idx.reshape(tokens * TOP_K)
            dispatch_weights = topk_weights.reshape(tokens * TOP_K)
            sort_idx = jnp.argsort(expert_ids, axis=0)
            token_ids = jnp.arange(tokens * TOP_K, dtype=jnp.int32) // TOP_K
            token_ids_sort = token_ids[sort_idx]
            x_sort = x_flat[token_ids_sort]
            w_sort = dispatch_weights[sort_idx].astype(x_flat.dtype)
            group_sizes = jnp.bincount(expert_ids, length=NUM_EXPERTS).astype(jnp.int32)
            w13_out = jax.lax.ragged_dot(x_sort, moe_w13, group_sizes)
            gate, up = jnp.split(w13_out, [MOE_DIM], axis=-1)
            hidden = jax.nn.silu(gate) * up
            out_dispatch = jax.lax.ragged_dot(hidden, moe_w2, group_sizes)
            out_flat = jnp.zeros_like(x_flat).at[token_ids_sort].add(out_dispatch * w_sort[:, None], mode='drop')
            return out_flat.reshape(b, s, d)
        return _moe_forward(x, moe_router, moe_w13, moe_w2)
    x = _layernorm(x + _L0_attn_ref(x, L0_attn_x_r, L0_attn_x_w, L0_attn_x_k, L0_attn_x_v, L0_attn_x_a, L0_attn_x_g, L0_attn_k_k, L0_attn_k_a, L0_attn_r_k, L0_attn_W_r, L0_attn_W_k, L0_attn_W_v, L0_attn_W_o, L0_attn_w_lora_a, L0_attn_w_lora_b, L0_attn_w_lora_bias, L0_attn_a_lora_a, L0_attn_a_lora_b, L0_attn_a_lora_bias, L0_attn_g_lora_a, L0_attn_g_lora_b, L0_attn_g_lora_bias, L0_attn_gn_weight, L0_attn_gn_bias), axis=-1)
    x = _layernorm(x + _L0_xattn_ref(x, ctx_512, ctx_512, L0_xattn_Wq, L0_xattn_bq, L0_xattn_Wk, L0_xattn_bk, L0_xattn_Wv, L0_xattn_bv, L0_xattn_Wo, L0_xattn_bo), axis=-1)
    x = _layernorm(x + _L0_ffn_ref(x, L0_ffn_moe_router, L0_ffn_moe_w13, L0_ffn_moe_w2), axis=-1)
    return x

_drawn_inputs = setup_inputs


def setup_inputs(seed=0):
    import zlib

    import numpy as np

    out = dict(_drawn_inputs(seed))
    spreads = {'L0_attn_a_lora_bias': (0.0, 0.8),
     'L0_attn_g_lora_bias': (0.0, 0.1),
     'L0_attn_gn_weight': (1.0, 0.6),
     'L0_attn_gn_bias': (0.0, 0.8),
     'L0_xattn_bq': (0.0, 0.371),
     'L0_xattn_bk': (0.0, 0.8),
     'L0_xattn_bv': (0.0, 0.1),
     'L0_xattn_bo': (0.0, 0.1)}
    factors = {'L0_attn_x_w': 8.0,
     'L0_attn_x_a': 8.0,
     'L0_attn_k_k': 7.114,
     'L0_attn_k_a': 4.53,
     'L0_attn_r_k': 8.0,
     'L0_attn_w_lora_a': 8.0,
     'L0_attn_w_lora_b': 8.0,
     'L0_attn_w_lora_bias': 8.0,
     'L0_attn_a_lora_a': 8.0,
     'L0_attn_a_lora_b': 8.0,
     'L0_attn_g_lora_a': 8.0,
     'L0_ffn_moe_router': 3.822,
     'L0_ffn_moe_w13': 3.322,
     'L0_ffn_moe_w2': 3.312}
    for name, (base, spread) in spreads.items():
        noise = np.random.default_rng([zlib.crc32(name.encode()), seed]).standard_normal(out[name].shape)
        drawn = base * np.exp(spread * noise) if base else spread * noise
        out[name] = jnp.asarray(drawn.astype(out[name].dtype))
    for name, factor in factors.items():
        out[name] = (out[name] * factor).astype(out[name].dtype)
    return out
```

```python
from contextlib import ExitStack

import concourse.bass as bass
from concourse import mybir

F32 = mybir.dt.float32
U32 = mybir.dt.uint32
I32 = mybir.dt.int32
ALU = mybir.AluOpType
ACT = mybir.ActivationFunctionType
AX = mybir.AxisListType

P = 128
B, T, C, H, D = 32, 256, 256, 16, 16
CC = C // P
TT = T // P
NT = B * TT
Q = P // B
HQ = H // Q
G = HQ * D
NC6 = 6
R_, W_, K_, V_, A_, B_ = range(NC6)
RL = 64
RG = 128
LKV, CD = 120, 128
NE, MD = 8, 512
SLOTT = 2 * B * T // P + NE
TB = 8
EPS = 1e-5
EXP_HALF = 0.6065306597126334


def decoder_kernel(nc, d, out):
    ctx = ExitStack()
    with ctx:
        def dram(name, shape):
            return nc.dram_tensor(name, shape, F32, kind="Internal").ap()

        coef_d = dram("coef_d", (B, Q, T, NC6 * G))
        bg_d = dram("bg_d", (B * T, 2 * C))
        o_d = dram("o_d", (B, Q, T, G))
        xs_d = dram("xs_d", (SLOTT * P, C))
        ys_d = dram("ys_d", (SLOTT * P, C))
        x2_d = dram("x2_d", (B * T, C))

        def sb(name, shape, dt=F32):
            return ctx.enter_context(nc.sbuf_tensor(name, shape, dt))

        ident = sb("ident", [P, P])
        w13 = sb("w13", [P, NE * CC * 2 * MD])
        w2 = sb("w2", [P, NE * (MD // P) * C])
        s_const = nc.alloc_semaphore("s_const")
        s_w13 = nc.alloc_semaphore("s_w13")
        s_xs0 = nc.alloc_semaphore("s_xs0")
        zero = sb("zero", [P, C])

        constants(nc, ident, zero, s_const)
        mark = nc.snapshot_sems()
        project(nc, d, ident, coef_d, bg_d)
        reuse_semaphores(nc, mark)
        scan(nc, d, ident, zero, coef_d, o_d, w13, w2, xs_d, s_w13, s_xs0)
        logits = sb("logits", [P, NT, NE])
        mark = nc.snapshot_sems()
        attend(nc, d, ident, o_d, bg_d, x2_d, logits)
        reuse_semaphores(nc, mark)
        slots = sb("slots", [P, 2, NT], U32)
        gates = sb("gates", [P, 2, NT])
        tile_expert = sb("tile_expert", [1, SLOTT], I32)
        dispatch(nc, logits, slots, gates, tile_expert)
        scatter(nc, x2_d, slots, xs_d, s_xs0)
        experts(nc, ident, w13, w2, s_w13, tile_expert, xs_d, ys_d)
        combine(nc, x2_d, slots, gates, ys_d, out)


def reuse_semaphores(nc, mark):
    nc.clear_and_free_semaphores(nc.allocated_since(mark))
    nc.all_engine_barrier()


def constants(nc, ident, zero, s_const):
    with nc.Block() as block:
        @block.gpsimd
        def _(pool):
            pool.memset(zero[:], 0.0).then_inc(s_const, 1)
            pool.memset(ident[:], 0.0).then_inc(s_const, 1)
            pool.wait_ge(s_const, 2)
            pool.affine_select(out=ident[:], in_=ident[:], compare_op=ALU.not_equal, fill=1.0, base=0,
                               pattern=[[-1, P]], channel_multiplier=1).then_inc(s_const, 1)


def project(nc, d, ident, coef_d, bg_d):
    ctx = ExitStack()
    with ctx:
        def sb(name, shape, dt=F32):
            return ctx.enter_context(nc.sbuf_tensor(name, shape, dt))

        def ps(name, shape):
            return ctx.enter_context(nc.psum_tensor(name, shape, F32))

        def sem(name):
            return nc.alloc_semaphore(name)

        MIX = ("r", "k", "v", "w", "a")
        w_rkv = sb("w_rkv", [P, 3, CC, C])
        w_lora = sb("w_lora", [P, 2, CC, 2 * RL])
        lora_raw = sb("lora_raw", [P, CC, 2 * RL])
        mix_w = sb("mix_w", [P, len(MIX), CC])
        omx = sb("omx", [P, len(MIX), CC])
        wa_b = sb("wa_b", [P, 2 * C])
        wr_t = sb("wr_t", [P, CC, C])
        ga = sb("ga", [P, CC, RG])
        w_rg = sb("w_rg", [P, CC, RG])
        g_b = sb("g_b", [P, C])
        bias_wa = sb("bias_wa", [P, 2, C])
        bias_g = sb("bias_g", [P, C])
        kk_row = sb("kk_row", [P, C])
        ka_row = sb("ka_row", [P, C])
        oma_row = sb("oma_row", [P, C])
        rk_row = sb("rk_row", [P, C])

        x_in = sb("x_in", [P, 2, TT, C])
        x_t = sb("x_t", [P, 2, CC, 1 + T])
        delta = sb("delta", [P, CC, T])
        mixed = sb("mixed", [P, 2, 3, CC, T])
        th = sb("th", [P, 2, T])
        sg = sb("sg", [P, 2, T])
        za = sb("za", [P, TT, 2 * C])
        wa = sb("wa", [P, TT, 2 * C])
        kk0 = sb("kk0", [P, TT, C])
        sq = sb("sq", [P, TT, C])
        ss = sb("ss", [P, TT, H])
        inv = sb("inv", [P, TT, H])
        nt = sb("nt", [P, TT, H])
        kk = sb("kk", [P, TT, C])
        u = sb("u", [P, TT, C])
        rr = sb("rr", [P, TT, C])
        bs = sb("bs", [P, TT, H])
        coef = sb("coef", [P, TT, Q, NC6, G])
        bg = sb("bg", [P, TT, 2, C])

        xt_p = ps("xt_p", [P, CC, T])
        l_p = ps("l_p", [P, 2, T])
        rv_p = [ps(f"rv_p{i}", [P, 2, C]) for i in range(TT)]
        kg_p = [ps(f"kg_p{i}", [P, 2, C]) for i in range(TT)]
        wa_p = [ps(f"wa_p{i}", [P, 2 * C]) for i in range(TT)]

        wld, wload = sem("p_wld"), sem("p_wload")
        zeroed, omx_ok, prep, wrt, wrt_ok, wrg, wrg_ok = (
            sem(n) for n in ("p_zeroed", "p_omx", "p_prep", "p_wrt", "p_wrt_ok", "p_wrg", "p_wrg_ok"))
        x_ld = [sem(f"p_x_ld{i}") for i in range(2)]
        stored = [sem(f"p_stored{i}") for i in range(TT)]
        (xt, xt_ok, dlt, mix_ok, lora, th_ok, pe_done, rv, g_m, wa_m, za_ok, kk0_ok, sq_ok, ss_ok, kk_ok,
         k_ok, g_ok, bs_ok, rv_ok, wa_ok, neg_ok, u0_ok, u_ok, rr0_ok, rr_ok, b_ok, bonus_ok) = (
            sem("p_" + n) for n in (
                "xt", "xt_ok", "dlt", "mix_ok", "lora", "th_ok", "pe_done", "rv", "g_m", "wa_m", "za_ok", "kk0_ok",
                "sq_ok", "ss_ok", "kk_ok", "k_ok", "g_ok", "bs_ok", "rv_ok", "wa_ok", "neg_ok",
                "u0_ok", "u_ok", "rr0_ok", "rr_ok", "b_ok", "bonus_ok"))
        newton, NEWTON = sem("p_newton"), 12

        def vec(name):
            v = d["L0_attn_" + name]
            return v if len(v.shape) == 1 else v.rearrange("h d -> (h d)")

        def heads(ap):
            return ap.rearrange("p (h e) -> p h e", h=H)

        def over(ap):
            return ap.unsqueeze(2).broadcast_to([P, H, D])

        def hq(ap):
            return ap.rearrange("p (q g) -> p q g", q=Q)

        with nc.Block() as block:
            @block.tensor
            def _(pe):
                pe.wait_ge(wload, 1)
                for m in range(CC):
                    for c in range(CC):
                        last = pe.transpose(xt_p[:, m, c * P:(c + 1) * P], w_rkv[:, 0, c, m * P:(m + 1) * P], ident[:])
                last.then_inc(wrt, 1)
                pe.wait_ge(wrt_ok, 1)
                for c in range(CC):
                    for m in range(CC):
                        last = pe.matmul(l_p[:, 0, c * RG:(c + 1) * RG], wr_t[:, m, c * P:(c + 1) * P], ga[:, m],
                                         start=m == 0, stop=m == CC - 1)
                last.then_inc(wrg, 1)
                pe.wait_ge(wrg_ok, 1)
                pe.wait_ge(prep, 1)
                with pe.Fori(0, B // 2) as i:
                    for s in range(2):
                        b = i * 2 + s
                        b1 = pe.snap(b + 1)
                        pe.wait_ge(x_ld[s], (i + 1) * 16)
                        pe.wait_ge(xt_ok, b)
                        for t in range(TT):
                            for c in range(CC):
                                last = pe.transpose(xt_p[:, c, t * P:(t + 1) * P], x_in[:, s, t, c * P:(c + 1) * P], ident[:])
                        last.then_inc(xt, 1)
                        pe.wait_ge(xt_ok, b1)
                        pe.wait_ge(th_ok, b * 2)
                        for sh in range(2):
                            for c in range(CC):
                                pe.matmul(l_p[:, 0], w_lora[:, sh, c], x_t[:, s, c, 1 - sh:1 - sh + T],
                                          start=sh == 0 and c == 0, stop=sh == 1 and c == CC - 1)
                        pe.wait_ge(mix_ok, b1)
                        for c in range(CC):
                            last = pe.matmul(l_p[:, 1], w_rg[:, c], mixed[:, s, 0, c], start=c == 0, stop=c == CC - 1)
                        last.then_inc(lora, 1)
                        for t in range(TT):
                            tok = slice(t * P, (t + 1) * P)
                            pe.wait_ge(stored[t], b1 * 32)
                            for n, bank, done in ((1, kg_p[t][:, 0], None), (0, rv_p[t][:, 0], None), (2, rv_p[t][:, 1], rv)):
                                for c in range(CC):
                                    last = pe.matmul(bank, mixed[:, s, n, c, tok], w_rkv[:, n, c],
                                                     start=c == 0, stop=c == CC - 1)
                                if done is not None:
                                    last.then_inc(done, 1)
                            pe.wait_ge(th_ok, b * 2 + 2)
                            pe.matmul(kg_p[t][:, 1], sg[:, s, tok], g_b[:], start=True, stop=True).then_inc(g_m, 1)
                            last = pe.matmul(wa_p[t][:], th[:, s, tok], wa_b[:], start=True, stop=True)
                            last.then_inc(wa_m, 1)
                        pe.sem_inc(pe_done, 1)

            @block.scalar
            def _(act):
                act.wait_ge(wrt, 1)
                act.copy(wr_t[:], xt_p[:]).then_inc(wrt_ok, 1)
                act.wait_ge(wrg, 1)
                act.copy(w_rg[:].rearrange("p c n -> p (c n)"), l_p[:, 0]).then_inc(wrg_ok, 1)
                act.wait_ge(zeroed, 2)
                with act.Fori(0, B // 2) as i:
                    for s in range(2):
                        b = i * 2 + s
                        b1 = act.snap(b + 1)
                        act.wait_ge(xt, b1)
                        act.wait_ge(pe_done, b1)
                        act.copy(x_t[:, s, :, 1:1 + T], xt_p[:]).then_inc(xt_ok, 1)
                        act.wait_ge(lora, b1)
                        act.activation(th[0:RL, s], l_p[0:RL, 0], ACT.Tanh)
                        act.copy(th[RL:P, s], l_p[RL:P, 0]).then_inc(th_ok, 1)
                        act.activation(sg[:, s], l_p[:, 1], ACT.Sigmoid).then_inc(th_ok, 1)
                        n = [act.snap(b * TT + t + 1) for t in range(TT)]
                        for t in range(TT):
                            act.wait_ge(rv, n[t])
                            act.wait_ge(stored[t], b1 * 32)
                            act.copy(coef[:, t, :, R_], hq(rv_p[t][:, 0]))
                            act.copy(coef[:, t, :, V_], hq(rv_p[t][:, 1])).then_inc(rv_ok, 1)
                            act.wait_ge(kk0_ok, n[t])
                            act.activation(sq[:, t], kk0[:, t], ACT.Square).then_inc(sq_ok, 1)
                            act.wait_ge(za_ok, n[t])
                            act.activation(wa[:, t], za[:, t], ACT.Sigmoid).then_inc(wa_ok, 1)
                        for t in range(TT):
                            act.wait_ge(wa_ok, n[t])
                            act.mul(coef[:, t, :, W_], hq(wa[:, t, 0:C]), EXP_HALF)
                        for t in range(TT):
                            act.wait_ge(kk_ok, n[t])
                            act.mul(coef[:, t, :, A_], hq(kk[:, t]), -1.0).then_inc(neg_ok, 1)

            @block.sync
            def _(sp):
                for n, name in enumerate(("W_r", "W_k", "W_v")):
                    sp.dma_start(w_rkv[:, n], d["L0_attn_" + name].rearrange("(c p) n -> p c n", p=P)).then_inc(wld, 16)
                sp.dma_start(lora_raw[:, :, 0:RL], d["L0_attn_w_lora_a"].rearrange("(c p) n -> p c n", p=P)).then_inc(wld, 16)
                sp.dma_start(lora_raw[:, :, RL:], d["L0_attn_a_lora_a"].rearrange("(c p) n -> p c n", p=P)).then_inc(wld, 16)
                sp.dma_start(ga[:], d["L0_attn_g_lora_a"].rearrange("(c p) n -> p c n", p=P)).then_inc(wld, 16)
                sp.dma_start(g_b[:], d["L0_attn_g_lora_b"]).then_inc(wld, 16)
                for n, m in enumerate(MIX):
                    sp.dma_start(mix_w[:, n], vec("x_" + m).rearrange("(c p) -> p c", p=P), allow_slow_non_contiguous=True).then_inc(wld, 16)
                for t, name in ((bias_wa[:, 0], "w_lora_bias"), (bias_wa[:, 1], "a_lora_bias"), (bias_g[:], "g_lora_bias"),
                                (kk_row[:], "k_k"), (ka_row[:], "k_a"), (rk_row[:], "r_k")):
                    sp.dma_start(t, vec(name).unsqueeze(0).broadcast_to([P, C])).then_inc(wld, 16)
                sp.wait_ge(zeroed, 1)
                sp.dma_start(wa_b[0:RL, 0:C], d["L0_attn_w_lora_b"]).then_inc(wld, 16)
                sp.dma_start(wa_b[RL:2 * RL, C:], d["L0_attn_a_lora_b"]).then_inc(wld, 16)
                sp.wait_ge(wld, 16 * 20)
                sp.sem_inc(wload, 1)
                def load_x(b, s, transposed):
                    sp.wait_ge(xt, transposed)
                    sp.dma_start(x_in[:, s], d["x"][bass.ds(b, 1)].rearrange("o (t p) c -> p (o t) c", p=P)).then_inc(x_ld[s], 16)

                def store(b):
                    for t in range(TT):
                        n1 = b * TT + t + 1
                        sp.wait_ge(neg_ok, n1)
                        sp.wait_ge(k_ok, n1)
                        sp.wait_ge(b_ok, n1)
                        sp.dma_start(coef_d[bass.ds(b, 1), :, t * P:(t + 1) * P].rearrange("o q t f -> t (o q) f"),
                                     coef[:, t].rearrange("p q n g -> p q (n g)")).then_inc(stored[t], 16)
                        sp.wait_ge(g_ok, n1)
                        sp.wait_ge(bonus_ok, n1)
                        sp.dma_start(bg_d[bass.ds((b * TT + t) * P, P)], bg[:, t].rearrange("p k c -> p (k c)")).then_inc(stored[t], 16)

                load_x(0, 0, 0)
                with sp.Fori(0, B // 2 - 1) as i:
                    load_x(i * 2 + 1, 1, i * 2)
                    store(i * 2)
                    load_x(i * 2 + 2, 0, i * 2 + 1)
                    store(i * 2 + 1)
                load_x(B - 1, 1, B - 2)
                store(B - 2)
                store(B - 1)
                for t in range(TT):
                    sp.wait_ge(stored[t], 32 * (B + 1))

            @block.vector
            def _(dve):
                dve.memset(wa_b[:], 0.0).then_inc(zeroed, 1)
                dve.memset(x_t[:, :, :, 0:1], 0.0).then_inc(zeroed, 1)
                for t in range(TT):
                    dve.sem_inc(stored[t], 32)
                dve.sem_inc(pe_done, 2)
                dve.wait_ge(wload, 1)
                dve.tensor_scalar(omx[:], mix_w[:], -1.0, 1.0, ALU.mult, ALU.add).then_inc(omx_ok, 1)
                dve.tensor_scalar(oma_row[:], ka_row[:], -1.0, 1.0, ALU.mult, ALU.add)
                dve.wait_ge(omx_ok, 1)
                for c in range(CC):
                    for n, col in ((3, slice(0, RL)), (4, slice(RL, 2 * RL))):
                        dve.tensor_scalar(w_lora[:, 0, c, col], lora_raw[:, c, col], omx[:, n, c:c + 1], None, ALU.mult)
                        last = dve.tensor_scalar(w_lora[:, 1, c, col], lora_raw[:, c, col], mix_w[:, n, c:c + 1], None, ALU.mult)
                last.then_inc(prep, 1)
                with dve.Fori(0, B // 2) as i:
                    for s in range(2):
                        b = i * 2 + s
                        b1 = dve.snap(b + 1)
                        dve.wait_ge(xt_ok, b1)
                        dve.wait_ge(mix_ok, b)
                        dve.tensor_tensor(delta[:], x_t[:, s, :, 0:T], x_t[:, s, :, 1:1 + T], ALU.subtract).then_inc(dlt, 1)
                        dve.wait_ge(dlt, b1)
                        for n in range(3):
                            for c in range(CC):
                                last = dve.scalar_tensor_tensor(mixed[:, s, n, c], delta[:, c], mix_w[:, n, c:c + 1],
                                                                x_t[:, s, c, 1:1 + T], ALU.mult, ALU.add)
                        last.then_inc(mix_ok, 1)
                        n = [dve.snap(b * TT + t + 1) for t in range(TT)]
                        for t in range(TT):
                            dve.wait_ge(stored[t], b1 * 32)
                            dve.wait_ge(g_m, n[t])
                            dve.tensor_tensor(kk0[:, t], kg_p[t][:, 0], kk_row[:], ALU.mult).then_inc(kk0_ok, 1)
                            dve.tensor_tensor(bg[:, t, 1], kg_p[t][:, 1], bias_g[:], ALU.add).then_inc(g_ok, 1)
                            dve.wait_ge(wa_m, n[t])
                            dve.tensor_tensor(za[:, t], wa_p[t][:], bias_wa[:].rearrange("p k c -> p (k c)"), ALU.add).then_inc(za_ok, 1)
                        for t in range(TT):
                            dve.wait_ge(sq_ok, n[t])
                            dve.tensor_reduce(ss[:, t], heads(sq[:, t]), AX.X, ALU.add).then_inc(ss_ok, 1)
                        dve.wait_ge(ss_ok, b * TT + TT)
                        dve.tensor_scalar(ss[:], ss[:], 1e-24, None, ALU.max).then_inc(newton, 1)
                        dve.wait_ge(newton, b * NEWTON + 1)
                        dve.tensor_scalar(inv[:].bitcast(I32), ss[:].bitcast(I32), 1, None, ALU.arith_shift_right).then_inc(newton, 1)
                        dve.wait_ge(newton, b * NEWTON + 2)
                        dve.tensor_scalar(inv[:].bitcast(I32), inv[:].bitcast(I32), -1.0, float(0x5f3759df), ALU.mult, ALU.add).then_inc(newton, 1)
                        for k in range(3):
                            dve.wait_ge(newton, b * NEWTON + 3 * k + 3)
                            dve.tensor_tensor(nt[:], inv[:], inv[:], ALU.mult).then_inc(newton, 1)
                            dve.wait_ge(newton, b * NEWTON + 3 * k + 4)
                            dve.scalar_tensor_tensor(nt[:], nt[:], -0.5, ss[:], ALU.mult, ALU.mult).then_inc(newton, 1)
                            dve.wait_ge(newton, b * NEWTON + 3 * k + 5)
                            dve.scalar_tensor_tensor(inv[:], nt[:], 1.5, inv[:], ALU.add, ALU.mult).then_inc(newton, 1)
                        dve.wait_ge(newton, b1 * NEWTON)
                        for t in range(TT):
                            dve.tensor_tensor(heads(kk[:, t]), heads(kk0[:, t]), over(inv[:, t]), ALU.mult).then_inc(kk_ok, 1)
                        for t in range(TT):
                            dve.wait_ge(u_ok, n[t])
                            dve.tensor_tensor(coef[:, t, :, K_], hq(kg_p[t][:, 0]), hq(u[:, t]), ALU.mult).then_inc(k_ok, 1)
                        for t in range(TT):
                            dve.wait_ge(rr_ok, n[t])
                            dve.tensor_reduce(bs[:, t], heads(rr[:, t]), AX.X, ALU.add).then_inc(bs_ok, 1)

            @block.gpsimd
            def _(pool):
                pool.wait_ge(prep, 1)
                with pool.Fori(0, B // 2) as i:
                    for s in range(2):
                        b = i * 2 + s
                        n = [pool.snap(b * TT + t + 1) for t in range(TT)]
                        a = [wa[:, t, C:2 * C] for t in range(TT)]
                        for t in range(TT):
                            pool.wait_ge(rv_ok, n[t])
                            pool.tensor_tensor(hq(rr[:, t]), coef[:, t, :, R_], hq(rk_row[:]), ALU.mult).then_inc(rr0_ok, 1)
                        for t in range(TT):
                            pool.wait_ge(wa_ok, n[t])
                            pool.tensor_tensor(u[:, t], a[t], ka_row[:], ALU.mult).then_inc(u0_ok, 1)
                        for t in range(TT):
                            pool.wait_ge(u0_ok, n[t])
                            pool.tensor_tensor(u[:, t], u[:, t], oma_row[:], ALU.add).then_inc(u_ok, 1)
                        for t in range(TT):
                            pool.wait_ge(kk_ok, n[t])
                            pool.tensor_tensor(coef[:, t, :, B_], hq(kk[:, t]), hq(a[t]), ALU.mult).then_inc(b_ok, 1)
                        for t in range(TT):
                            pool.wait_ge(rr0_ok, n[t])
                            pool.wait_ge(k_ok, n[t])
                            pool.tensor_tensor(hq(rr[:, t]), hq(rr[:, t]), coef[:, t, :, K_], ALU.mult).then_inc(rr_ok, 1)
                        for t in range(TT):
                            pool.wait_ge(bs_ok, n[t])
                            pool.tensor_tensor(bg[:, t, 0].rearrange("p (q h e) -> p q h e", q=Q, h=HQ),
                                               coef[:, t, :, V_].rearrange("p q (h e) -> p q h e", h=HQ),
                                               bs[:, t].rearrange("p (q h) -> p q h", q=Q).unsqueeze(3).broadcast_to([P, Q, HQ, D]),
                                               ALU.mult).then_inc(bonus_ok, 1)


def scan(nc, d, ident, zero, coef_d, o_d, w13, w2, xs_d, s_w13, s_xs0):
    ctx = ExitStack()
    with ctx:
        def sb(name, shape, dt=F32):
            return ctx.enter_context(nc.sbuf_tensor(name, shape, dt))

        def sem(name):
            return nc.alloc_semaphore(name)

        CS = 3
        NBK = T // TB
        coef = sb("sc_coef", [P, 2, TB, NC6, G])
        state = sb("sc_state", [P, 2, D, G])
        ta = sb("sc_ta", [P, D, G])
        sa = sb("sc_sa", [P, G])
        y = sb("sc_y", [P, 2, D, G])
        x = sb("sc_x", [P, 2, D, G])
        z = sb("sc_z", [P, D, G])
        xy = sb("sc_xy", [P, D, G])
        r = sb("sc_r", [P, 2, D, G])
        o_sb = sb("sc_o", [P, 2, TB, G])
        o_p = [ctx.enter_context(nc.psum_tensor(f"sc_o_p{i}", [P, 512], F32)) for i in range(2)]
        ld = [sem(f"c_ld{i}") for i in range(2)]
        stored = [sem(f"c_stored{i}") for i in range(2)]
        used = sem("c_used")
        ta_ok, sa_ok, y_ok, x_ok, yx_ok, z_ok, s_ok, r_ok, o_ok, o_out = (
            sem("c_" + n) for n in ("ta", "sa", "y", "x", "yx", "z", "s", "r", "o", "o_out"))
        w13_v = d["L0_ffn_moe_w13"].rearrange("e k n -> (e k) n")
        w2_v = d["L0_ffn_moe_w2"].rearrange("e k n -> (e k) n")
        xs_v = xs_d.rearrange("(n p) c -> p n c", p=P)
        ZN = SLOTT // (NBK // 2)
        assert NE * CC == NBK // 2 and NE * MD // P == NBK and 0 < SLOTT - ZN * NBK // 2
        coef_v = coef_d.rearrange("b q t f -> (b q) t f")
        o_v = o_d.rearrange("b q t g -> (b q) t g")

        def heads(ap):
            return ap.rearrange("p j (h i) -> p j h i", h=HQ)

        def by_j(s, k, c):
            return coef[:, s, k, c].rearrange("p (h j) -> p j h", j=D).unsqueeze(3).broadcast_to([P, D, HQ, D])

        def by_i(ap):
            return ap.rearrange("p (h i) -> p h i", h=HQ).unsqueeze(1).broadcast_to([P, D, HQ, D])

        with nc.Block() as block:
            @block.sync
            def _(sp):
                with sp.Fori(0, NBK // 2) as i:
                    for s in range(2):
                        blk = i * 2 + s
                        sp.wait_ge(used, blk + 1)
                        sp.dma_start(coef[:, s].rearrange("p t n g -> p t (n g)"), coef_v[:, bass.ds(blk * TB, TB)]).then_inc(ld[s], 16)
                    sp.dma_start(w13[:, bass.ds(i * (2 * MD), 2 * MD)], w13_v[bass.ds(i * P, P)]).then_inc(s_w13, 16)
                    for k in range(2):
                        sp.dma_start(w2[:, bass.ds((i * 2 + k) * C, C)], w2_v[bass.ds((i * 2 + k) * P, P)]).then_inc(s_w13, 16)
                    sp.dma_start(xs_v[:, bass.ds(i * ZN, ZN)], zero[:].unsqueeze(1).broadcast_to([P, ZN, C])).then_inc(s_xs0, 16)
                sp.dma_start(xs_v[:, ZN * NBK // 2:], zero[:].unsqueeze(1).broadcast_to([P, SLOTT - ZN * NBK // 2, C])).then_inc(s_xs0, 16)

            @block.gpsimd
            def _(pool):
                def read_out(s, k, t, n):
                    pool.wait_ge(o_ok, n)
                    pool.tensor_tensor(heads(r[:, k % 2]), heads(state[:, k % 2]), by_j(s, k, R_), ALU.mult).then_inc(r_ok, 1)

                def steps(blk, s, first):
                    pool.wait_ge(ld[s], (blk // 2 + 1) * 16 if first else (blk + 1) * 16)
                    for k in range(TB):
                        p = k % 2
                        t = k + s * TB if first else pool.snap((blk * 2 + s) * TB + k)
                        t1 = t + 1 if first else pool.snap(t + 1)
                        pool.wait_ge(yx_ok, t)
                        pool.tensor_tensor(heads(x[:, p]), by_i(coef[:, s, k, V_]), by_j(s, k, K_), ALU.mult).then_inc(x_ok, 1)
                        pool.wait_ge(s_ok, t1)
                        pool.tensor_tensor(heads(y[:, p]), heads(state[:, 1 - p]), by_j(s, k, W_), ALU.mult).then_inc(y_ok, 1)
                        if not (first and s == 0 and k == 0):
                            read_out(s if k else 1 - s, (k - 1) % TB, t - 1, t - 1)
                            if k == 0:
                                pool.wait_ge(r_ok, t)
                                pool.sem_inc(used, 1)

                pool.sem_inc(used, 2)
                for s in range(2):
                    steps(s, s, True)
                with pool.Fori(1, NBK // 2) as i:
                    for s in range(2):
                        steps(i, s, False)
                pool.wait_ge(s_ok, T + 1)
                read_out(1, TB - 1, T - 1, T - 1)

            @block.vector
            def _(dve):
                dve.memset(state[:], 0.0).then_inc(s_ok, 1)
                with dve.Fori(0, NBK // 2) as i:
                    for s in range(2):
                        dve.wait_ge(ld[s], (i + 1) * 16)
                        for k in range(TB):
                            p = k % 2
                            t = dve.snap((i * 2 + s) * TB + k)
                            t1 = dve.snap(t + 1)
                            dve.wait_ge(s_ok, t1)
                            dve.tensor_tensor(heads(ta[:]), heads(state[:, 1 - p]), by_j(s, k, A_), ALU.mult).then_inc(ta_ok, 1)
                            dve.wait_ge(ta_ok, t1)
                            dve.tensor_reduce(sa[:], ta[:].rearrange("p j g -> p g j"), AX.X, ALU.add).then_inc(sa_ok, 1)
                            dve.wait_ge(x_ok, t1)
                            dve.wait_ge(y_ok, t1)
                            dve.tensor_tensor(xy[:], x[:, p], y[:, p], ALU.add).then_inc(yx_ok, 1)
                            dve.wait_ge(sa_ok, t1)
                            dve.tensor_tensor(heads(z[:]), by_i(sa[:]), by_j(s, k, B_), ALU.mult).then_inc(z_ok, 1)
                            dve.wait_ge(z_ok, t1)

                            dve.tensor_tensor(state[:, p], xy[:], z[:], ALU.add).then_inc(s_ok, 1)

            @block.tensor
            def _(pe):
                with pe.Fori(0, NBK // 2) as i:
                    for s in range(2):
                        for k in range(TB):
                            p = k % 2
                            t = pe.snap((i * 2 + s) * TB + k)
                            pe.wait_ge(r_ok, t + 1)
                            pe.wait_ge(o_out, t)
                            for j in range(D):
                                last = pe.matmul(o_p[p][:, 0:G], ident[:], r[:, p, j], start=j == 0, stop=j == D - 1)
                            last.then_inc(o_ok, 1)

            @block.scalar
            def _(act):
                for s in range(2):
                    act.sem_inc(stored[s], 16)
                with act.Fori(0, NBK // 2) as i:
                    for s in range(2):
                        act.wait_ge(stored[s], (i + 1) * 16)
                        for k in range(TB):
                            t = act.snap((i * 2 + s) * TB + k)
                            act.wait_ge(o_ok, t + 1)
                            act.copy(o_sb[:, s, k], o_p[k % 2][:, 0:G]).then_inc(o_out, 1)
                        act.wait_ge(o_out, (i * 2 + s + 1) * TB)
                        act.dma_start(o_v[:, bass.ds((i * 2 + s) * TB, TB)], o_sb[:, s]).then_inc(stored[s], 16)
                for s in range(2):
                    act.wait_ge(stored[s], 16 * (NBK // 2 + 1))


def attend(nc, d, ident, o_d, bg_d, x2_d, logits):
    ctx = ExitStack()
    with ctx:
        def sb(name, shape, dt=F32):
            return ctx.enter_context(nc.sbuf_tensor(name, shape, dt))

        def ps(name, shape):
            return ctx.enter_context(nc.psum_tensor(name, shape, F32))

        def sem(name):
            return nc.alloc_semaphore(name)

        HG = 4
        DP = P // HG
        w_o = sb("w_o", [P, CC, C])
        w_q = sb("w_q", [P, CC, HG, HG, DP])
        w_k = sb("w_k", [CD, HG, HG, DP])
        w_v = sb("w_v", [CD, C])
        w_xo = sb("w_xo", [P, CC, C])
        router = sb("router", [P, CC, NE])
        q_raw = sb("q_raw", [P, CC, C])
        k_raw = sb("k_raw", [CD, C])
        b_q = sb("b_q", [P, HG])
        b_k = sb("b_k", [P, HG])
        b_ks = sb("b_ks", [P, HG])
        bv_row = sb("bv_row", [P, C])
        bo_row = sb("bo_row", [P, C])
        gw_row = sb("gw_row", [P, C])
        gb_row = sb("gb_row", [P, C])

        o_in = sb("o_in", [P, TT, Q, G])
        bg_in = sb("bg_in", [P, TT, 2, C])
        x_in = sb("a_x_in", [P, TT, C])
        ctx_in = sb("ctx_in", [LKV, CD])
        ctx_t = sb("ctx_t", [CD, LKV])
        k_t = sb("k_t", [P, HG, LKV])
        v_aug = sb("v_aug", [LKV, H, D + 1])
        mu = sb("mu", [P, TT, H])
        oc = sb("oc", [P, TT, C])
        sq = sb("a_sq", [P, TT, C])
        ss = sb("a_ss", [P, TT, H])
        rs = sb("rs", [P, TT, H])
        zz = sb("zz", [P, TT, C])
        flip = sb("flip", [P, TT, CC, P])
        y1 = sb("y1", [P, TT, C])
        bn6 = sb("bn6", [P, TT, 6])
        mv = sb("mv", [P, TT, 2])
        rstd = sb("rstd", [P, TT, 1])
        std = sb("std", [P, TT, 1])
        sd = sb("sd", [P, TT, H])
        eps = sb("eps", [P, 1])
        x1 = sb("x1", [P, TT, C])
        x1b = sb("x1b", [P, TT, C])
        x2 = sb("x2", [P, TT, C])
        q_t = sb("q_t", [P, TT, HG, P])
        mx = sb("mx", [P, TT, HG, HG])
        pr = sb("pr", [P, TT, HG, HG, LKV])
        p_t = sb("p_t", [LKV, TT, H, P])
        rden = sb("rden", [P, TT, H])
        at = sb("at", [P, TT, C])

        sc_p = ps("sc_p", [P, HG, 512])
        pt_p = [ps(f"pt_p{i}", [P, HG, P]) for i in range(2)]
        m_p = [ps(f"m_p{i}", [P, 512]) for i in range(TT)]

        wld, cld, zeroed, wload, prep = (sem("a_" + n) for n in ("wld", "cld", "zeroed", "wload", "prep"))
        ld_o, ld_bg, ld_x, x2_st = (sem("a_" + n) for n in ("ld_o", "ld_bg", "ld_x", "x2_st"))
        (ctx_m, ctx_ok, k_m, k_ok, v_m, v_ok, mu_ok, oc_ok, sq_ok, ss_ok, rs_ok, on_ok, z1, z2, z3, z_ok,
         zt, zt_ok, y_m, y_ok, bn_ok, mv_ok, rstd_ok, x1_ok, x1t, x1t_ok, x1b_ok, q_m, q_ok, sc, mx_ok, sub_ok,
         pr_ok, ptm, ptc, pv, rd_ok, at_ok, att, att_ok, y2_m, y2_ok, bn2_ok, mv2_ok, rstd2_ok, x2_ok, x2t, x2t_ok,
         lg_m, lg_ok, sd_ok, std_ok, std2_ok) = (
            sem("a_" + n) for n in (
                "ctx_m ctx_ok k_m k_ok v_m v_ok mu_ok oc_ok sq_ok ss_ok rs_ok on_ok z1 z2 z3 z_ok "
                "zt zt_ok y_m y_ok bn_ok mv_ok rstd_ok x1_ok x1t x1t_ok x1b_ok q_m q_ok sc mx_ok sub_ok "
                "pr_ok ptm ptc pv rd_ok at_ok att att_ok y2_m y2_ok bn2_ok mv2_ok rstd2_ok x2_ok x2t x2t_ok "
                "lg_m lg_ok sd_ok std_ok std2_ok").split())
        passed = sem("a_passed")

        def row(name):
            return d[name].unsqueeze(0).broadcast_to([P, C])

        def heads(ap):
            return ap.rearrange("p (h e) -> p h e", h=H)

        def over(ap):
            return ap.unsqueeze(2).broadcast_to([P, H, D])

        loads = [(w_o[:], d["L0_attn_W_o"].rearrange("(c p) n -> p c n", p=P)),
                 (q_raw[:], d["L0_xattn_Wq"].rearrange("(c p) n -> p c n", p=P)),
                 (k_raw[:], d["L0_xattn_Wk"]), (w_v[:], d["L0_xattn_Wv"]),
                 (w_xo[:], d["L0_xattn_Wo"].rearrange("(c p) n -> p c n", p=P)),
                 (router[:], d["L0_ffn_moe_router"].rearrange("(c p) n -> p c n", p=P)),
                 (bv_row[:], row("L0_xattn_bv")), (bo_row[:], row("L0_xattn_bo")),
                 (gw_row[:], row("L0_attn_gn_weight")), (gb_row[:], row("L0_attn_gn_bias"))]
        for h in range(HG):
            for t, name in ((b_q, "L0_xattn_bq"), (b_k, "L0_xattn_bk")):
                loads.append((t[h * DP:h * DP + D, :], d[name].rearrange("(g h e) -> h e g", g=HG, h=HG)[h]))

        with nc.Block() as block:
            @block.sync
            def _(sp):
                sp.wait_ge(zeroed, 1)
                for dst, src in loads:
                    sp.dma_start(dst, src, allow_slow_non_contiguous=True).then_inc(wld, 16)
                sp.wait_ge(wld, 16 * len(loads))
                sp.sem_inc(wload, 1)
                with sp.Fori(0, B) as b:
                    sp.wait_ge(oc_ok, b * TT)
                    for t in range(TT):
                        sp.dma_start(o_in[:, t], o_d[bass.ds(b, 1), :, t * P:(t + 1) * P].rearrange("o q p g -> p (o q) g")).then_inc(ld_o, 16)
                    sp.wait_ge(ctx_m, b)
                    sp.dma_start(ctx_in[:], d["ctx_512"][bass.ds(b, 1)].rearrange("o k c -> (o k) c")).then_inc(cld, 16)
                    sp.wait_ge(z_ok, b * TT)
                    for t in range(TT):
                        sp.dma_start(bg_in[:, t].rearrange("p k c -> p (k c)"), bg_d[bass.ds((b * TT + t) * P, P)]).then_inc(ld_bg, 16)
                    sp.wait_ge(y_ok, b * TT)
                    sp.dma_start(x_in[:], d["x"][bass.ds(b, 1)].rearrange("o (t p) c -> p (o t) c", p=P)).then_inc(ld_x, 16)

            @block.tensor
            def _(pe):
                pe.wait_ge(prep, 1)
                with pe.Fori(0, B) as b:
                    b1 = pe.snap(b + 1)
                    n = [pe.snap(b * TT + t + 1) for t in range(TT)]
                    pe.wait_ge(cld, b1 * 16)
                    pe.wait_ge(lg_ok, b * TT)
                    pe.transpose(m_p[0][:, 0:LKV], ctx_in[:], ident[0:LKV, 0:LKV]).then_inc(ctx_m, 1)
                    pe.wait_ge(ctx_ok, b1)
                    for g in range(HG):
                        last = pe.matmul(m_p[0][:, g * LKV:(g + 1) * LKV], w_k[:, g].rearrange("p h e -> p (h e)"), ctx_t[:],
                                         start=True, stop=True)
                    last.then_inc(k_m, 1)
                    pe.matmul(m_p[1][0:LKV, 0:C], ctx_t[:], w_v[:], start=True, stop=True).then_inc(v_m, 1)
                    pe.wait_ge(k_ok, b1)
                    pe.wait_ge(v_ok, b1)

                    def turn(t, src, done):
                        for c in range(CC):
                            last = pe.transpose(m_p[t][:, c * P:(c + 1) * P], src[:, c * P:(c + 1) * P], ident[:])
                        last.then_inc(done, 1)

                    def times(t, w, cols, done):
                        for c in range(CC):
                            last = pe.matmul(m_p[t][:, 0:cols], flip[:, t, c], w[:, c], start=c == 0, stop=c == CC - 1)
                        last.then_inc(done, 1)

                    for t in range(TT):
                        pe.wait_ge(z_ok, n[t])
                        turn(t, zz[:, t], zt)
                    for t in range(TT):
                        pe.wait_ge(zt_ok, n[t])
                        times(t, w_o, C, y_m)
                    for t in range(TT):
                        pe.wait_ge(x1_ok, n[t])
                        turn(t, x1[:, t], x1t)
                    for t in range(TT):
                        pe.wait_ge(x1t_ok, n[t])
                        for g in range(HG):
                            for c in range(CC):
                                last = pe.matmul(m_p[t][:, g * P:(g + 1) * P], w_q[:, c, g].rearrange("p h e -> p (h e)"),
                                                 flip[:, t, c], start=c == 0, stop=c == CC - 1)
                        last.then_inc(q_m, 1)
                    for t in range(TT):
                        pe.wait_ge(q_ok, n[t])
                        pe.wait_ge(sub_ok, b * TT + t)
                        for g in range(HG):
                            for h in range(HG):
                                last = pe.matmul(sc_p[:, h, g * LKV:(g + 1) * LKV], q_t[h * DP:h * DP + D, t, g],
                                                 k_t[h * DP:h * DP + D, g], start=True, stop=True)
                        last.then_inc(sc, 1)
                    for t in range(TT):
                        pe.wait_ge(pr_ok, n[t])
                        for h in range(HG):
                            pe.wait_ge(ptc, (b * TT + t) * HG + h)
                            for g in range(HG):
                                last = pe.transpose(pt_p[h % 2][0:LKV, g], pr[:, t, h, g], ident[:])
                            last.then_inc(ptm, 1)
                        pe.wait_ge(ptc, (b * TT + t + 1) * HG + 1)
                        for g in range(HG):
                            for h in range(HG):
                                k = g * HG + h
                                last = pe.matmul(m_p[t][:, k * (D + 1):(k + 1) * (D + 1)], p_t[:, t, h * HG + g],
                                                 v_aug[:, k], start=True, stop=True)
                        last.then_inc(pv, 1)
                    for t in range(TT):
                        pe.wait_ge(at_ok, n[t])
                        turn(t, at[:, t], att)
                    for t in range(TT):
                        pe.wait_ge(att_ok, n[t])
                        times(t, w_xo, C, y2_m)
                    for t in range(TT):
                        pe.wait_ge(x2_ok, n[t])
                        turn(t, x2[:, t], x2t)
                    for t in range(TT):
                        pe.wait_ge(x2t_ok, n[t])
                        times(t, router, NE, lg_m)

            @block.scalar
            def _(act):
                act.sem_inc(ptc, 1)
                act.wait_ge(wload, 1)
                act.mul(b_ks[:], b_k[:], 0.25)
                act.wait_ge(prep, 1)
                with act.Fori(0, B) as b:
                    b1 = act.snap(b + 1)
                    n = [act.snap(b * TT + t + 1) for t in range(TT)]

                    def unflip(t, ready, done):
                        act.wait_ge(ready, n[t])
                        act.copy(flip[:, t].rearrange("p c n -> p (c n)"), m_p[t][:, 0:C]).then_inc(done, 1)

                    act.wait_ge(ctx_m, b1)
                    act.copy(ctx_t[:], m_p[0][:, 0:LKV]).then_inc(ctx_ok, 1)
                    act.wait_ge(k_m, b1)
                    for g in range(HG):
                        last = act.activation(k_t[:, g], m_p[0][:, g * LKV:(g + 1) * LKV], ACT.Identity,
                                              bias=b_ks[:, g:g + 1], scale=0.25)
                    last.then_inc(k_ok, 1)
                    for t in range(TT):
                        act.wait_ge(oc_ok, n[t])
                        act.activation(sq[:, t], oc[:, t], ACT.Square).then_inc(sq_ok, 1)
                    for t in range(TT):
                        act.wait_ge(ss_ok, n[t])
                        act.activation(sd[:, t], ss[:, t], ACT.Sqrt, bias=eps[:], scale=1.0 / D).then_inc(sd_ok, 1)
                    for t in range(TT):
                        unflip(t, zt, zt_ok)
                    for t in range(TT):
                        act.wait_ge(mv_ok, n[t])
                        act.activation(std[:, t], mv[:, t, 1:2], ACT.Sqrt, bias=eps[:]).then_inc(std_ok, 1)
                    for t in range(TT):
                        unflip(t, x1t, x1t_ok)
                    for t in range(TT):
                        act.wait_ge(q_m, n[t])
                        for g in range(HG):
                            last = act.activation(q_t[:, t, g], m_p[t][:, g * P:(g + 1) * P], ACT.Identity, bias=b_q[:, g:g + 1])
                        last.then_inc(q_ok, 1)
                    for t in range(TT):
                        act.wait_ge(sub_ok, n[t])
                        act.activation(pr[:, t], pr[:, t], ACT.Exp).then_inc(pr_ok, 1)
                    for t in range(TT):
                        for h in range(HG):
                            act.wait_ge(ptm, (b * TT + t) * HG + h + 1)
                            act.copy(p_t[:, t, h * HG:(h + 1) * HG], pt_p[h % 2][0:LKV]).then_inc(ptc, 1)
                    for t in range(TT):
                        unflip(t, att, att_ok)
                    for t in range(TT):
                        act.wait_ge(mv2_ok, n[t])
                        act.activation(std[:, t], mv[:, t, 1:2], ACT.Sqrt, bias=eps[:]).then_inc(std2_ok, 1)
                    for t in range(TT):
                        unflip(t, x2t, x2t_ok)
                    for t in range(TT):
                        act.wait_ge(x2_ok, n[t])
                        act.dma_start(x2_d[bass.ds((b * TT + t) * P, P)], x2[:, t]).then_inc(x2_st, 16)
                act.wait_ge(x2_st, B * TT * 16)

            @block.vector
            def _(dve):
                dve.memset(b_q[:], 0.0)
                dve.memset(b_k[:], 0.0).then_inc(zeroed, 1)
                dve.memset(w_q[:], 0.0)
                dve.memset(w_k[:], 0.0).then_inc(zeroed, 1)
                dve.memset(v_aug[:, :, D:D + 1], 1.0)
                dve.memset(eps[:], EPS)
                dve.wait_ge(zeroed, 2)
                dve.wait_ge(wload, 1)
                for c in range(CC):
                    dve.tensor_copy(w_q[:, c, :, :, 0:D], q_raw[:, c].rearrange("p (g h e) -> p g h e", g=HG, h=HG))
                dve.tensor_copy(w_k[:, :, :, 0:D], k_raw[:].rearrange("p (g h e) -> p g h e", g=HG, h=HG)).then_inc(prep, 1)
                with dve.Fori(0, B) as b:
                    b1 = dve.snap(b + 1)
                    n = [dve.snap(b * TT + t + 1) for t in range(TT)]

                    def norm(t, src, bn_d, mv_d, std_d, rstd_d, dst, done):
                        dve.bn_stats(bn6[:, t], src).then_inc(bn_d, 1)
                        dve.wait_ge(bn_d, n[t])
                        dve.sem_inc(passed, 1)
                        dve.bn_aggr(mv[:, t], bn6[:, t]).then_inc(mv_d, 1)
                        dve.wait_ge(std_d, n[t])
                        dve.reciprocal(rstd[:, t], std[:, t]).then_inc(rstd_d, 1)
                        dve.wait_ge(rstd_d, n[t])
                        dve.tensor_scalar(dst, src, mv[:, t, 0:1], rstd[:, t], ALU.subtract, ALU.mult).then_inc(done, 1)

                    dve.wait_ge(ld_o, b1 * (16 * TT))
                    for t in range(TT):
                        dve.tensor_reduce(mu[:, t], o_in[:, t].rearrange("p q (h e) -> p (q h) e", e=D), AX.X, ALU.add).then_inc(mu_ok, 1)
                    for t in range(TT):
                        dve.wait_ge(mu_ok, n[t])
                        dve.scalar_tensor_tensor(heads(oc[:, t]), over(mu[:, t]), -1.0 / D,
                                                 o_in[:, t].rearrange("p q (h e) -> p (q h) e", e=D), ALU.mult, ALU.add).then_inc(oc_ok, 1)
                    for t in range(TT):
                        dve.wait_ge(sq_ok, n[t])
                        dve.tensor_reduce(ss[:, t], heads(sq[:, t]), AX.X, ALU.add).then_inc(ss_ok, 1)
                    for t in range(TT):
                        dve.wait_ge(sd_ok, n[t])
                        dve.reciprocal(rs[:, t], sd[:, t]).then_inc(rs_ok, 1)
                    for t in range(TT):
                        dve.wait_ge(rs_ok, n[t])
                        dve.tensor_tensor(heads(zz[:, t]), heads(oc[:, t]), over(rs[:, t]), ALU.mult).then_inc(on_ok, 1)
                    dve.wait_ge(v_m, b1)
                    dve.tensor_tensor(v_aug[:, :, 0:D], m_p[1][0:LKV, 0:C].rearrange("p (h e) -> p h e", h=H),
                                      bv_row[0:LKV].rearrange("p (h e) -> p h e", h=H), ALU.add).then_inc(v_ok, 1)
                    dve.wait_ge(ld_x, b1 * 16)
                    for t in range(TT):
                        dve.wait_ge(y_m, n[t])
                        dve.tensor_tensor(y1[:, t], m_p[t][:, 0:C], x_in[:, t], ALU.add).then_inc(y_ok, 1)
                        dve.wait_ge(y_ok, n[t])
                        norm(t, y1[:, t], bn_ok, mv_ok, std_ok, rstd_ok, x1[:, t], x1_ok)
                    for t in range(TT):
                        dve.wait_ge(sc, n[t])
                        scores = sc_p[:, :, 0:HG * LKV].rearrange("p h (g k) -> p h g k", g=HG)
                        dve.tensor_reduce(mx[:, t], scores, AX.X, ALU.max).then_inc(mx_ok, 1)
                        dve.wait_ge(mx_ok, n[t])
                        for h in range(HG):
                            last = dve.tensor_tensor(pr[:, t, h], scores[:, h], mx[:, t, h].unsqueeze(2).broadcast_to([P, HG, LKV]), ALU.subtract)
                        last.then_inc(sub_ok, 1)
                    for t in range(TT):
                        dve.wait_ge(pv, n[t])
                        pvv = m_p[t][:, 0:H * (D + 1)].rearrange("p (h e) -> p h e", h=H)
                        dve.reciprocal(rden[:, t].unsqueeze(2), pvv[:, :, D:D + 1]).then_inc(rd_ok, 1)
                        dve.wait_ge(rd_ok, n[t])
                        dve.tensor_tensor(heads(at[:, t]), pvv[:, :, 0:D], over(rden[:, t]), ALU.mult).then_inc(at_ok, 1)
                    for t in range(TT):
                        dve.wait_ge(y2_m, n[t])
                        dve.wait_ge(x1b_ok, n[t])
                        dve.tensor_tensor(x1b[:, t], m_p[t][:, 0:C], x1b[:, t], ALU.add).then_inc(y2_ok, 1)
                        dve.wait_ge(y2_ok, n[t])
                        if t == 0:
                            dve.wait_ge(x2_st, b * (16 * TT))
                        norm(t, x1b[:, t], bn2_ok, mv2_ok, std2_ok, rstd2_ok, x2[:, t], x2_ok)
                    for t in range(TT):
                        dve.wait_ge(lg_m, n[t])
                        dve.tensor_copy(logits[:, bass.ds(b * TT + t, 1)].rearrange("p o e -> p (o e)"), m_p[t][:, 0:NE]).then_inc(lg_ok, 1)

            @block.gpsimd
            def _(pool):
                pool.wait_ge(wload, 1)
                with pool.Fori(0, B) as b:
                    n = [pool.snap(b * TT + t + 1) for t in range(TT)]
                    pool.wait_ge(ld_bg, (b + 1) * (16 * TT))
                    for t in range(TT):
                        pool.wait_ge(on_ok, n[t])
                        pool.tensor_tensor(zz[:, t], zz[:, t], gw_row[:], ALU.mult).then_inc(z1, 1)
                    for t in range(TT):
                        pool.wait_ge(z1, n[t])
                        pool.tensor_tensor(zz[:, t], zz[:, t], gb_row[:], ALU.add).then_inc(z2, 1)
                    for t in range(TT):
                        pool.wait_ge(z2, n[t])
                        pool.tensor_tensor(zz[:, t], zz[:, t], bg_in[:, t, 0], ALU.add).then_inc(z3, 1)
                    for t in range(TT):
                        pool.wait_ge(z3, n[t])
                        pool.tensor_tensor(zz[:, t], zz[:, t], bg_in[:, t, 1], ALU.mult).then_inc(z_ok, 1)
                    for t in range(TT):
                        pool.wait_ge(x1_ok, n[t])
                        pool.tensor_tensor(x1b[:, t], x1[:, t], bo_row[:], ALU.add).then_inc(x1b_ok, 1)


def dispatch(nc, logits, slots, gates, tile_expert):
    ctx = ExitStack()
    with ctx:
        def sb(name, shape, dt=F32):
            return ctx.enter_context(nc.sbuf_tensor(name, shape, dt))

        def sem(name):
            return nc.alloc_semaphore(name)

        FULL = [P, NT, NE]
        e_int = sb("e_int", [P, NE], I32)
        j_int = sb("j_int", [1, SLOTT], I32)
        e_row, e8_row = sb("e_row", [P, NE]), sb("e8_row", [P, NE])
        j_row = sb("j_row", [1, SLOTT])
        before = sb("before", [P, P])
        ones = sb("ones", [P, P])
        top = [sb(f"top{k}", [P, NT]) for k in range(2)]
        idx = [sb(f"idx{k}", [P, NT]) for k in range(2)]
        mask = [sb(f"mask{k}", FULL) for k in range(2)]
        eq, cand, l2 = sb("eq", FULL), sb("cand", FULL), sb("l2", FULL)
        gap, ex, den = sb("gap", [P, NT]), sb("ex", [P, NT]), sb("den", [P, NT])
        both, tot = sb("both", FULL), sb("tot", FULL)
        run = [sb(f"run{k}", FULL) for k in range(2)]
        cnt, padded, cum0, cum1, off = (sb("d_" + n, [P, NE]) for n in ("cnt", "padded", "cum0", "cum1", "off"))
        cnt_i = sb("cnt_i", [P, NE], I32)
        slot_f = sb("slot_f", [P, NT])
        past = sb("past", [1, SLOTT, NE])
        te = sb("te", [1, SLOTT])
        pre_p = ctx.enter_context(nc.psum_tensor("pre_p", [P, 512], F32))
        tot_p = ctx.enter_context(nc.psum_tensor("tot_p", [P, 512], F32))
        consts, step, gap_ok, ex_ok, both_ok, ranks = (sem("d_" + n) for n in ("consts", "step", "gap_ok", "ex_ok", "both_ok", "ranks"))

        def per_tile(ap):
            return ap.unsqueeze(2).broadcast_to(FULL)

        def per_expert(ap):
            return ap.unsqueeze(1).broadcast_to(FULL)

        with nc.Block() as block:
            @block.gpsimd
            def _(pool):
                pool.iota(e_int[:], pattern=[[1, NE]], base=0, channel_multiplier=0).then_inc(consts, 1)
                pool.iota(j_int[:], pattern=[[P, SLOTT]], base=0, channel_multiplier=0).then_inc(consts, 1)
                pool.memset(ones[:], 1.0).then_inc(consts, 1)
                pool.wait_ge(consts, 3)
                pool.affine_select(out=before[:], in_=ones[:], compare_op=ALU.is_gt, fill=0.0, base=0,
                                   pattern=[[1, P]], channel_multiplier=-1).then_inc(consts, 1)

            @block.tensor
            def _(pe):
                pe.wait_ge(consts, 4)
                pe.wait_ge(both_ok, 1)
                rhs = both[:].rearrange("p n e -> p (n e)")
                pe.matmul(pre_p[:], before[:], rhs, start=True, stop=True)
                pe.matmul(tot_p[:], ones[:], rhs, start=True, stop=True).then_inc(ranks, 1)

            @block.scalar
            def _(act):
                act.wait_ge(gap_ok, 1)
                act.activation(ex[:], gap[:], ACT.Exp).then_inc(ex_ok, 1)

            @block.vector
            def _(dve):
                count = [0]

                def then(ins):
                    count[0] += 1
                    ins.then_inc(step, 1)
                    dve.wait_ge(step, count[0])

                dve.wait_ge(consts, 2)
                dve.tensor_copy(j_row[:], j_int[:])
                then(dve.tensor_copy(e_row[:], e_int[:]))
                then(dve.tensor_scalar(e8_row[:], e_row[:], float(NE), None, ALU.add))
                values = logits[:]
                for k in range(2):
                    then(dve.tensor_reduce(top[k][:], values, AX.X, ALU.max))
                    then(dve.tensor_tensor(eq[:], values, per_tile(top[k][:]), ALU.is_equal))
                    then(dve.scalar_tensor_tensor(cand[:], eq[:], -float(NE), per_expert(e8_row[:]), ALU.mult, ALU.add))
                    then(dve.tensor_reduce(idx[k][:], cand[:], AX.X, ALU.min))
                    then(dve.tensor_tensor(mask[k][:], per_expert(e_row[:]), per_tile(idx[k][:]), ALU.is_equal))
                    if k == 0:
                        then(dve.scalar_tensor_tensor(l2[:], mask[0][:], -3e38, logits[:], ALU.mult, ALU.add))
                        values = l2[:]
                dve.tensor_tensor(gap[:], top[1][:], top[0][:], ALU.subtract).then_inc(gap_ok, 1)
                dve.tensor_tensor(both[:], mask[0][:], mask[1][:], ALU.add).then_inc(both_ok, 1)
                dve.wait_ge(ex_ok, 1)
                then(dve.tensor_scalar(den[:], ex[:], 1.0, None, ALU.add))
                then(dve.reciprocal(gates[:, 0], den[:]))
                then(dve.tensor_tensor(gates[:, 1], ex[:], gates[:, 0], ALU.mult))
                dve.wait_ge(ranks, 1)
                then(dve.tensor_copy(tot[:].rearrange("p n e -> p (n e)"), tot_p[:]))
                src, k, s = tot, 0, 1
                while s < NT:
                    dst = run[k]
                    dve.tensor_copy(dst[:, 0:s], src[:, 0:s])
                    then(dve.tensor_tensor(dst[:, s:], src[:, s:], src[:, 0:NT - s], ALU.add))
                    src, k, s = dst, 1 - k, 2 * s
                incl = src
                then(dve.tensor_scalar(cnt[:], incl[:, NT - 1], float(P - 1), None, ALU.add))
                then(dve.tensor_copy(cnt_i[:], cnt[:]))
                then(dve.tensor_scalar(cnt_i[:], cnt_i[:], -P, None, ALU.bitwise_and))
                then(dve.tensor_copy(padded[:], cnt_i[:]))
                a, k, s = padded, 0, 1
                while s < NE:
                    c = (cum0, cum1)[k]
                    dve.tensor_copy(c[:, 0:s], a[:, 0:s])
                    then(dve.tensor_tensor(c[:, s:], a[:, s:], a[:, 0:NE - s], ALU.add))
                    a, k, s = c, 1 - k, 2 * s
                then(dve.tensor_tensor(off[:], a[:], padded[:], ALU.subtract))
                base = run[0] if incl is run[1] else run[1]
                then(dve.tensor_tensor(base[:], incl[:], tot[:], ALU.subtract))
                then(dve.tensor_tensor(base[:], base[:], per_expert(off[:]), ALU.add))
                then(dve.tensor_tensor(base[:].rearrange("p n e -> p (n e)"), pre_p[:], base[:].rearrange("p n e -> p (n e)"), ALU.add))
                for k in range(2):
                    then(dve.tensor_tensor(eq[:], mask[k][:], base[:], ALU.mult))
                    then(dve.tensor_reduce(slot_f[:], eq[:], AX.X, ALU.add))
                    then(dve.tensor_copy(slots[:, k], slot_f[:]))
                wide = [1, SLOTT, NE]
                then(dve.tensor_tensor(past[:], j_row[:].unsqueeze(2).broadcast_to(wide), a[0:1].unsqueeze(1).broadcast_to(wide), ALU.is_ge))
                then(dve.tensor_reduce(te[:], past[:], AX.X, ALU.add))
                then(dve.tensor_scalar(te[:], te[:], float(NE - 1), None, ALU.min))
                then(dve.tensor_copy(tile_expert[:], te[:]))


def scatter(nc, x2_d, slots, xs_d, s_xs0):
    ctx = ExitStack()
    with ctx:
        row = ctx.enter_context(nc.sbuf_tensor("sx_row", [P, 2, C], F32))
        at = ctx.enter_context(nc.sbuf_tensor("sx_at", [P, 2, 2, 1], U32))
        sem = nc.alloc_semaphore
        at_ok, passed = sem("x_at_ok"), sem("x_passed")
        row_ld = [sem(f"x_row_ld{s}") for s in range(2)]
        sent = [sem(f"x_sent{s}") for s in range(2)]
        with nc.Block() as block:
            @block.sync
            def _(sp):
                with sp.Fori(0, NT // 2) as i:
                    for s in range(2):
                        sp.wait_ge(sent[s], i * 32)
                        sp.dma_start(row[:, s], x2_d[bass.ds((i * 2 + s) * P, P)]).then_inc(row_ld[s], 16)

            @block.gpsimd
            def _(pool):
                pool.wait_ge(s_xs0, 16 * (T // TB // 2 + 1))
                with pool.Fori(0, NT // 2) as i:
                    for s in range(2):
                        pool.wait_ge(sent[s], i * 32)
                        for k in range(2):
                            pool.tensor_copy(at[:, s, k], slots[:, k, bass.ds(i * 2 + s, 1)]).then_inc(at_ok, 1)
                        pool.wait_ge(at_ok, (i * 2 + s + 1) * 2)
                        pool.wait_ge(row_ld[s], (i + 1) * 16)
                        pool.sem_inc(passed, 1)
                        for k in range(2):
                            pool.indirect_dma_start(xs_d, bass.IndirectOffsetOnAxis(at[:, s, k], 0), row[:, s], None).then_inc(sent[s], 16)
                for s in range(2):
                    pool.wait_ge(sent[s], NT // 2 * 32)


def experts(nc, ident, w13, w2, s_w13, tile_expert, xs_d, ys_d):
    ctx = ExitStack()
    with ctx:
        def sb(name, shape, dt=F32):
            return ctx.enter_context(nc.sbuf_tensor(name, shape, dt))

        def ps(name, shape):
            return ctx.enter_context(nc.psum_tensor(name, shape, F32))

        def sem(name):
            return nc.alloc_semaphore(name)

        MC = MD // P
        x = sb("e_x", [P, 2, C])
        x_t = sb("e_x_t", [P, 2, CC, P])
        h = sb("e_h", [P, 2, MD])
        h_t = sb("e_h_t", [P, 2, MC, P])
        y = sb("e_y", [P, 2, C])
        xt_p = ps("e_xt_p", [P, 512])
        ht_p = ps("e_ht_p", [P, MC, P])
        gate_p = [ps(f"e_gate_p{i}", [P, MD]) for i in range(2)]
        up_p = [ps(f"e_up_p{i}", [P, MD]) for i in range(2)]
        y_p = [ps(f"e_y_p{i}", [P, 512]) for i in range(2)]
        ld = [sem(f"e_ld{i}") for i in range(2)]
        stored = [sem(f"e_stored{i}") for i in range(2)]
        xt, xt_ok, gu, silu_ok, h_ok, ht, ht_ok, y_m, y_ok = (
            sem("e_" + n) for n in "xt xt_ok gu silu_ok h_ok ht ht_ok y_m y_ok".split())
        with nc.Block() as block:
            @block.sync
            def _(sp):
                with sp.Fori(0, SLOTT // 2) as i:
                    for s in range(2):
                        sp.wait_ge(xt, i * 2)
                        sp.dma_start(x[:, s], xs_d[bass.ds((i * 2 + s) * P, P)]).then_inc(ld[s], 16)

            @block.tensor
            def _(pe):
                pe.wait_ge(s_w13, 16 * 3 * T // TB // 2)
                with pe.Fori(0, SLOTT // 2) as i:
                    j = [i * 2 + s for s in range(2)]
                    e = [pe.value_load(tile_expert[0:1, bass.ds(j[s], 1)], min_val=0, max_val=NE - 1) for s in range(2)]
                    for s in range(2):
                        pe.wait_ge(ld[s], (i + 1) * 16)
                        pe.wait_ge(xt_ok, j[s])
                        for c in range(CC):
                            last = pe.transpose(xt_p[:, c * P:(c + 1) * P], x[:, s, c * P:(c + 1) * P], ident[:])
                        last.then_inc(xt, 1)
                    for s in range(2):
                        pe.wait_ge(xt_ok, j[s] + 1)
                        pe.wait_ge(h_ok, i * 2)
                        for half, bank in enumerate((gate_p[s], up_p[s])):
                            for c in range(CC):
                                last = pe.matmul(bank[:], x_t[:, s, c], w13[:, bass.ds(e[s] * (CC * 2 * MD) + (c * 2 + half) * MD, MD)],
                                                 start=c == 0, stop=c == CC - 1)
                        last.then_inc(gu, 1)
                    for s in range(2):
                        pe.wait_ge(h_ok, j[s] + 1)
                        pe.wait_ge(ht_ok, j[s])
                        for m in range(MC):
                            last = pe.transpose(ht_p[:, m], h[:, s, m * P:(m + 1) * P], ident[:])
                        last.then_inc(ht, 1)
                        pe.wait_ge(ht_ok, j[s] + 1)
                        pe.wait_ge(y_ok, i * 2)
                        for m in range(MC):
                            last = pe.matmul(y_p[s][:, 0:C], h_t[:, s, m], w2[:, bass.ds(e[s] * (MC * C) + m * C, C)],
                                             start=m == 0, stop=m == MC - 1)
                        last.then_inc(y_m, 1)

            @block.scalar
            def _(act):
                for s in range(2):
                    act.sem_inc(stored[s], 16)
                with act.Fori(0, SLOTT // 2) as i:
                    for s in range(2):
                        act.wait_ge(gu, i * 2 + s + 1)
                        act.activation(h[:, s], gate_p[s][:], ACT.Silu).then_inc(silu_ok, 1)
                    for s in range(2):
                        act.wait_ge(y_m, i * 2 + s + 1)
                        act.wait_ge(stored[s], (i + 1) * 16)
                        act.copy(y[:, s], y_p[s][:, 0:C]).then_inc(y_ok, 1)
                        act.wait_ge(y_ok, i * 2 + s + 1)
                        act.dma_start(ys_d[bass.ds((i * 2 + s) * P, P)], y[:, s]).then_inc(stored[s], 16)
                for s in range(2):
                    act.wait_ge(stored[s], 16 * (SLOTT // 2 + 1))

            @block.vector
            def _(dve):
                with dve.Fori(0, SLOTT // 2) as i:
                    for s in range(2):
                        dve.wait_ge(xt, i * 2 + s + 1)
                        dve.tensor_copy(x_t[:, s].rearrange("p c n -> p (c n)"), xt_p[:, 0:C]).then_inc(xt_ok, 1)
                    for s in range(2):
                        dve.wait_ge(silu_ok, i * 2 + s + 1)
                        dve.tensor_tensor(h[:, s], up_p[s][:], h[:, s], ALU.mult).then_inc(h_ok, 1)
                    for s in range(2):
                        dve.wait_ge(ht, i * 2 + s + 1)
                        dve.tensor_copy(h_t[:, s], ht_p[:]).then_inc(ht_ok, 1)


def combine(nc, x2_d, slots, gates, ys_d, out):
    ctx = ExitStack()
    with ctx:
        def sb(name, shape, dt=F32):
            return ctx.enter_context(nc.sbuf_tensor(name, shape, dt))

        def sem(name):
            return nc.alloc_semaphore(name)

        at = sb("f_at", [P, 2, 2, 1], U32)
        ya = [[sb(f"f_y{s}{k}", [P, C]) for k in range(2)] for s in range(2)]
        x2 = sb("f_x2", [P, 2, C])
        acc = sb("f_acc", [P, 2, C])
        bn6 = sb("f_bn6", [P, 2, 6])
        mv = sb("f_mv", [P, 2, 2])
        rstd = sb("f_rstd", [P, 2, 1])
        std = sb("f_std", [P, 2, 1])
        eps = sb("f_eps", [P, 1])
        res = sb("f_res", [P, 2, C])
        got = [sem(f"f_got{i}") for i in range(2)]
        ld = [sem(f"f_ld{i}") for i in range(2)]
        stored = [sem(f"f_stored{i}") for i in range(2)]
        passed, at_go = sem("f_passed"), sem("f_at_go")
        at_ok, acc0, acc1, bn_ok, mv_ok, std_ok, rstd_ok, res_ok, eps_ok = (
            sem("f_" + n) for n in "at_ok acc0 acc1 bn_ok mv_ok std_ok rstd_ok res_ok eps_ok".split())
        out_v = out.rearrange("b t c -> (b t) c")
        with nc.Block() as block:
            @block.gpsimd
            def _(pool):
                with pool.Fori(0, NT // 2) as i:
                    for s in range(2):
                        pool.wait_ge(got[s], i * 32)
                        for k in range(2):
                            pool.tensor_copy(at[:, s, k], slots[:, k, bass.ds(i * 2 + s, 1)]).then_inc(at_ok, 1)
                        pool.wait_ge(at_ok, (i * 2 + s + 1) * 2)
                        pool.wait_ge(acc1, i * 2)
                        pool.sem_inc(at_go, 1)
                        for k in range(2):
                            pool.indirect_dma_start(ya[s][k][:], None, ys_d, bass.IndirectOffsetOnAxis(at[:, s, k], 0)).then_inc(got[s], 16)

            @block.vector
            def _(dve):
                dve.memset(eps[:], EPS).then_inc(eps_ok, 1)
                with dve.Fori(0, NT // 2) as i:
                    n = [dve.snap(i * 2 + s + 1) for s in range(2)]

                    def gate(k, s):
                        return gates[:, k, bass.ds(i * 2 + s, 1)]

                    dve.wait_ge(res_ok, i * 2)
                    for s in range(2):
                        dve.wait_ge(got[s], (i + 1) * 32)
                        dve.wait_ge(ld[s], (i + 1) * 16)
                        dve.scalar_tensor_tensor(acc[:, s], ya[s][0][:], gate(0, s), x2[:, s], ALU.mult, ALU.add).then_inc(acc0, 1)
                    for s in range(2):
                        dve.wait_ge(acc0, n[s])
                        dve.scalar_tensor_tensor(acc[:, s], ya[s][1][:], gate(1, s), acc[:, s], ALU.mult, ALU.add).then_inc(acc1, 1)
                    for s in range(2):
                        dve.wait_ge(acc1, n[s])
                        dve.bn_stats(bn6[:, s], acc[:, s]).then_inc(bn_ok, 1)
                    for s in range(2):
                        dve.wait_ge(bn_ok, n[s])
                        dve.sem_inc(passed, 1)
                        dve.bn_aggr(mv[:, s], bn6[:, s]).then_inc(mv_ok, 1)
                    for s in range(2):
                        dve.wait_ge(std_ok, n[s])
                        dve.reciprocal(rstd[:, s], std[:, s]).then_inc(rstd_ok, 1)
                    for s in range(2):
                        dve.wait_ge(rstd_ok, n[s])
                        dve.wait_ge(stored[s], i * 16)
                        dve.tensor_scalar(res[:, s], acc[:, s], mv[:, s, 0:1], rstd[:, s], ALU.subtract, ALU.mult).then_inc(res_ok, 1)

            @block.scalar
            def _(act):
                act.wait_ge(eps_ok, 1)
                with act.Fori(0, NT // 2) as i:
                    for s in range(2):
                        act.wait_ge(acc0, i * 2)
                        act.dma_start(x2[:, s], x2_d[bass.ds((i * 2 + s) * P, P)]).then_inc(ld[s], 16)
                    for s in range(2):
                        act.wait_ge(mv_ok, i * 2 + s + 1)
                        act.activation(std[:, s], mv[:, s, 1:2], ACT.Sqrt, bias=eps[:]).then_inc(std_ok, 1)

            @block.sync
            def _(sp):
                with sp.Fori(0, NT // 2) as i:
                    for s in range(2):
                        sp.wait_ge(res_ok, i * 2 + s + 1)
                        sp.dma_start(out_v[bass.ds((i * 2 + s) * P, P)], res[:, s]).then_inc(stored[s], 16)
                for s in range(2):
                    sp.wait_ge(stored[s], NT // 2 * 16)


_INS = ["x", "ctx_512"] + ["L0_attn_" + n for n in (
    "x_r x_w x_k x_v x_a x_g k_k k_a r_k W_r W_k W_v W_o w_lora_a w_lora_b w_lora_bias a_lora_a a_lora_b "
    "a_lora_bias g_lora_a g_lora_b g_lora_bias gn_weight gn_bias").split()] + [
    "L0_xattn_" + n for n in "Wq bq Wk bk Wv bv Wo bo".split()] + [
    "L0_ffn_" + n for n in "moe_router moe_w13 moe_w2".split()]
_UNUSED = {"L0_attn_x_g"}


def kernel(**inputs):
    import numpy as _np
    import concourse.bacc as _bacc
    from concourse import mybir as _mybir
    from concourse.bass_utils import run_bass_kernel_spmd as _run

    nc = _bacc.Bacc("TRN2", target_bir_lowering=False, num_devices=1)
    arrays, aps = {}, {}
    for name in _INS:
        if name in _UNUSED:
            continue
        a = _np.ascontiguousarray(inputs[name])
        arrays[f"in_{name}_dram"] = a
        aps[name] = nc.dram_tensor(f"in_{name}_dram", a.shape, _mybir.dt.from_np(a.dtype), kind="ExternalInput").ap()
    out = nc.dram_tensor("out_0_dram", (B, T, C), F32, kind="ExternalOutput").ap()
    decoder_kernel(nc, aps, out)
    r = _run(nc, [arrays], core_ids=[0])
    return r.results[0]["out_0_dram"]
```

```python
from contextlib import ExitStack

import concourse.bass as bass
from concourse import mybir

F32 = mybir.dt.float32
U32 = mybir.dt.uint32
I32 = mybir.dt.int32
ALU = mybir.AluOpType
ACT = mybir.ActivationFunctionType
AX = mybir.AxisListType

P = 128
B, T, C, H, D = 32, 256, 256, 16, 16
CC = C // P
TT = T // P
NT = B * TT
Q = P // B
HQ = H // Q
G = HQ * D
NC6 = 6
R_, W_, K_, V_, A_, B_ = range(NC6)
RL = 64
RG = 128
LKV, CD = 120, 128
NE, MD = 8, 512
SLOTT = 2 * B * T // P + NE
TB = 8
EPS = 1e-5
EXP_HALF = 0.6065306597126334


def decoder_kernel(nc, d, out):
    ctx = ExitStack()
    with ctx:
        def dram(name, shape):
            return nc.dram_tensor(name, shape, F32, kind="Internal").ap()

        coef_d = dram("coef_d", (B, Q, T, NC6 * G))
        bg_d = dram("bg_d", (B * T, 2 * C))
        o_d = dram("o_d", (B, Q, T, G))
        xs_d = dram("xs_d", (SLOTT * P, C))
        ys_d = dram("ys_d", (SLOTT * P, C))
        x2_d = dram("x2_d", (B * T, C))

        def sb(name, shape, dt=F32):
            return ctx.enter_context(nc.sbuf_tensor(name, shape, dt))

        ident = sb("ident", [P, P])
        w13 = sb("w13", [P, NE * CC * 2 * MD])
        s_const = nc.alloc_semaphore("s_const")
        s_w13 = nc.alloc_semaphore("s_w13")
        s_xs0 = nc.alloc_semaphore("s_xs0")
        zero = sb("zero", [P, C])

        constants(nc, ident, zero, s_const)
        mark = nc.snapshot_sems()
        project(nc, d, ident, coef_d, bg_d)
        reuse_semaphores(nc, mark)
        scan(nc, d, ident, zero, coef_d, o_d, w13, xs_d, s_w13, s_xs0)
        logits = sb("logits", [P, NT, NE])
        mark = nc.snapshot_sems()
        attend(nc, d, ident, o_d, bg_d, x2_d, logits)
        reuse_semaphores(nc, mark)
        w2 = sb("w2", [P, NE * (MD // P), C])
        s_w2 = nc.alloc_semaphore("s_w2")
        slots = sb("slots", [P, 2, NT], U32)
        gates = sb("gates", [P, 2, NT])
        tile_expert = sb("tile_expert", [1, SLOTT], I32)
        dispatch(nc, d, logits, slots, gates, tile_expert, w2, s_w2)
        scatter(nc, x2_d, slots, xs_d, s_xs0)
        experts(nc, ident, w13, w2, s_w13, s_w2, tile_expert, xs_d, ys_d)
        combine(nc, x2_d, slots, gates, ys_d, out)


def reuse_semaphores(nc, mark):
    nc.clear_and_free_semaphores(nc.allocated_since(mark))
    nc.all_engine_barrier()


def constants(nc, ident, zero, s_const):
    with nc.Block() as block:
        @block.gpsimd
        def _(pool):
            pool.memset(zero[:], 0.0).then_inc(s_const, 1)
            pool.memset(ident[:], 0.0).then_inc(s_const, 1)
            pool.wait_ge(s_const, 2)
            pool.affine_select(out=ident[:], in_=ident[:], compare_op=ALU.not_equal, fill=1.0, base=0,
                               pattern=[[-1, P]], channel_multiplier=1).then_inc(s_const, 1)


def project(nc, d, ident, coef_d, bg_d):
    ctx = ExitStack()
    with ctx:
        def sb(name, shape, dt=F32):
            return ctx.enter_context(nc.sbuf_tensor(name, shape, dt))

        def ps(name, shape):
            return ctx.enter_context(nc.psum_tensor(name, shape, F32))

        def sem(name):
            return nc.alloc_semaphore(name)

        MIX = ("r", "k", "v", "w", "a")
        w_rkv = sb("w_rkv", [P, 3, CC, C])
        w_lora = sb("w_lora", [P, 2, CC, 2 * RL])
        lora_raw = sb("lora_raw", [P, CC, 2 * RL])
        mix_w = sb("mix_w", [P, len(MIX), CC])
        omx = sb("omx", [P, len(MIX), CC])
        wa_b = sb("wa_b", [P, 2 * C])
        wr_t = sb("wr_t", [P, CC, C])
        ga = sb("ga", [P, CC, RG])
        w_rg = sb("w_rg", [P, CC, RG])
        g_b = sb("g_b", [P, C])
        bias_wa = sb("bias_wa", [P, 2, C])
        bias_g = sb("bias_g", [P, C])
        kk_row = sb("kk_row", [P, C])
        ka_row = sb("ka_row", [P, C])
        oma_row = sb("oma_row", [P, C])
        rk_row = sb("rk_row", [P, C])

        x_in = sb("x_in", [P, 2, TT, C])
        x_t = sb("x_t", [P, 2, CC, 1 + T])
        delta = sb("delta", [P, CC, T])
        mixed = sb("mixed", [P, 2, 3, CC, T])
        th = sb("th", [P, 2, T])
        sg = sb("sg", [P, 2, T])
        za = sb("za", [P, TT, 2 * C])
        wa = sb("wa", [P, TT, 2 * C])
        kk0 = sb("kk0", [P, TT, C])
        sq = sb("sq", [P, TT, C])
        ss = sb("ss", [P, TT, H])
        inv = sb("inv", [P, TT, H])
        nt = sb("nt", [P, TT, H])
        kk = sb("kk", [P, TT, C])
        u = sb("u", [P, TT, C])
        rr = sb("rr", [P, TT, C])
        bs = sb("bs", [P, TT, H])
        coef = sb("coef", [P, TT, Q, NC6, G])
        bg = sb("bg", [P, TT, 2, C])

        xt_p = ps("xt_p", [P, CC, T])
        l_p = ps("l_p", [P, 2, T])
        rv_p = [ps(f"rv_p{i}", [P, 2, C]) for i in range(TT)]
        kg_p = [ps(f"kg_p{i}", [P, 2, C]) for i in range(TT)]
        wa_p = [ps(f"wa_p{i}", [P, 2 * C]) for i in range(TT)]

        wld, wload = sem("p_wld"), sem("p_wload")
        zeroed, omx_ok, prep, wrt, wrt_ok, wrg, wrg_ok = (
            sem(n) for n in ("p_zeroed", "p_omx", "p_prep", "p_wrt", "p_wrt_ok", "p_wrg", "p_wrg_ok"))
        x_ld = [sem(f"p_x_ld{i}") for i in range(2)]
        stored = [sem(f"p_stored{i}") for i in range(TT)]
        (xt, xt_ok, dlt, mix_ok, lora, th_ok, pe_done, rv, g_m, wa_m, za_ok, kk0_ok, sq_ok, ss_ok, kk_ok,
         k_ok, g_ok, bs_ok, rv_ok, wa_ok, neg_ok, u0_ok, u_ok, rr0_ok, rr_ok, b_ok, bonus_ok) = (
            sem("p_" + n) for n in (
                "xt", "xt_ok", "dlt", "mix_ok", "lora", "th_ok", "pe_done", "rv", "g_m", "wa_m", "za_ok", "kk0_ok",
                "sq_ok", "ss_ok", "kk_ok", "k_ok", "g_ok", "bs_ok", "rv_ok", "wa_ok", "neg_ok",
                "u0_ok", "u_ok", "rr0_ok", "rr_ok", "b_ok", "bonus_ok"))
        newton, NEWTON = sem("p_newton"), 12

        def vec(name):
            v = d["L0_attn_" + name]
            return v if len(v.shape) == 1 else v.rearrange("h d -> (h d)")

        def heads(ap):
            return ap.rearrange("p (h e) -> p h e", h=H)

        def over(ap):
            return ap.unsqueeze(2).broadcast_to([P, H, D])

        def hq(ap):
            return ap.rearrange("p (q g) -> p q g", q=Q)

        with nc.Block() as block:
            @block.tensor
            def _(pe):
                pe.wait_ge(wload, 1)
                for m in range(CC):
                    for c in range(CC):
                        last = pe.transpose(xt_p[:, m, c * P:(c + 1) * P], w_rkv[:, 0, c, m * P:(m + 1) * P], ident[:])
                last.then_inc(wrt, 1)
                pe.wait_ge(wrt_ok, 1)
                for c in range(CC):
                    for m in range(CC):
                        last = pe.matmul(l_p[:, 0, c * RG:(c + 1) * RG], wr_t[:, m, c * P:(c + 1) * P], ga[:, m],
                                         start=m == 0, stop=m == CC - 1)
                last.then_inc(wrg, 1)
                pe.wait_ge(wrg_ok, 1)
                pe.wait_ge(prep, 1)
                with pe.Fori(0, B // 2) as i:
                    for s in range(2):
                        b = i * 2 + s
                        b1 = pe.snap(b + 1)
                        pe.wait_ge(x_ld[s], (i + 1) * 16)
                        pe.wait_ge(xt_ok, b)
                        for t in range(TT):
                            for c in range(CC):
                                last = pe.transpose(xt_p[:, c, t * P:(t + 1) * P], x_in[:, s, t, c * P:(c + 1) * P], ident[:])
                        last.then_inc(xt, 1)
                        pe.wait_ge(xt_ok, b1)
                        pe.wait_ge(th_ok, b * 2)
                        for sh in range(2):
                            for c in range(CC):
                                pe.matmul(l_p[:, 0], w_lora[:, sh, c], x_t[:, s, c, 1 - sh:1 - sh + T],
                                          start=sh == 0 and c == 0, stop=sh == 1 and c == CC - 1)
                        pe.wait_ge(mix_ok, b1)
                        for c in range(CC):
                            last = pe.matmul(l_p[:, 1], w_rg[:, c], mixed[:, s, 0, c], start=c == 0, stop=c == CC - 1)
                        last.then_inc(lora, 1)
                        for t in range(TT):
                            tok = slice(t * P, (t + 1) * P)
                            pe.wait_ge(stored[t], b1 * 32)
                            for n, bank, done in ((1, kg_p[t][:, 0], None), (0, rv_p[t][:, 0], None), (2, rv_p[t][:, 1], rv)):
                                for c in range(CC):
                                    last = pe.matmul(bank, mixed[:, s, n, c, tok], w_rkv[:, n, c],
                                                     start=c == 0, stop=c == CC - 1)
                                if done is not None:
                                    last.then_inc(done, 1)
                            pe.wait_ge(th_ok, b * 2 + 2)
                            pe.matmul(kg_p[t][:, 1], sg[:, s, tok], g_b[:], start=True, stop=True).then_inc(g_m, 1)
                            last = pe.matmul(wa_p[t][:], th[:, s, tok], wa_b[:], start=True, stop=True)
                            last.then_inc(wa_m, 1)
                        pe.sem_inc(pe_done, 1)

            @block.scalar
            def _(act):
                act.wait_ge(wrt, 1)
                act.copy(wr_t[:], xt_p[:]).then_inc(wrt_ok, 1)
                act.wait_ge(wrg, 1)
                act.copy(w_rg[:].rearrange("p c n -> p (c n)"), l_p[:, 0]).then_inc(wrg_ok, 1)
                act.wait_ge(zeroed, 2)
                with act.Fori(0, B // 2) as i:
                    for s in range(2):
                        b = i * 2 + s
                        b1 = act.snap(b + 1)
                        act.wait_ge(xt, b1)
                        act.wait_ge(pe_done, b1)
                        act.copy(x_t[:, s, :, 1:1 + T], xt_p[:]).then_inc(xt_ok, 1)
                        act.wait_ge(lora, b1)
                        act.activation(th[0:RL, s], l_p[0:RL, 0], ACT.Tanh)
                        act.copy(th[RL:P, s], l_p[RL:P, 0]).then_inc(th_ok, 1)
                        act.activation(sg[:, s], l_p[:, 1], ACT.Sigmoid).then_inc(th_ok, 1)
                        n = [act.snap(b * TT + t + 1) for t in range(TT)]
                        for t in range(TT):
                            act.wait_ge(rv, n[t])
                            act.wait_ge(stored[t], b1 * 32)
                            act.copy(coef[:, t, :, R_], hq(rv_p[t][:, 0]))
                            act.copy(coef[:, t, :, V_], hq(rv_p[t][:, 1])).then_inc(rv_ok, 1)
                            act.wait_ge(kk0_ok, n[t])
                            act.activation(sq[:, t], kk0[:, t], ACT.Square).then_inc(sq_ok, 1)
                            act.wait_ge(za_ok, n[t])
                            act.activation(wa[:, t], za[:, t], ACT.Sigmoid).then_inc(wa_ok, 1)
                        for t in range(TT):
                            act.wait_ge(wa_ok, n[t])
                            act.mul(coef[:, t, :, W_], hq(wa[:, t, 0:C]), EXP_HALF)
                        for t in range(TT):
                            act.wait_ge(kk_ok, n[t])
                            act.mul(coef[:, t, :, A_], hq(kk[:, t]), -1.0).then_inc(neg_ok, 1)

            @block.sync
            def _(sp):
                for n, name in enumerate(("W_r", "W_k", "W_v")):
                    sp.dma_start(w_rkv[:, n], d["L0_attn_" + name].rearrange("(c p) n -> p c n", p=P)).then_inc(wld, 16)
                sp.dma_start(lora_raw[:, :, 0:RL], d["L0_attn_w_lora_a"].rearrange("(c p) n -> p c n", p=P)).then_inc(wld, 16)
                sp.dma_start(lora_raw[:, :, RL:], d["L0_attn_a_lora_a"].rearrange("(c p) n -> p c n", p=P)).then_inc(wld, 16)
                sp.dma_start(ga[:], d["L0_attn_g_lora_a"].rearrange("(c p) n -> p c n", p=P)).then_inc(wld, 16)
                sp.dma_start(g_b[:], d["L0_attn_g_lora_b"]).then_inc(wld, 16)
                for n, m in enumerate(MIX):
                    sp.dma_start(mix_w[:, n], vec("x_" + m).rearrange("(c p) -> p c", p=P), allow_slow_non_contiguous=True).then_inc(wld, 16)
                for t, name in ((bias_wa[:, 0], "w_lora_bias"), (bias_wa[:, 1], "a_lora_bias"), (bias_g[:], "g_lora_bias"),
                                (kk_row[:], "k_k"), (ka_row[:], "k_a"), (rk_row[:], "r_k")):
                    sp.dma_start(t, vec(name).unsqueeze(0).broadcast_to([P, C])).then_inc(wld, 16)
                sp.wait_ge(zeroed, 1)
                sp.dma_start(wa_b[0:RL, 0:C], d["L0_attn_w_lora_b"]).then_inc(wld, 16)
                sp.dma_start(wa_b[RL:2 * RL, C:], d["L0_attn_a_lora_b"]).then_inc(wld, 16)
                sp.wait_ge(wld, 16 * 20)
                sp.sem_inc(wload, 1)
                def load_x(b, s, transposed):
                    sp.wait_ge(xt, transposed)
                    sp.dma_start(x_in[:, s], d["x"][bass.ds(b, 1)].rearrange("o (t p) c -> p (o t) c", p=P)).then_inc(x_ld[s], 16)

                def store(b):
                    for t in range(TT):
                        n1 = b * TT + t + 1
                        sp.wait_ge(neg_ok, n1)
                        sp.wait_ge(k_ok, n1)
                        sp.wait_ge(b_ok, n1)
                        sp.dma_start(coef_d[bass.ds(b, 1), :, t * P:(t + 1) * P].rearrange("o q t f -> t (o q) f"),
                                     coef[:, t].rearrange("p q n g -> p q (n g)")).then_inc(stored[t], 16)
                        sp.wait_ge(g_ok, n1)
                        sp.wait_ge(bonus_ok, n1)
                        sp.dma_start(bg_d[bass.ds((b * TT + t) * P, P)], bg[:, t].rearrange("p k c -> p (k c)")).then_inc(stored[t], 16)

                load_x(0, 0, 0)
                with sp.Fori(0, B // 2 - 1) as i:
                    load_x(i * 2 + 1, 1, i * 2)
                    store(i * 2)
                    load_x(i * 2 + 2, 0, i * 2 + 1)
                    store(i * 2 + 1)
                load_x(B - 1, 1, B - 2)
                store(B - 2)
                store(B - 1)
                for t in range(TT):
                    sp.wait_ge(stored[t], 32 * (B + 1))

            @block.vector
            def _(dve):
                dve.memset(wa_b[:], 0.0).then_inc(zeroed, 1)
                dve.memset(x_t[:, :, :, 0:1], 0.0).then_inc(zeroed, 1)
                for t in range(TT):
                    dve.sem_inc(stored[t], 32)
                dve.sem_inc(pe_done, 2)
                dve.wait_ge(wload, 1)
                dve.tensor_scalar(omx[:], mix_w[:], -1.0, 1.0, ALU.mult, ALU.add).then_inc(omx_ok, 1)
                dve.tensor_scalar(oma_row[:], ka_row[:], -1.0, 1.0, ALU.mult, ALU.add)
                dve.wait_ge(omx_ok, 1)
                for c in range(CC):
                    for n, col in ((3, slice(0, RL)), (4, slice(RL, 2 * RL))):
                        dve.tensor_scalar(w_lora[:, 0, c, col], lora_raw[:, c, col], omx[:, n, c:c + 1], None, ALU.mult)
                        last = dve.tensor_scalar(w_lora[:, 1, c, col], lora_raw[:, c, col], mix_w[:, n, c:c + 1], None, ALU.mult)
                last.then_inc(prep, 1)
                with dve.Fori(0, B // 2) as i:
                    for s in range(2):
                        b = i * 2 + s
                        b1 = dve.snap(b + 1)
                        dve.wait_ge(xt_ok, b1)
                        dve.wait_ge(mix_ok, b)
                        dve.tensor_tensor(delta[:], x_t[:, s, :, 0:T], x_t[:, s, :, 1:1 + T], ALU.subtract).then_inc(dlt, 1)
                        dve.wait_ge(dlt, b1)
                        for n in range(3):
                            for c in range(CC):
                                last = dve.scalar_tensor_tensor(mixed[:, s, n, c], delta[:, c], mix_w[:, n, c:c + 1],
                                                                x_t[:, s, c, 1:1 + T], ALU.mult, ALU.add)
                        last.then_inc(mix_ok, 1)
                        n = [dve.snap(b * TT + t + 1) for t in range(TT)]
                        for t in range(TT):
                            dve.wait_ge(stored[t], b1 * 32)
                            dve.wait_ge(g_m, n[t])
                            dve.tensor_tensor(kk0[:, t], kg_p[t][:, 0], kk_row[:], ALU.mult).then_inc(kk0_ok, 1)
                            dve.tensor_tensor(bg[:, t, 1], kg_p[t][:, 1], bias_g[:], ALU.add).then_inc(g_ok, 1)
                            dve.wait_ge(wa_m, n[t])
                            dve.tensor_tensor(za[:, t], wa_p[t][:], bias_wa[:].rearrange("p k c -> p (k c)"), ALU.add).then_inc(za_ok, 1)
                        for t in range(TT):
                            dve.wait_ge(sq_ok, n[t])
                            dve.tensor_reduce(ss[:, t], heads(sq[:, t]), AX.X, ALU.add).then_inc(ss_ok, 1)
                        dve.wait_ge(ss_ok, b * TT + TT)
                        dve.tensor_scalar(ss[:], ss[:], 1e-24, None, ALU.max).then_inc(newton, 1)
                        dve.wait_ge(newton, b * NEWTON + 1)
                        dve.tensor_scalar(inv[:].bitcast(I32), ss[:].bitcast(I32), 1, None, ALU.arith_shift_right).then_inc(newton, 1)
                        dve.wait_ge(newton, b * NEWTON + 2)
                        dve.tensor_scalar(inv[:].bitcast(I32), inv[:].bitcast(I32), -1.0, float(0x5f3759df), ALU.mult, ALU.add).then_inc(newton, 1)
                        for k in range(3):
                            dve.wait_ge(newton, b * NEWTON + 3 * k + 3)
                            dve.tensor_tensor(nt[:], inv[:], inv[:], ALU.mult).then_inc(newton, 1)
                            dve.wait_ge(newton, b * NEWTON + 3 * k + 4)
                            dve.scalar_tensor_tensor(nt[:], nt[:], -0.5, ss[:], ALU.mult, ALU.mult).then_inc(newton, 1)
                            dve.wait_ge(newton, b * NEWTON + 3 * k + 5)
                            dve.scalar_tensor_tensor(inv[:], nt[:], 1.5, inv[:], ALU.add, ALU.mult).then_inc(newton, 1)
                        dve.wait_ge(newton, b1 * NEWTON)
                        for t in range(TT):
                            dve.tensor_tensor(heads(kk[:, t]), heads(kk0[:, t]), over(inv[:, t]), ALU.mult).then_inc(kk_ok, 1)
                        for t in range(TT):
                            dve.wait_ge(u_ok, n[t])
                            dve.tensor_tensor(coef[:, t, :, K_], hq(kg_p[t][:, 0]), hq(u[:, t]), ALU.mult).then_inc(k_ok, 1)
                        for t in range(TT):
                            dve.wait_ge(rr_ok, n[t])
                            dve.tensor_reduce(bs[:, t], heads(rr[:, t]), AX.X, ALU.add).then_inc(bs_ok, 1)

            @block.gpsimd
            def _(pool):
                pool.wait_ge(prep, 1)
                with pool.Fori(0, B // 2) as i:
                    for s in range(2):
                        b = i * 2 + s
                        n = [pool.snap(b * TT + t + 1) for t in range(TT)]
                        a = [wa[:, t, C:2 * C] for t in range(TT)]
                        for t in range(TT):
                            pool.wait_ge(rv_ok, n[t])
                            pool.tensor_tensor(hq(rr[:, t]), coef[:, t, :, R_], hq(rk_row[:]), ALU.mult).then_inc(rr0_ok, 1)
                        for t in range(TT):
                            pool.wait_ge(wa_ok, n[t])
                            pool.tensor_tensor(u[:, t], a[t], ka_row[:], ALU.mult).then_inc(u0_ok, 1)
                        for t in range(TT):
                            pool.wait_ge(u0_ok, n[t])
                            pool.tensor_tensor(u[:, t], u[:, t], oma_row[:], ALU.add).then_inc(u_ok, 1)
                        for t in range(TT):
                            pool.wait_ge(kk_ok, n[t])
                            pool.tensor_tensor(coef[:, t, :, B_], hq(kk[:, t]), hq(a[t]), ALU.mult).then_inc(b_ok, 1)
                        for t in range(TT):
                            pool.wait_ge(rr0_ok, n[t])
                            pool.wait_ge(k_ok, n[t])
                            pool.tensor_tensor(hq(rr[:, t]), hq(rr[:, t]), coef[:, t, :, K_], ALU.mult).then_inc(rr_ok, 1)
                        for t in range(TT):
                            pool.wait_ge(bs_ok, n[t])
                            pool.tensor_tensor(bg[:, t, 0].rearrange("p (q h e) -> p q h e", q=Q, h=HQ),
                                               coef[:, t, :, V_].rearrange("p q (h e) -> p q h e", h=HQ),
                                               bs[:, t].rearrange("p (q h) -> p q h", q=Q).unsqueeze(3).broadcast_to([P, Q, HQ, D]),
                                               ALU.mult).then_inc(bonus_ok, 1)


def scan(nc, d, ident, zero, coef_d, o_d, w13, xs_d, s_w13, s_xs0):
    ctx = ExitStack()
    with ctx:
        def sb(name, shape, dt=F32):
            return ctx.enter_context(nc.sbuf_tensor(name, shape, dt))

        def sem(name):
            return nc.alloc_semaphore(name)

        CS = 3
        NBK = T // TB
        coef = sb("sc_coef", [P, 2, TB, NC6, G])
        state = sb("sc_state", [P, 2, D, G])
        ta = sb("sc_ta", [P, D, G])
        sa = sb("sc_sa", [P, G])
        y = sb("sc_y", [P, 2, D, G])
        x = sb("sc_x", [P, 2, D, G])
        z = sb("sc_z", [P, D, G])
        r = sb("sc_r", [P, 2, D, G])
        LAG = 3
        JP = 4
        part = sb("sc_part", [P, 2, TB, JP, G])
        o_sb = sb("sc_o", [P, 2, TB, G])
        xy_p = [ctx.enter_context(nc.psum_tensor(f"sc_xy_p{i}", [P, D, G], F32)) for i in range(2)]
        r_p = [ctx.enter_context(nc.psum_tensor(f"sc_r_p{i}", [P, 512], F32)) for i in range(2)]
        o_p = [ctx.enter_context(nc.psum_tensor(f"sc_o_p{i}", [P, TB, G], F32)) for i in range(2)]
        ld = [sem(f"c_ld{i}") for i in range(2)]
        stored = [sem(f"c_stored{i}") for i in range(2)]
        used = sem("c_used")
        ta_ok, sa_ok, y_ok, x_ok, xy_ok, z_ok, s_ok, r_ok, r_sum, part_ok, o_m, o_ok = (
            sem("c_" + n) for n in ("ta", "sa", "y", "x", "xy", "z", "s", "r", "r_sum", "part", "o_m", "o"))
        w13_v = d["L0_ffn_moe_w13"].rearrange("e k n -> (e k) n")
        xs_v = xs_d.rearrange("(n p) c -> p n c", p=P)
        ZN = SLOTT // (NBK // 2)
        assert NE * CC == NBK // 2 and 0 < SLOTT - ZN * NBK // 2
        coef_v = coef_d.rearrange("b q t f -> (b q) t f")
        o_v = o_d.rearrange("b q t g -> (b q) t g")

        def heads(ap):
            return ap.rearrange("p j (h i) -> p j h i", h=HQ)

        def by_j(s, k, c):
            return coef[:, s, k, c].rearrange("p (h j) -> p j h", j=D).unsqueeze(3).broadcast_to([P, D, HQ, D])

        def by_i(ap):
            return ap.rearrange("p (h i) -> p h i", h=HQ).unsqueeze(1).broadcast_to([P, D, HQ, D])

        with nc.Block() as block:
            @block.sync
            def _(sp):
                with sp.Fori(0, NBK // 2) as i:
                    for s in range(2):
                        blk = i * 2 + s
                        sp.wait_ge(used, blk + 1)
                        sp.dma_start(coef[:, s].rearrange("p t n g -> p t (n g)"), coef_v[:, bass.ds(blk * TB, TB)]).then_inc(ld[s], 16)
                    sp.dma_start(w13[:, bass.ds(i * (2 * MD), 2 * MD)], w13_v[bass.ds(i * P, P)]).then_inc(s_w13, 16)
                    sp.dma_start(xs_v[:, bass.ds(i * ZN, ZN)], zero[:].unsqueeze(1).broadcast_to([P, ZN, C])).then_inc(s_xs0, 16)
                sp.dma_start(xs_v[:, ZN * NBK // 2:], zero[:].unsqueeze(1).broadcast_to([P, SLOTT - ZN * NBK // 2, C])).then_inc(s_xs0, 16)

            @block.gpsimd
            def _(pool):
                def read_out(s, k, t1):
                    pool.wait_ge(r_sum, t1)
                    pool.tensor_tensor(heads(r[:, k % 2]), heads(state[:, k % 2]), by_j(s, k, R_), ALU.mult).then_inc(r_ok, 1)

                def steps(blk, s, first):
                    pool.wait_ge(ld[s], (blk // 2 + 1) * 16 if first else (blk + 1) * 16)
                    for k in range(TB):
                        p = k % 2
                        t = k + s * TB if first else pool.snap((blk * 2 + s) * TB + k)
                        t1 = t + 1 if first else pool.snap(t + 1)
                        pool.wait_ge(xy_ok, t1)
                        pool.tensor_tensor(heads(x[:, p]), by_i(coef[:, s, k, V_]), by_j(s, k, K_), ALU.mult).then_inc(x_ok, 1)
                        pool.wait_ge(s_ok, t1)
                        pool.tensor_tensor(heads(y[:, p]), heads(state[:, 1 - p]), by_j(s, k, W_), ALU.mult).then_inc(y_ok, 1)
                        if not (first and s == 0 and k == 0):
                            read_out(s if k else 1 - s, (k - 1) % TB, t)
                            if k == 0:
                                pool.wait_ge(r_ok, t)
                                pool.sem_inc(used, 1)

                pool.sem_inc(used, 2)
                pool.sem_inc(xy_ok, 2)
                pool.sem_inc(r_sum, 2)
                for s in range(2):
                    steps(s, s, True)
                with pool.Fori(1, NBK // 2) as i:
                    for s in range(2):
                        steps(i, s, False)
                pool.wait_ge(s_ok, T + 1)
                read_out(1, TB - 1, T)

            @block.vector
            def _(dve):
                dve.memset(state[:], 0.0).then_inc(s_ok, 1)
                with dve.Fori(0, NBK // 2) as i:
                    for s in range(2):
                        dve.wait_ge(ld[s], (i + 1) * 16)
                        for k in range(TB):
                            p = k % 2
                            t = dve.snap((i * 2 + s) * TB + k)
                            t1 = dve.snap(t + 1)
                            dve.wait_ge(s_ok, t1)
                            dve.tensor_tensor(heads(ta[:]), heads(state[:, 1 - p]), by_j(s, k, A_), ALU.mult).then_inc(ta_ok, 1)
                            dve.wait_ge(ta_ok, t1)
                            dve.tensor_reduce(sa[:], ta[:].rearrange("p j g -> p g j"), AX.X, ALU.add).then_inc(sa_ok, 1)
                            dve.wait_ge(sa_ok, t1)
                            dve.tensor_tensor(heads(z[:]), by_i(sa[:]), by_j(s, k, B_), ALU.mult).then_inc(z_ok, 1)
                            dve.wait_ge(z_ok, t1)
                            dve.wait_ge(xy_ok, t + 3)
                            dve.tensor_tensor(state[:, p], xy_p[p][:], z[:], ALU.add).then_inc(s_ok, 1)

            @block.tensor
            def _(pe):
                HJ = D // 2

                def add(src, p, start):
                    for h in range(2):
                        last = pe.matmul(xy_p[p][:, h * HJ:(h + 1) * HJ].rearrange("p j g -> p (j g)"), ident[:],
                                         src[:, p, h * HJ:(h + 1) * HJ].rearrange("p j g -> p (j g)"), start=start, stop=not start)
                    return last

                def sum_r(p, t1):
                    pe.wait_ge(r_ok, t1)
                    pe.wait_ge(part_ok, t1)
                    for j in range(D // JP):
                        last = pe.matmul(r_p[p][:, 0:JP * G], ident[:], r[:, p, j * JP:(j + 1) * JP].rearrange("p j g -> p (j g)"),
                                         start=j == 0, stop=j == D // JP - 1)
                    last.then_inc(r_sum, 1)

                def sum_parts(s, blk1):
                    pe.wait_ge(part_ok, blk1 * TB + 2)
                    pe.wait_ge(o_ok, blk1)
                    for j in range(JP):
                        last = pe.matmul(o_p[s][:], ident[:], part[:, s, :, j], start=j == 0, stop=j == JP - 1)
                    last.then_inc(o_m, 1)

                def steps(i, s, first):
                    for k in range(TB):
                        p = k % 2
                        t = s * TB + k if first else pe.snap((i * 2 + s) * TB + k)
                        t1 = t + 1 if first else pe.snap(t + 1)
                        pe.wait_ge(x_ok, t1)
                        if not (first and s == 0 and k == 0):
                            pe.wait_ge(s_ok, t)
                        add(x, p, True)
                        pe.wait_ge(y_ok, t1)
                        add(y, p, False).then_inc(xy_ok, 1)
                        if not (first and s == 0 and k == 0):
                            sum_r(1 - p, t)
                        if k == LAG - 1 and not (first and s == 0):
                            sum_parts(1 - s, i * 2 + s)

                for s in range(2):
                    steps(0, s, True)
                with pe.Fori(1, NBK // 2) as i:
                    for s in range(2):
                        steps(i, s, False)
                sum_r(1, T)
                sum_parts(1, NBK)

            @block.scalar
            def _(act):
                for s in range(2):
                    act.sem_inc(stored[s], 16)
                act.sem_inc(part_ok, 2)
                act.sem_inc(o_ok, 2)

                def steps(i, s, ks):
                    for k in ks:
                        t = act.snap((i * 2 + s) * TB + k)
                        act.wait_ge(r_sum, t + 3)
                        act.copy(part[:, s, k].rearrange("p j g -> p (j g)"), r_p[k % 2][:, 0:JP * G]).then_inc(part_ok, 1)

                def leave(s, blk1):
                    act.wait_ge(o_m, blk1)
                    act.wait_ge(stored[s], (blk1 + 1) // 2 * 16 if isinstance(blk1, int) else (i + 1 - s) * 16)
                    act.copy(o_sb[:, s], o_p[s][:]).then_inc(o_ok, 1)
                    act.wait_ge(o_ok, blk1 + 2)
                    act.dma_start(o_v[:, bass.ds((blk1 - 1) * TB, TB)], o_sb[:, s]).then_inc(stored[s], 16)

                steps(0, 0, range(TB))
                steps(0, 1, range(LAG))
                leave(0, 1)
                steps(0, 1, range(LAG, TB))
                with act.Fori(1, NBK // 2) as i:
                    for s in range(2):
                        steps(i, s, range(LAG))
                        leave(1 - s, act.snap(i * 2 + s))
                        steps(i, s, range(LAG, TB))
                leave(1, NBK)
                for s in range(2):
                    act.wait_ge(stored[s], 16 * (NBK // 2 + 1))


def attend(nc, d, ident, o_d, bg_d, x2_d, logits):
    ctx = ExitStack()
    with ctx:
        def sb(name, shape, dt=F32):
            return ctx.enter_context(nc.sbuf_tensor(name, shape, dt))

        def ps(name, shape):
            return ctx.enter_context(nc.psum_tensor(name, shape, F32))

        HC = H // CC
        HB = HC // 2
        HV = HB * D
        SG = H // HB
        assert HB * LKV <= 512 and 2 * HV == P
        w_o = sb("w_o", [P, CC, C])
        w_q = sb("w_q", [P, CC, C])
        w_k = sb("w_k", [CD, C])
        w_v = sb("w_v", [CD, C])
        w_xo = sb("w_xo", [P, CC, C])
        router = sb("router", [P, CC, NE])
        b_q = sb("b_q", [P, CC])
        b_k = sb("b_k", [P, CC])
        b_ks = sb("b_ks", [P, CC])
        bv_row = sb("bv_row", [P, C])
        bo_row = sb("bo_row", [P, C])
        gw_row = sb("gw_row", [P, C])
        gb_row = sb("gb_row", [P, C])
        own = sb("own", [P, HC])
        eps = sb("eps", [P, 1])

        o_in = sb("o_in", [P, TT, Q, G])
        bg_in = sb("bg_in", [P, TT, 2, C])
        x_in = sb("a_x_in", [P, TT, C])
        ctx_in = sb("ctx_in", [LKV, CD])
        mu = sb("mu", [P, TT * H])
        oc = sb("oc", [P, TT, C])
        sq = sb("a_sq", [P, TT, C])
        ss = sb("a_ss", [P, TT * H])
        sd = sb("sd", [P, TT * H])
        rs = sb("rs", [P, TT * H])
        zz = sb("zz", [P, TT, C])
        z_t = sb("z_t", [P, CC, T])
        y1 = sb("y1", [P, TT, C])
        x1 = sb("x1", [P, TT, C])
        x1b = sb("x1b", [P, 2, TT, C])
        x1_t = sb("x1_t", [P, CC, T])
        q_t = sb("q_t", [P, CC, T])
        ctx_t = sb("ctx_t", [CD, LKV])
        k_t = sb("k_t", [P, CC, LKV])
        k_own = sb("k_own", [P, CC, HC, LKV])
        v_own = sb("v_own", [LKV, 2, H, P])
        mx = sb("mx", [P, TT, CC, HC])
        pr = sb("pr", [P, TT, CC, HC, LKV])
        p_t = sb("p_t", [LKV, H, T])
        rden = sb("rden", [HV, CC, 2 * T])
        at_t = sb("at_t", [P, CC, T])
        y2 = sb("y2", [P, TT, C])
        x2 = sb("x2", [P, TT, C])
        x2_t = sb("x2_t", [P, CC, T])
        norms = {n: [sb(f"{n}_{k}", [P, TT, w]) for k, w in (("bn6", 6), ("mv", 2), ("std", 1), ("rstd", 1))] for n in ("n1", "n2")}

        a_p = ps("a_p", [P, 512])
        c_p = ps("c_p", [P, 512])
        sc_p = [ps(f"sc_p{i}", [P, 2, 512]) for i in range(CC)]
        pt_p = [ps(f"pt_p{i}", [P, HB, P]) for i in range(2)]
        pv_p = sc_p[1]

        names = ("wld zeroed own wload consts ld_o ld_bg ld_x ld_ctx x2_st mu oc sq ss sd rs zz z1 z2 z3 z zt zt_ok y y1 bn1 mv1 std1 "
                 "rstd1 x1 x1b x1t x1t_ok q q_ok ctx ctx_ok kv k_ok v_ok k_own sc mx sub ex pt pt_ok pv rden at y2 y2_ok "
                 "bn2 mv2 std2 rstd2 x2 x2t x2t_ok lg lg_ok passed")
        S = {n: nc.alloc_semaphore("a_" + n) for n in names.split()}

        def wait(eng, name, value):
            if not (isinstance(value, int) and value <= 0):
                eng.wait_ge(S[name], value)

        def row(name):
            return d[name].unsqueeze(0).broadcast_to([P, C])

        def flat(ap):
            return ap.rearrange("p a b -> p (a b)")

        def heads(ap):
            return ap.rearrange("p t (h e) -> p (t h) e", h=H)

        def over(ap):
            return ap.unsqueeze(2).broadcast_to([P, TT * H, D])

        def rounds(eng, G_A_B_C):
            def one(j, par):
                G_A_B_C(j, par, True, True, True, True)
            for j in range(4):
                G_A_B_C(j, j % 2, True, j >= 1, j >= 2, j >= 3)
            with eng.Fori(2, B // 2) as i:
                for par in range(2):
                    one(eng.snap(i * 2 + par), par)
            for j in range(B, B + 3):
                G_A_B_C(j, j % 2, False, j < B + 1, j < B + 2, True)

        loads = [(w_o[:], d["L0_attn_W_o"].rearrange("(c p) n -> p c n", p=P)),
                 (w_q[:], d["L0_xattn_Wq"].rearrange("(c p) n -> p c n", p=P)),
                 (w_k[:], d["L0_xattn_Wk"]), (w_v[:], d["L0_xattn_Wv"]),
                 (w_xo[:], d["L0_xattn_Wo"].rearrange("(c p) n -> p c n", p=P)),
                 (router[:], d["L0_ffn_moe_router"].rearrange("(c p) n -> p c n", p=P)),
                 (bv_row[:], row("L0_xattn_bv")), (bo_row[:], row("L0_xattn_bo")),
                 (gw_row[:], row("L0_attn_gn_weight")), (gb_row[:], row("L0_attn_gn_bias")),
                 (b_q[:], d["L0_xattn_bq"].rearrange("(c p) -> p c", p=P)),
                 (b_k[:], d["L0_xattn_bk"].rearrange("(c p) -> p c", p=P))]

        with nc.Block() as block:
            @block.sync
            def _(sp):
                for dst, src in loads:
                    sp.dma_start(dst, src, allow_slow_non_contiguous=True).then_inc(S["wld"], 16)
                sp.wait_ge(S["wld"], 16 * len(loads))
                sp.sem_inc(S["wload"], 1)

                def load(j, par, g, a, b, c):
                    if g:
                        wait(sp, "oc", j)
                        for t in range(TT):
                            sp.dma_start(o_in[:, t], o_d[bass.ds(j, 1), :, t * P:(t + 1) * P].rearrange("o q p g -> p (o q) g")).then_inc(S["ld_o"], 16)
                    if a:
                        wait(sp, "y1", j - 1)
                        sp.dma_start(x_in[:], d["x"][bass.ds(j - 1, 1)].rearrange("o (t p) c -> p (o t) c", p=P)).then_inc(S["ld_x"], 16)
                        wait(sp, "ctx", j - 1)
                        sp.dma_start(ctx_in[:], d["ctx_512"][bass.ds(j - 1, 1)].rearrange("o k c -> (o k) c")).then_inc(S["ld_ctx"], 16)
                    if g:
                        wait(sp, "z", j)
                        sp.dma_start(bg_in[:].rearrange("p t k c -> p t (k c)"),
                                     bg_d[bass.ds(j * T, T)].rearrange("(t p) f -> p t f", p=P)).then_inc(S["ld_bg"], 16)
                rounds(sp, load)

            @block.tensor
            def _(pe):
                pe.wait_ge(S["wload"], 1)
                pe.wait_ge(S["consts"], 2)

                def turn(dst, src):
                    for t in range(TT):
                        for c in range(CC):
                            last = pe.transpose(dst[:, c * T + t * P:c * T + (t + 1) * P], src[:, t, c * P:(c + 1) * P], ident[:])
                    return last

                def times(dst, src_t, w, cols):
                    for t in range(TT):
                        for c in range(CC):
                            last = pe.matmul(dst[:, t * cols:(t + 1) * cols], src_t[:, c, t * P:(t + 1) * P], w[:, c],
                                             start=c == 0, stop=c == CC - 1)
                    return last

                def scores(b, t, c):
                    n = b * (TT * CC) + t * CC + c
                    if t == 0:
                        wait(pe, "q_ok", b + 1)
                        wait(pe, "k_own", b + 1)
                        if c == 1:
                            wait(pe, "at", b)
                    wait(pe, "sub", n - 1)
                    for f in range(2):
                        last = pe.matmul(sc_p[c][:, f, 0:HB * LKV], q_t[:, c, t * P:(t + 1) * P],
                                         k_own[:, c, f * HB:(f + 1) * HB].rearrange("p h k -> p (h k)"), start=True, stop=True)
                    last.then_inc(S["sc"], 1)

                def turn_probs(b, t):
                    for g in range(SG):
                        n = b * (TT * SG) + t * SG + g
                        if g % 2 == 0:
                            wait(pe, "ex", b * (TT * CC) + t * CC + g // 2 + 1)
                        wait(pe, "pt_ok", n - 1)
                        for h in range(HB):
                            last = pe.transpose(pt_p[g % 2][0:LKV, h], pr[:, t, g // 2, (g % 2) * HB + h], ident[:])
                        last.then_inc(S["pt"], 1)

                def round_(j, par, g, a, b, c):
                    if b:
                        scores(j - 2, 0, 0)
                    if c:
                        wait(pe, "at", j - 2)
                        wait(pe, "lg_ok", j - 3)
                        times(c_p, at_t, w_xo, C).then_inc(S["y2"], 1)
                    if b:
                        scores(j - 2, 0, 1)
                    if a:
                        wait(pe, "z", j)
                        wait(pe, "q_ok", j - 1)
                        turn(a_p, zz).then_inc(S["zt"], 1)
                    if b:
                        scores(j - 2, 1, 0)
                    if a:
                        wait(pe, "zt_ok", j)
                        times(a_p, z_t, w_o, C).then_inc(S["y"], 1)
                    if b:
                        scores(j - 2, 1, 1)
                    if a:
                        wait(pe, "y1", j)
                        wait(pe, "ld_ctx", j * 16)
                        pe.transpose(a_p[:, 0:LKV], ctx_in[:], ident[0:LKV, 0:LKV]).then_inc(S["ctx"], 1)
                    if c:
                        wait(pe, "x2", j - 2)
                        turn(c_p, x2).then_inc(S["x2t"], 1)
                    if b:
                        turn_probs(j - 2, 0)
                    if a:
                        wait(pe, "ctx_ok", j)
                        for m in range(CC):
                            pe.matmul(a_p[:, m * LKV:(m + 1) * LKV], w_k[:, m * P:(m + 1) * P], ctx_t[:], start=True, stop=True)
                        pe.matmul(a_p[0:LKV, CC * LKV:CC * LKV + C], ctx_t[:], w_v[:], start=True, stop=True).then_inc(S["kv"], 1)
                    if b:
                        turn_probs(j - 2, 1)
                    if a:
                        wait(pe, "x1", j)
                        wait(pe, "k_ok", j)
                        wait(pe, "v_ok", j)
                        turn(a_p, x1).then_inc(S["x1t"], 1)
                    if c:
                        wait(pe, "x2t_ok", j - 2)
                        times(c_p, x2_t, router, NE).then_inc(S["lg"], 1)
                    if b:
                        wait(pe, "sub", (j - 1) * (TT * CC))
                        for g in range(SG):
                            if g == 0:
                                wait(pe, "pt_ok", (j - 1) * (TT * SG))
                            if g == 2 and a:
                                wait(pe, "x1t_ok", j)
                                for m in range(CC):
                                    for k in range(CC):
                                        last = pe.matmul(a_p[:, m * T:(m + 1) * T], w_q[:, k, m * P:(m + 1) * P], x1_t[:, k],
                                                         start=k == 0, stop=k == CC - 1)
                                last.then_inc(S["q"], 1)
                            for h in range(HB):
                                last = pe.matmul(pv_p[:, g // 2, (g % 2) * T:(g % 2 + 1) * T], v_own[:, par, g * HB + h], p_t[:, g * HB + h],
                                                 start=h == 0, stop=h == HB - 1)
                            if g % 2:
                                last.then_inc(S["pv"], 1)
                    elif a:
                        wait(pe, "x1t_ok", j)
                        for m in range(CC):
                            for k in range(CC):
                                last = pe.matmul(a_p[:, m * T:(m + 1) * T], w_q[:, k, m * P:(m + 1) * P], x1_t[:, k],
                                                 start=k == 0, stop=k == CC - 1)
                        last.then_inc(S["q"], 1)
                rounds(pe, round_)

            @block.scalar
            def _(act):
                act.wait_ge(S["wload"], 1)
                act.wait_ge(S["consts"], 2)
                act.mul(b_ks[:], b_k[:], 0.25)

                def leave_probs(b, t):
                    for g in range(SG):
                        wait(act, "pt", b * (TT * SG) + t * SG + g + 1)
                        if t == 0 and g == 0:
                            wait(act, "pv", b * 2)
                        act.copy(p_t[:, g * HB:(g + 1) * HB, t * P:(t + 1) * P], pt_p[g % 2][0:LKV]).then_inc(S["pt_ok"], 1)

                def exp(b, t, c):
                    wait(act, "sub", b * (TT * CC) + t * CC + c + 1)
                    act.activation(pr[:, t, c], pr[:, t, c], ACT.Exp).then_inc(S["ex"], 1)

                def round_(j, par, g, a, b, c):
                    if g:
                        wait(act, "oc", j + 1)
                        act.activation(flat(sq[:]), flat(oc[:]), ACT.Square).then_inc(S["sq"], 1)
                    if a:
                        wait(act, "zt", j)
                        act.copy(flat(z_t[:]), a_p[:]).then_inc(S["zt_ok"], 1)
                    if c:
                        bn6, mv, std, rstd = norms["n2"]
                        wait(act, "mv2", j - 2)
                        act.activation(std[:], mv[:, :, 1:2], ACT.Sqrt, bias=eps[:]).then_inc(S["std2"], 1)
                    if g:
                        wait(act, "ss", j + 1)
                        act.activation(sd[:], ss[:], ACT.Sqrt, bias=eps[:], scale=1.0 / D).then_inc(S["sd"], 1)
                    if b:
                        exp(j - 2, 0, 0)
                        exp(j - 2, 0, 1)
                    if c:
                        wait(act, "x2t", j - 2)
                        act.copy(flat(x2_t[:]), c_p[:]).then_inc(S["x2t_ok"], 1)
                        act.dma_start(x2_d[bass.ds((j - 3) * T, T)].rearrange("(t p) c -> p t c", p=P), x2[:]).then_inc(S["x2_st"], 16)
                    if b:
                        leave_probs(j - 2, 0)
                        exp(j - 2, 1, 0)
                        exp(j - 2, 1, 1)
                    if a:
                        wait(act, "ctx", j)
                        act.copy(ctx_t[:], a_p[:, 0:LKV]).then_inc(S["ctx_ok"], 1)
                        bn6, mv, std, rstd = norms["n1"]
                        wait(act, "mv1", j)
                        act.activation(std[:], mv[:, :, 1:2], ACT.Sqrt, bias=eps[:]).then_inc(S["std1"], 1)
                        wait(act, "kv", j)
                        wait(act, "k_own", j - 1)
                        for m in range(CC):
                            last = act.activation(k_t[:, m], a_p[:, m * LKV:(m + 1) * LKV], ACT.Identity, bias=b_ks[:, m:m + 1], scale=0.25)
                        last.then_inc(S["k_ok"], 1)
                    if b:
                        leave_probs(j - 2, 1)
                    if a:
                        wait(act, "x1t", j)
                        act.copy(flat(x1_t[:]), a_p[:]).then_inc(S["x1t_ok"], 1)
                        wait(act, "q", j)
                        wait(act, "sc", (j - 1) * (TT * CC))
                        for m in range(CC):
                            last = act.activation(q_t[:, m], a_p[:, m * T:(m + 1) * T], ACT.Identity, bias=b_q[:, m:m + 1])
                        last.then_inc(S["q_ok"], 1)
                rounds(act, round_)
                act.wait_ge(S["x2_st"], B * 16)

            @block.vector
            def _(dve):
                dve.memset(v_own[:], 0.0).then_inc(S["zeroed"], 1)
                dve.wait_ge(S["zeroed"], 1)
                for h in range(HB):
                    for s in range(2):
                        dve.memset(v_own[:, s].rearrange("p (g h) n -> p g h n", h=HB)[:, :, h, HV + h * D:HV + (h + 1) * D], 1.0)
                dve.memset(eps[:], EPS).then_inc(S["consts"], 1)
                dve.wait_ge(S["wload"], 1)

                def moments(n, src, bn_s, mv_s, value):
                    bn6, mv, std, rstd = norms[n]
                    for t in range(TT):
                        last = dve.bn_stats(bn6[:, t], src[:, t])
                    last.then_inc(S[bn_s], 1)
                    wait(dve, bn_s, value)
                    dve.sem_inc(S["passed"], 1)
                    for t in range(TT):
                        last = dve.bn_aggr(mv[:, t], bn6[:, t])
                    last.then_inc(S[mv_s], 1)

                def normalise(n, dst, src, std_s, rstd_s, done, value):
                    bn6, mv, std, rstd = norms[n]
                    wait(dve, std_s, value)
                    dve.reciprocal(rstd[:], std[:]).then_inc(S[rstd_s], 1)
                    wait(dve, rstd_s, value)
                    for t in range(TT):
                        last = dve.tensor_scalar(dst[:, t], src[:, t], mv[:, t, 0:1], rstd[:, t], ALU.subtract, ALU.mult)
                    last.then_inc(S[done], 1)

                def shift(b, t, c):
                    n = b * (TT * CC) + t * CC + c + 1
                    wait(dve, "sc", n)
                    view = sc_p[c][:, :, 0:HB * LKV].rearrange("p f (h k) -> p f h k", h=HB)
                    m = mx[:, t, c].rearrange("p (f h) -> p f h", f=2)
                    wait(dve, "sub", n - TT * CC)
                    dve.tensor_reduce(m, view, AX.X, ALU.max).then_inc(S["mx"], 1)
                    wait(dve, "mx", n)
                    if c == 0:
                        wait(dve, "pt", (b - 1) * (TT * SG) + (t + 1) * SG)
                    dve.tensor_tensor(pr[:, t, c].rearrange("p (f h) k -> p f h k", f=2), view,
                                      m.unsqueeze(3).broadcast_to([P, 2, HB, LKV]), ALU.subtract).then_inc(S["sub"], 1)

                def round_(j, par, g, a, b, c):
                    if g:
                        src = o_in[:].rearrange("p t q (h e) -> p (t q h) e", e=D)
                        wait(dve, "ld_o", (j + 1) * (16 * TT))
                        dve.tensor_reduce(mu[:], src, AX.X, ALU.add).then_inc(S["mu"], 1)
                        wait(dve, "mu", j + 1)
                        wait(dve, "zz", j)
                        dve.scalar_tensor_tensor(heads(oc[:]), over(mu[:]), -1.0 / D, src, ALU.mult, ALU.add).then_inc(S["oc"], 1)
                    if b:
                        shift(j - 2, 0, 0)
                    if c:
                        wait(dve, "y2", j - 2)
                        wait(dve, "x1b", j - 2)
                        wait(dve, "x2", j - 3)
                        dve.tensor_tensor(flat(y2[:]), c_p[:], flat(x1b[:, 1 - par]), ALU.add).then_inc(S["y2_ok"], 1)
                        wait(dve, "y2_ok", j - 2)
                        moments("n2", y2, "bn2", "mv2", j - 2)
                    if b:
                        shift(j - 2, 0, 1)
                    if g:
                        wait(dve, "sq", j + 1)
                        wait(dve, "sd", j)
                        dve.tensor_reduce(ss[:], heads(sq[:]), AX.X, ALU.add).then_inc(S["ss"], 1)
                    if c:
                        wait(dve, "x2_st", (j - 3) * 16)
                        wait(dve, "x2t", j - 3)
                        normalise("n2", x2, y2, "std2", "rstd2", "x2", j - 2)
                    if b:
                        shift(j - 2, 1, 0)
                        shift(j - 2, 1, 1)
                    if a:
                        wait(dve, "y", j)
                        wait(dve, "ld_x", j * 16)
                        wait(dve, "x1", j - 1)
                        dve.tensor_tensor(flat(y1[:]), a_p[:], flat(x_in[:]), ALU.add).then_inc(S["y1"], 1)
                        wait(dve, "y1", j)
                        moments("n1", y1, "bn1", "mv1", j)
                    if g:
                        wait(dve, "sd", j + 1)
                        wait(dve, "zz", j)
                        dve.reciprocal(rs[:], sd[:]).then_inc(S["rs"], 1)
                        wait(dve, "rs", j + 1)
                        wait(dve, "zt", j)
                        dve.tensor_tensor(heads(zz[:]), heads(oc[:]), over(rs[:]), ALU.mult).then_inc(S["zz"], 1)
                    if a:
                        wait(dve, "x1b", j - 1)
                        wait(dve, "x1t", j - 1)
                        normalise("n1", x1, y1, "std1", "rstd1", "x1", j)
                        wait(dve, "kv", j)
                        wait(dve, "k_ok", j)
                        wait(dve, "pv", (j - 2) * 2)
                        for h in range(HB):
                            last = dve.tensor_tensor(
                                v_own[:, 1 - par].rearrange("p (g h) n -> p g h n", h=HB)[:, :, h, h * D:(h + 1) * D],
                                a_p[0:LKV, CC * LKV:CC * LKV + C].rearrange("p (g h e) -> p g h e", h=HB, e=D)[:, :, h],
                                bv_row[0:LKV].rearrange("p (g h e) -> p g h e", h=HB, e=D)[:, :, h], ALU.add)
                        last.then_inc(S["v_ok"], 1)
                    if c:
                        wait(dve, "lg", j - 2)
                        dve.tensor_copy(logits[:, bass.ds((j - 3) * TT, TT)].rearrange("p t e -> p (t e)"), c_p[:, 0:TT * NE]).then_inc(S["lg_ok"], 1)
                    if b:
                        for f in range(CC):
                            n = (j - 2) * 2 + f + 1
                            wait(dve, "pv", n)
                            wait(dve, "at", j - 2)
                            dve.reciprocal(rden[:, f], pv_p[HV:2 * HV, f]).then_inc(S["rden"], 1)
                            wait(dve, "rden", n)
                            wait(dve, "y2", j - 2)
                            for e in range(2):
                                last = dve.tensor_tensor(at_t[e * HV:(e + 1) * HV, f], pv_p[0:HV, f, e * T:(e + 1) * T],
                                                         rden[:, f, e * T:(e + 1) * T], ALU.mult)
                        last.then_inc(S["at"], 1)
                rounds(dve, round_)

            @block.gpsimd
            def _(pool):
                pool.memset(own[:], 1.0).then_inc(S["own"], 1)
                pool.wait_ge(S["own"], 1)
                pool.affine_select(out=own[:], in_=own[:], compare_op=ALU.is_ge, fill=0.0, base=0,
                                   pattern=[[-D, HC]], channel_multiplier=1).then_inc(S["own"], 1)
                pool.wait_ge(S["own"], 2)
                pool.affine_select(out=own[:], in_=own[:], compare_op=ALU.is_ge, fill=0.0, base=D - 1,
                                   pattern=[[D, HC]], channel_multiplier=-1).then_inc(S["consts"], 1)
                pool.wait_ge(S["consts"], 2)
                pool.wait_ge(S["wload"], 1)

                def round_(j, par, g, a, b, c):
                    def tiles(ap):
                        return ap.unsqueeze(1).broadcast_to([P, TT, C])
                    if g:
                        wait(pool, "zz", j + 1)
                        pool.tensor_tensor(zz[:], zz[:], tiles(gw_row[:]), ALU.mult).then_inc(S["z1"], 1)
                        wait(pool, "z1", j + 1)
                        pool.tensor_tensor(zz[:], zz[:], tiles(gb_row[:]), ALU.add).then_inc(S["z2"], 1)
                        wait(pool, "z2", j + 1)
                        wait(pool, "ld_bg", (j + 1) * 16)
                        pool.tensor_tensor(zz[:], zz[:], bg_in[:, :, 0], ALU.add).then_inc(S["z3"], 1)
                        wait(pool, "z3", j + 1)
                        pool.tensor_tensor(zz[:], zz[:], bg_in[:, :, 1], ALU.mult).then_inc(S["z"], 1)
                    if a:
                        wait(pool, "k_ok", j)
                        wait(pool, "sc", (j - 1) * (TT * CC))
                        for m in range(CC):
                            last = pool.tensor_tensor(k_own[:, m], k_t[:, m].unsqueeze(1).broadcast_to([P, HC, LKV]),
                                                      own[:].unsqueeze(2).broadcast_to([P, HC, LKV]), ALU.mult)
                        last.then_inc(S["k_own"], 1)
                        wait(pool, "x1", j)
                        wait(pool, "x2", j - 3)
                        pool.tensor_tensor(x1b[:, 1 - par], x1[:], tiles(bo_row[:]), ALU.add).then_inc(S["x1b"], 1)
                rounds(pool, round_)


def dispatch(nc, d, logits, slots, gates, tile_expert, w2, s_w2):
    ctx = ExitStack()
    with ctx:
        def sb(name, shape, dt=F32):
            return ctx.enter_context(nc.sbuf_tensor(name, shape, dt))

        def sem(name):
            return nc.alloc_semaphore(name)

        FULL = [P, NT, NE]
        e_int = sb("e_int", [P, NE], I32)
        j_int = sb("j_int", [1, SLOTT], I32)
        e_row, e8_row = sb("e_row", [P, NE]), sb("e8_row", [P, NE])
        j_row = sb("j_row", [1, SLOTT])
        before = sb("before", [P, P])
        ones = sb("ones", [P, P])
        top = [sb(f"top{k}", [P, NT]) for k in range(2)]
        idx = [sb(f"idx{k}", [P, NT]) for k in range(2)]
        mask = [sb(f"mask{k}", FULL) for k in range(2)]
        eq, cand, l2 = sb("eq", FULL), sb("cand", FULL), sb("l2", FULL)
        gap, ex, den = sb("gap", [P, NT]), sb("ex", [P, NT]), sb("den", [P, NT])
        both, tot = sb("both", FULL), sb("tot", FULL)
        run = [sb(f"run{k}", FULL) for k in range(2)]
        cnt, padded, cum0, cum1, off = (sb("d_" + n, [P, NE]) for n in ("cnt", "padded", "cum0", "cum1", "off"))
        cnt_i = sb("cnt_i", [P, NE], I32)
        slot_f = sb("slot_f", [P, NT])
        past = sb("past", [1, SLOTT, NE])
        te = sb("te", [1, SLOTT])
        pre_p = ctx.enter_context(nc.psum_tensor("pre_p", [P, 512], F32))
        tot_p = ctx.enter_context(nc.psum_tensor("tot_p", [P, 512], F32))
        consts, step, gap_ok, ex_ok, both_ok, ranks = (sem("d_" + n) for n in ("consts", "step", "gap_ok", "ex_ok", "both_ok", "ranks"))

        def per_tile(ap):
            return ap.unsqueeze(2).broadcast_to(FULL)

        def per_expert(ap):
            return ap.unsqueeze(1).broadcast_to(FULL)

        w2_v = d["L0_ffn_moe_w2"].rearrange("e (m p) n -> p (e m) n", p=P)
        with nc.Block() as block:
            @block.sync
            def _(sp):
                for n in range(4):
                    part = slice(n * (NE * MD // P // 4), (n + 1) * (NE * MD // P // 4))
                    sp.dma_start(w2[:, part], w2_v[:, part]).then_inc(s_w2, 16)

            @block.gpsimd
            def _(pool):
                pool.iota(e_int[:], pattern=[[1, NE]], base=0, channel_multiplier=0).then_inc(consts, 1)
                pool.iota(j_int[:], pattern=[[P, SLOTT]], base=0, channel_multiplier=0).then_inc(consts, 1)
                pool.memset(ones[:], 1.0).then_inc(consts, 1)
                pool.wait_ge(consts, 3)
                pool.affine_select(out=before[:], in_=ones[:], compare_op=ALU.is_gt, fill=0.0, base=0,
                                   pattern=[[1, P]], channel_multiplier=-1).then_inc(consts, 1)

            @block.tensor
            def _(pe):
                pe.wait_ge(consts, 4)
                pe.wait_ge(both_ok, 1)
                rhs = both[:].rearrange("p n e -> p (n e)")
                pe.matmul(pre_p[:], before[:], rhs, start=True, stop=True)
                pe.matmul(tot_p[:], ones[:], rhs, start=True, stop=True).then_inc(ranks, 1)

            @block.scalar
            def _(act):
                act.wait_ge(gap_ok, 1)
                act.activation(ex[:], gap[:], ACT.Exp).then_inc(ex_ok, 1)

            @block.vector
            def _(dve):
                count = [0]

                def then(ins):
                    count[0] += 1
                    ins.then_inc(step, 1)
                    dve.wait_ge(step, count[0])

                dve.wait_ge(consts, 2)
                dve.tensor_copy(j_row[:], j_int[:])
                then(dve.tensor_copy(e_row[:], e_int[:]))
                then(dve.tensor_scalar(e8_row[:], e_row[:], float(NE), None, ALU.add))
                values = logits[:]
                for k in range(2):
                    then(dve.tensor_reduce(top[k][:], values, AX.X, ALU.max))
                    then(dve.tensor_tensor(eq[:], values, per_tile(top[k][:]), ALU.is_equal))
                    then(dve.scalar_tensor_tensor(cand[:], eq[:], -float(NE), per_expert(e8_row[:]), ALU.mult, ALU.add))
                    then(dve.tensor_reduce(idx[k][:], cand[:], AX.X, ALU.min))
                    then(dve.tensor_tensor(mask[k][:], per_expert(e_row[:]), per_tile(idx[k][:]), ALU.is_equal))
                    if k == 0:
                        then(dve.scalar_tensor_tensor(l2[:], mask[0][:], -3e38, logits[:], ALU.mult, ALU.add))
                        values = l2[:]
                dve.tensor_tensor(gap[:], top[1][:], top[0][:], ALU.subtract).then_inc(gap_ok, 1)
                dve.tensor_tensor(both[:], mask[0][:], mask[1][:], ALU.add).then_inc(both_ok, 1)
                dve.wait_ge(ex_ok, 1)
                then(dve.tensor_scalar(den[:], ex[:], 1.0, None, ALU.add))
                then(dve.reciprocal(gates[:, 0], den[:]))
                then(dve.tensor_tensor(gates[:, 1], ex[:], gates[:, 0], ALU.mult))
                dve.wait_ge(ranks, 1)
                then(dve.tensor_copy(tot[:].rearrange("p n e -> p (n e)"), tot_p[:]))
                src, k, s = tot, 0, 1
                while s < NT:
                    dst = run[k]
                    dve.tensor_copy(dst[:, 0:s], src[:, 0:s])
                    then(dve.tensor_tensor(dst[:, s:], src[:, s:], src[:, 0:NT - s], ALU.add))
                    src, k, s = dst, 1 - k, 2 * s
                incl = src
                then(dve.tensor_scalar(cnt[:], incl[:, NT - 1], float(P - 1), None, ALU.add))
                then(dve.tensor_copy(cnt_i[:], cnt[:]))
                then(dve.tensor_scalar(cnt_i[:], cnt_i[:], -P, None, ALU.bitwise_and))
                then(dve.tensor_copy(padded[:], cnt_i[:]))
                a, k, s = padded, 0, 1
                while s < NE:
                    c = (cum0, cum1)[k]
                    dve.tensor_copy(c[:, 0:s], a[:, 0:s])
                    then(dve.tensor_tensor(c[:, s:], a[:, s:], a[:, 0:NE - s], ALU.add))
                    a, k, s = c, 1 - k, 2 * s
                then(dve.tensor_tensor(off[:], a[:], padded[:], ALU.subtract))
                base = run[0] if incl is run[1] else run[1]
                then(dve.tensor_tensor(base[:], incl[:], tot[:], ALU.subtract))
                then(dve.tensor_tensor(base[:], base[:], per_expert(off[:]), ALU.add))
                then(dve.tensor_tensor(base[:].rearrange("p n e -> p (n e)"), pre_p[:], base[:].rearrange("p n e -> p (n e)"), ALU.add))
                for k in range(2):
                    then(dve.tensor_tensor(eq[:], mask[k][:], base[:], ALU.mult))
                    then(dve.tensor_reduce(slot_f[:], eq[:], AX.X, ALU.add))
                    then(dve.tensor_copy(slots[:, k], slot_f[:]))
                wide = [1, SLOTT, NE]
                then(dve.tensor_tensor(past[:], j_row[:].unsqueeze(2).broadcast_to(wide), a[0:1].unsqueeze(1).broadcast_to(wide), ALU.is_ge))
                then(dve.tensor_reduce(te[:], past[:], AX.X, ALU.add))
                then(dve.tensor_scalar(te[:], te[:], float(NE - 1), None, ALU.min))
                then(dve.tensor_copy(tile_expert[:], te[:]))


def scatter(nc, x2_d, slots, xs_d, s_xs0):
    ctx = ExitStack()
    with ctx:
        row = ctx.enter_context(nc.sbuf_tensor("sx_row", [P, 2, C], F32))
        at = ctx.enter_context(nc.sbuf_tensor("sx_at", [P, 2, 2, 1], U32))
        sem = nc.alloc_semaphore
        at_ok, passed = sem("x_at_ok"), sem("x_passed")
        row_ld = [sem(f"x_row_ld{s}") for s in range(2)]
        sent = [sem(f"x_sent{s}") for s in range(2)]
        with nc.Block() as block:
            @block.sync
            def _(sp):
                with sp.Fori(0, NT // 2) as i:
                    for s in range(2):
                        sp.wait_ge(sent[s], i * 32)
                        sp.dma_start(row[:, s], x2_d[bass.ds((i * 2 + s) * P, P)]).then_inc(row_ld[s], 16)

            @block.gpsimd
            def _(pool):
                pool.wait_ge(s_xs0, 16 * (T // TB // 2 + 1))
                with pool.Fori(0, NT // 2) as i:
                    for s in range(2):
                        pool.wait_ge(sent[s], i * 32)
                        for k in range(2):
                            pool.tensor_copy(at[:, s, k], slots[:, k, bass.ds(i * 2 + s, 1)]).then_inc(at_ok, 1)
                        pool.wait_ge(at_ok, (i * 2 + s + 1) * 2)
                        pool.wait_ge(row_ld[s], (i + 1) * 16)
                        pool.sem_inc(passed, 1)
                        for k in range(2):
                            pool.indirect_dma_start(xs_d, bass.IndirectOffsetOnAxis(at[:, s, k], 0), row[:, s], None).then_inc(sent[s], 16)
                for s in range(2):
                    pool.wait_ge(sent[s], NT // 2 * 32)


def experts(nc, ident, w13, w2, s_w13, s_w2, tile_expert, xs_d, ys_d):
    ctx = ExitStack()
    with ctx:
        def sb(name, shape, dt=F32):
            return ctx.enter_context(nc.sbuf_tensor(name, shape, dt))

        def ps(name, shape):
            return ctx.enter_context(nc.psum_tensor(name, shape, F32))

        def sem(name):
            return nc.alloc_semaphore(name)

        MC = MD // P
        x = sb("e_x", [P, 2, C])
        x_t = sb("e_x_t", [P, 2, CC, P])
        h = sb("e_h", [P, 2, MD])
        h_t = sb("e_h_t", [P, 2, MC, P])
        y = sb("e_y", [P, 2, C])
        xt_p = ps("e_xt_p", [P, 512])
        ht_p = ps("e_ht_p", [P, MC, P])
        gate_p = [ps(f"e_gate_p{i}", [P, MD]) for i in range(2)]
        up_p = [ps(f"e_up_p{i}", [P, MD]) for i in range(2)]
        y_p = [ps(f"e_y_p{i}", [P, 512]) for i in range(2)]
        ld = [sem(f"e_ld{i}") for i in range(2)]
        stored = [sem(f"e_stored{i}") for i in range(2)]
        xt, xt_ok, gu, silu_ok, h_ok, ht, ht_ok, y_m, y_ok = (
            sem("e_" + n) for n in "xt xt_ok gu silu_ok h_ok ht ht_ok y_m y_ok".split())
        with nc.Block() as block:
            @block.sync
            def _(sp):
                with sp.Fori(0, SLOTT // 2) as i:
                    for s in range(2):
                        sp.wait_ge(xt, i * 2)
                        sp.dma_start(x[:, s], xs_d[bass.ds((i * 2 + s) * P, P)]).then_inc(ld[s], 16)

            @block.tensor
            def _(pe):
                pe.wait_ge(s_w13, 16 * NE * CC)
                pe.wait_ge(s_w2, 16 * 4)
                with pe.Fori(0, SLOTT // 2) as i:
                    j = [i * 2 + s for s in range(2)]
                    e = [pe.value_load(tile_expert[0:1, bass.ds(j[s], 1)], min_val=0, max_val=NE - 1) for s in range(2)]
                    for s in range(2):
                        pe.wait_ge(ld[s], (i + 1) * 16)
                        pe.wait_ge(xt_ok, j[s])
                        for c in range(CC):
                            last = pe.transpose(xt_p[:, c * P:(c + 1) * P], x[:, s, c * P:(c + 1) * P], ident[:])
                        last.then_inc(xt, 1)
                    for s in range(2):
                        pe.wait_ge(xt_ok, j[s] + 1)
                        pe.wait_ge(h_ok, i * 2)
                        for half, bank in enumerate((gate_p[s], up_p[s])):
                            for c in range(CC):
                                last = pe.matmul(bank[:], x_t[:, s, c], w13[:, bass.ds(e[s] * (CC * 2 * MD) + (c * 2 + half) * MD, MD)],
                                                 start=c == 0, stop=c == CC - 1)
                        last.then_inc(gu, 1)
                    for s in range(2):
                        pe.wait_ge(h_ok, j[s] + 1)
                        pe.wait_ge(ht_ok, j[s])
                        for m in range(MC):
                            last = pe.transpose(ht_p[:, m], h[:, s, m * P:(m + 1) * P], ident[:])
                        last.then_inc(ht, 1)
                        pe.wait_ge(ht_ok, j[s] + 1)
                        pe.wait_ge(y_ok, i * 2)
                        for m in range(MC):
                            last = pe.matmul(y_p[s][:, 0:C], h_t[:, s, m], w2[:, bass.ds(e[s] * MC + m, 1)].rearrange("p o n -> p (o n)"),
                                             start=m == 0, stop=m == MC - 1)
                        last.then_inc(y_m, 1)

            @block.scalar
            def _(act):
                for s in range(2):
                    act.sem_inc(stored[s], 16)
                with act.Fori(0, SLOTT // 2) as i:
                    for s in range(2):
                        act.wait_ge(gu, i * 2 + s + 1)
                        act.activation(h[:, s], gate_p[s][:], ACT.Silu).then_inc(silu_ok, 1)
                    for s in range(2):
                        act.wait_ge(y_m, i * 2 + s + 1)
                        act.wait_ge(stored[s], (i + 1) * 16)
                        act.copy(y[:, s], y_p[s][:, 0:C]).then_inc(y_ok, 1)
                        act.wait_ge(y_ok, i * 2 + s + 1)
                        act.dma_start(ys_d[bass.ds((i * 2 + s) * P, P)], y[:, s]).then_inc(stored[s], 16)
                for s in range(2):
                    act.wait_ge(stored[s], 16 * (SLOTT // 2 + 1))

            @block.vector
            def _(dve):
                with dve.Fori(0, SLOTT // 2) as i:
                    for s in range(2):
                        dve.wait_ge(xt, i * 2 + s + 1)
                        dve.tensor_copy(x_t[:, s].rearrange("p c n -> p (c n)"), xt_p[:, 0:C]).then_inc(xt_ok, 1)
                    for s in range(2):
                        dve.wait_ge(silu_ok, i * 2 + s + 1)
                        dve.tensor_tensor(h[:, s], up_p[s][:], h[:, s], ALU.mult).then_inc(h_ok, 1)
                    for s in range(2):
                        dve.wait_ge(ht, i * 2 + s + 1)
                        dve.tensor_copy(h_t[:, s], ht_p[:]).then_inc(ht_ok, 1)


def combine(nc, x2_d, slots, gates, ys_d, out):
    ctx = ExitStack()
    with ctx:
        def sb(name, shape, dt=F32):
            return ctx.enter_context(nc.sbuf_tensor(name, shape, dt))

        def sem(name):
            return nc.alloc_semaphore(name)

        at = sb("f_at", [P, 2, 2, 1], U32)
        ya = [[sb(f"f_y{s}{k}", [P, C]) for k in range(2)] for s in range(2)]
        x2 = sb("f_x2", [P, 2, C])
        acc = sb("f_acc", [P, 2, C])
        bn6 = sb("f_bn6", [P, 2, 6])
        mv = sb("f_mv", [P, 2, 2])
        rstd = sb("f_rstd", [P, 2, 1])
        std = sb("f_std", [P, 2, 1])
        eps = sb("f_eps", [P, 1])
        res = sb("f_res", [P, 2, C])
        got = [sem(f"f_got{i}") for i in range(2)]
        ld = [sem(f"f_ld{i}") for i in range(2)]
        stored = [sem(f"f_stored{i}") for i in range(2)]
        passed, at_go = sem("f_passed"), sem("f_at_go")
        at_ok, acc0, acc1, bn_ok, mv_ok, std_ok, rstd_ok, res_ok, eps_ok = (
            sem("f_" + n) for n in "at_ok acc0 acc1 bn_ok mv_ok std_ok rstd_ok res_ok eps_ok".split())
        out_v = out.rearrange("b t c -> (b t) c")
        with nc.Block() as block:
            @block.gpsimd
            def _(pool):
                with pool.Fori(0, NT // 2) as i:
                    for s in range(2):
                        pool.wait_ge(got[s], i * 32)
                        for k in range(2):
                            pool.tensor_copy(at[:, s, k], slots[:, k, bass.ds(i * 2 + s, 1)]).then_inc(at_ok, 1)
                        pool.wait_ge(at_ok, (i * 2 + s + 1) * 2)
                        pool.wait_ge(acc1, i * 2)
                        pool.sem_inc(at_go, 1)
                        for k in range(2):
                            pool.indirect_dma_start(ya[s][k][:], None, ys_d, bass.IndirectOffsetOnAxis(at[:, s, k], 0)).then_inc(got[s], 16)

            @block.vector
            def _(dve):
                dve.memset(eps[:], EPS).then_inc(eps_ok, 1)
                with dve.Fori(0, NT // 2) as i:
                    n = [dve.snap(i * 2 + s + 1) for s in range(2)]

                    def gate(k, s):
                        return gates[:, k, bass.ds(i * 2 + s, 1)]

                    dve.wait_ge(res_ok, i * 2)
                    for s in range(2):
                        dve.wait_ge(got[s], (i + 1) * 32)
                        dve.wait_ge(ld[s], (i + 1) * 16)
                        dve.scalar_tensor_tensor(acc[:, s], ya[s][0][:], gate(0, s), x2[:, s], ALU.mult, ALU.add).then_inc(acc0, 1)
                    for s in range(2):
                        dve.wait_ge(acc0, n[s])
                        dve.scalar_tensor_tensor(acc[:, s], ya[s][1][:], gate(1, s), acc[:, s], ALU.mult, ALU.add).then_inc(acc1, 1)
                    for s in range(2):
                        dve.wait_ge(acc1, n[s])
                        dve.bn_stats(bn6[:, s], acc[:, s]).then_inc(bn_ok, 1)
                    for s in range(2):
                        dve.wait_ge(bn_ok, n[s])
                        dve.sem_inc(passed, 1)
                        dve.bn_aggr(mv[:, s], bn6[:, s]).then_inc(mv_ok, 1)
                    for s in range(2):
                        dve.wait_ge(std_ok, n[s])
                        dve.reciprocal(rstd[:, s], std[:, s]).then_inc(rstd_ok, 1)
                    for s in range(2):
                        dve.wait_ge(rstd_ok, n[s])
                        dve.wait_ge(stored[s], i * 16)
                        dve.tensor_scalar(res[:, s], acc[:, s], mv[:, s, 0:1], rstd[:, s], ALU.subtract, ALU.mult).then_inc(res_ok, 1)

            @block.scalar
            def _(act):
                act.wait_ge(eps_ok, 1)
                with act.Fori(0, NT // 2) as i:
                    for s in range(2):
                        act.wait_ge(acc0, i * 2)
                        act.dma_start(x2[:, s], x2_d[bass.ds((i * 2 + s) * P, P)]).then_inc(ld[s], 16)
                    for s in range(2):
                        act.wait_ge(mv_ok, i * 2 + s + 1)
                        act.activation(std[:, s], mv[:, s, 1:2], ACT.Sqrt, bias=eps[:]).then_inc(std_ok, 1)

            @block.sync
            def _(sp):
                with sp.Fori(0, NT // 2) as i:
                    for s in range(2):
                        sp.wait_ge(res_ok, i * 2 + s + 1)
                        sp.dma_start(out_v[bass.ds((i * 2 + s) * P, P)], res[:, s]).then_inc(stored[s], 16)
                for s in range(2):
                    sp.wait_ge(stored[s], NT // 2 * 16)


_INS = ["x", "ctx_512"] + ["L0_attn_" + n for n in (
    "x_r x_w x_k x_v x_a x_g k_k k_a r_k W_r W_k W_v W_o w_lora_a w_lora_b w_lora_bias a_lora_a a_lora_b "
    "a_lora_bias g_lora_a g_lora_b g_lora_bias gn_weight gn_bias").split()] + [
    "L0_xattn_" + n for n in "Wq bq Wk bk Wv bv Wo bo".split()] + [
    "L0_ffn_" + n for n in "moe_router moe_w13 moe_w2".split()]
_UNUSED = {"L0_attn_x_g"}


def kernel(**inputs):
    import numpy as _np
    import concourse.bacc as _bacc
    from concourse import mybir as _mybir
    from concourse.bass_utils import run_bass_kernel_spmd as _run

    nc = _bacc.Bacc("TRN2", target_bir_lowering=False, num_devices=1)
    arrays, aps = {}, {}
    for name in _INS:
        if name in _UNUSED:
            continue
        a = _np.ascontiguousarray(inputs[name])
        arrays[f"in_{name}_dram"] = a
        aps[name] = nc.dram_tensor(f"in_{name}_dram", a.shape, _mybir.dt.from_np(a.dtype), kind="ExternalInput").ap()
    out = nc.dram_tensor("out_0_dram", (B, T, C), F32, kind="ExternalOutput").ap()
    decoder_kernel(nc, aps, out)
    r = _run(nc, [arrays], core_ids=[0])
    return r.results[0]["out_0_dram"]
```

```python
from contextlib import ExitStack

import concourse.bass as bass
from concourse import mybir

F32 = mybir.dt.float32
U32 = mybir.dt.uint32
I32 = mybir.dt.int32
ALU = mybir.AluOpType
ACT = mybir.ActivationFunctionType
AX = mybir.AxisListType

P = 128
B, T, C, H, D = 32, 256, 256, 16, 16
CC = C // P
TT = T // P
NT = B * TT
Q = P // B
HQ = H // Q
G = HQ * D
NC6 = 6
R_, W_, K_, V_, A_, B_ = range(NC6)
RL = 64
RG = 128
LKV, CD = 120, 128
NE, MD = 8, 512
SLOTT = 2 * B * T // P + NE
TB = 8
EPS = 1e-5
EXP_HALF = 0.6065306597126334


def decoder_kernel(nc, d, out):
    ctx = ExitStack()
    with ctx:
        def dram(name, shape):
            return nc.dram_tensor(name, shape, F32, kind="Internal").ap()

        coef_d = dram("coef_d", (B, Q, T, NC6 * G))
        bg_d = dram("bg_d", (B * T, 2 * C))
        o_d = dram("o_d", (B, Q, T, G))
        xs_d = dram("xs_d", (SLOTT * P, C))
        ys_d = dram("ys_d", (SLOTT * P, C))
        x2_d = dram("x2_d", (B * T, C))

        def sb(name, shape, dt=F32):
            return ctx.enter_context(nc.sbuf_tensor(name, shape, dt))

        ident = sb("ident", [P, P])
        w13 = sb("w13", [P, NE * CC * 2 * MD])
        s_const = nc.alloc_semaphore("s_const")
        s_w13 = nc.alloc_semaphore("s_w13")
        s_xs0 = nc.alloc_semaphore("s_xs0")
        zero = sb("zero", [P, C])

        constants(nc, ident, zero, s_const)
        mark = nc.snapshot_sems()
        project(nc, d, ident, coef_d, bg_d)
        reuse_semaphores(nc, mark)
        scan(nc, d, ident, zero, coef_d, o_d, w13, xs_d, s_w13, s_xs0)
        logits = sb("logits", [P, NT, NE])
        mark = nc.snapshot_sems()
        attend(nc, d, ident, o_d, bg_d, x2_d, logits)
        reuse_semaphores(nc, mark)
        w2 = sb("w2", [P, NE * (MD // P), C])
        s_w2 = nc.alloc_semaphore("s_w2")
        slots = sb("slots", [P, 2, NT], U32)
        gates = sb("gates", [P, 2, NT])
        pair_experts = sb("pair_experts", [1, SLOTT // 2], I32)
        dispatch(nc, d, logits, slots, gates, pair_experts, w2, s_w2)
        scatter(nc, x2_d, slots, xs_d, s_xs0)
        experts(nc, ident, w13, w2, s_w13, s_w2, pair_experts, xs_d, ys_d)
        combine(nc, x2_d, slots, gates, ys_d, out)


def reuse_semaphores(nc, mark):
    nc.clear_and_free_semaphores(nc.allocated_since(mark))
    nc.all_engine_barrier()


def constants(nc, ident, zero, s_const):
    with nc.Block() as block:
        @block.gpsimd
        def _(pool):
            pool.memset(zero[:], 0.0).then_inc(s_const, 1)
            pool.memset(ident[:], 0.0).then_inc(s_const, 1)
            pool.wait_ge(s_const, 2)
            pool.affine_select(out=ident[:], in_=ident[:], compare_op=ALU.not_equal, fill=1.0, base=0,
                               pattern=[[-1, P]], channel_multiplier=1).then_inc(s_const, 1)


def project(nc, d, ident, coef_d, bg_d):
    ctx = ExitStack()
    with ctx:
        def sb(name, shape, dt=F32):
            return ctx.enter_context(nc.sbuf_tensor(name, shape, dt))

        def ps(name, shape):
            return ctx.enter_context(nc.psum_tensor(name, shape, F32))

        def sem(name):
            return nc.alloc_semaphore(name)

        MIX = ("r", "k", "v", "w", "a")
        w_rkv = sb("w_rkv", [P, 3, CC, C])
        w_lora = sb("w_lora", [P, 2, CC, 2 * RL])
        lora_raw = sb("lora_raw", [P, CC, 2 * RL])
        mix_w = sb("mix_w", [P, len(MIX), CC])
        omx = sb("omx", [P, len(MIX), CC])
        wa_b = sb("wa_b", [P, 2 * C])
        wr_t = sb("wr_t", [P, CC, C])
        ga = sb("ga", [P, CC, RG])
        w_rg = sb("w_rg", [P, CC, RG])
        g_b = sb("g_b", [P, C])
        bias_wa = sb("bias_wa", [P, 2, C])
        bias_g = sb("bias_g", [P, C])
        kk_row = sb("kk_row", [P, C])
        ka_row = sb("ka_row", [P, C])
        oma_row = sb("oma_row", [P, C])
        rk_row = sb("rk_row", [P, C])

        x_in = sb("x_in", [P, 2, TT, C])
        x_t = sb("x_t", [P, 2, CC, 1 + T])
        delta = sb("delta", [P, CC, T])
        mixed = sb("mixed", [P, 2, 3, CC, T])
        th = sb("th", [P, 2, T])
        sg = sb("sg", [P, 2, T])
        za = sb("za", [P, TT, 2 * C])
        wa = sb("wa", [P, TT, 2 * C])
        kk0 = sb("kk0", [P, TT, C])
        sq = sb("sq", [P, TT, C])
        ss = sb("ss", [P, TT, H])
        inv = sb("inv", [P, TT, H])
        nt = sb("nt", [P, TT, H])
        kk = sb("kk", [P, TT, C])
        u = sb("u", [P, TT, C])
        rr = sb("rr", [P, TT, C])
        bs = sb("bs", [P, TT, H])
        coef = sb("coef", [P, 2, TT, Q, NC6, G])
        bg = sb("bg", [P, 2, TT, 2, C])

        xt_p = ps("xt_p", [P, CC, T])
        l_p = ps("l_p", [P, 2, T])
        rv_p = [ps(f"rv_p{i}", [P, 2, C]) for i in range(TT)]
        kg_p = [ps(f"kg_p{i}", [P, 2, C]) for i in range(TT)]
        wa_p = [ps(f"wa_p{i}", [P, 2 * C]) for i in range(TT)]

        wld, wload = sem("p_wld"), sem("p_wload")
        zeroed, omx_ok, prep, wrt, wrt_ok, wrg, wrg_ok = (
            sem(n) for n in ("p_zeroed", "p_omx", "p_prep", "p_wrt", "p_wrt_ok", "p_wrg", "p_wrg_ok"))
        x_ld = [sem(f"p_x_ld{i}") for i in range(2)]
        stored = [sem(f"p_stored{i}") for i in range(2)]
        (xt, xt_ok, dlt, mix_ok, lora, th_ok, rv, g_m, wa_m, za_ok, kk0_ok, sq_ok, ss_ok, kk_ok,
         k_ok, g_ok, bs_ok, rv_ok, wa_ok, w_ok, k_cp, neg_ok, u0_ok, u_ok, rr0_ok, rr_ok, b_ok, bonus_ok) = (
            sem("p_" + n) for n in (
                "xt", "xt_ok", "dlt", "mix_ok", "lora", "th_ok", "rv", "g_m", "wa_m", "za_ok", "kk0_ok",
                "sq_ok", "ss_ok", "kk_ok", "k_ok", "g_ok", "bs_ok", "rv_ok", "wa_ok", "w_ok", "k_cp", "neg_ok",
                "u0_ok", "u_ok", "rr0_ok", "rr_ok", "b_ok", "bonus_ok"))
        newton, NEWTON = sem("p_newton"), 12

        def vec(name):
            v = d["L0_attn_" + name]
            return v if len(v.shape) == 1 else v.rearrange("h d -> (h d)")

        def heads(ap):
            return ap.rearrange("p (h e) -> p h e", h=H)

        def over(ap):
            return ap.unsqueeze(2).broadcast_to([P, H, D])

        def hq(ap):
            return ap.rearrange("p (q g) -> p q g", q=Q)

        def wait(eng, sem_, value):
            if not (isinstance(value, int) and value <= 0):
                eng.wait_ge(sem_, value)

        def batches(eng, body):
            for b in range(2):
                body(b, b, 0, True)
            with eng.Fori(1, B // 2 - 1) as i:
                for s in range(2):
                    body(eng.snap(i * 2 + s), s, i, True)
            for b in range(B - 2, B):
                body(b, b % 2, b // 2, b < B - 1)

        with nc.Block() as block:
            @block.tensor
            def _(pe):
                pe.wait_ge(wload, 1)
                for m in range(CC):
                    for c in range(CC):
                        last = pe.transpose(xt_p[:, m, c * P:(c + 1) * P], w_rkv[:, 0, c, m * P:(m + 1) * P], ident[:])
                last.then_inc(wrt, 1)
                pe.wait_ge(wrt_ok, 1)
                for c in range(CC):
                    for m in range(CC):
                        last = pe.matmul(l_p[:, 0, c * RG:(c + 1) * RG], wr_t[:, m, c * P:(c + 1) * P], ga[:, m],
                                         start=m == 0, stop=m == CC - 1)
                last.then_inc(wrg, 1)
                pe.wait_ge(wrg_ok, 1)
                pe.wait_ge(prep, 1)

                def turn_x(b, s, k):
                    pe.wait_ge(x_ld[s], (k + 1) * 16)
                    wait(pe, xt_ok, b)
                    for t in range(TT):
                        for c in range(CC):
                            last = pe.transpose(xt_p[:, c, t * P:(t + 1) * P], x_in[:, s, t, c * P:(c + 1) * P], ident[:])
                    last.then_inc(xt, 1)

                def loras(b, s):
                    pe.wait_ge(xt_ok, b + 1)
                    wait(pe, th_ok, b * 2)
                    for sh in range(2):
                        for c in range(CC):
                            pe.matmul(l_p[:, 0], w_lora[:, sh, c], x_t[:, s, c, 1 - sh:1 - sh + T],
                                      start=sh == 0 and c == 0, stop=sh == 1 and c == CC - 1)
                    pe.wait_ge(mix_ok, b + 1)
                    for c in range(CC):
                        last = pe.matmul(l_p[:, 1], w_rg[:, c], mixed[:, s, 0, c], start=c == 0, stop=c == CC - 1)
                    last.then_inc(lora, 1)

                def products(b, s, i, more):
                    if more:
                        turn_x(b + 1, 1 - s, i + s)
                    pe.wait_ge(th_ok, b * 2 + 2)
                    for t in range(TT):
                        tok = slice(t * P, (t + 1) * P)
                        before = b * TT + t + 1 - TT
                        wait(pe, k_cp, before)
                        for c in range(CC):
                            pe.matmul(kg_p[t][:, 0], mixed[:, s, 1, c, tok], w_rkv[:, 1, c], start=c == 0, stop=c == CC - 1)
                        pe.matmul(kg_p[t][:, 1], sg[:, s, tok], g_b[:], start=True, stop=True).then_inc(g_m, 1)
                        wait(pe, za_ok, before)
                        pe.matmul(wa_p[t][:], th[:, s, tok], wa_b[:], start=True, stop=True).then_inc(wa_m, 1)
                        wait(pe, rv_ok, before)
                        for n, half in ((0, 0), (2, 1)):
                            for c in range(CC):
                                last = pe.matmul(rv_p[t][:, half], mixed[:, s, n, c, tok], w_rkv[:, n, c],
                                                 start=c == 0, stop=c == CC - 1)
                        last.then_inc(rv, 1)
                    if more:
                        loras(b + 1, 1 - s)

                turn_x(0, 0, 0)
                loras(0, 0)
                batches(pe, products)

            @block.scalar
            def _(act):
                act.wait_ge(wrt, 1)
                act.copy(wr_t[:], xt_p[:]).then_inc(wrt_ok, 1)
                act.wait_ge(wrg, 1)
                act.copy(w_rg[:].rearrange("p c n -> p (c n)"), l_p[:, 0]).then_inc(wrg_ok, 1)
                act.wait_ge(zeroed, 2)

                def leave_x(b, s):
                    act.wait_ge(xt, b + 1)
                    wait(act, lora, b - 1)
                    wait(act, mix_ok, b - 1)
                    act.copy(x_t[:, s, :, 1:1 + T], xt_p[:]).then_inc(xt_ok, 1)

                def leave_loras(b, s):
                    act.wait_ge(lora, b + 1)
                    wait(act, wa_m, (b - 1) * TT)
                    act.activation(th[0:RL, s], l_p[0:RL, 0], ACT.Tanh)
                    act.copy(th[RL:P, s], l_p[RL:P, 0]).then_inc(th_ok, 1)
                    act.activation(sg[:, s], l_p[:, 1], ACT.Sigmoid).then_inc(th_ok, 1)

                def rows(b, s, i, more):
                    if more:
                        leave_x(b + 1, 1 - s)
                    n = [b * TT + t + 1 for t in range(TT)]
                    act.wait_ge(stored[s], (i + 1) * 64)
                    for t in range(TT):
                        act.wait_ge(kk0_ok, n[t])
                        wait(act, ss_ok, n[t] - TT)
                        act.activation(sq[:, t], kk0[:, t], ACT.Square).then_inc(sq_ok, 1)
                        act.wait_ge(g_ok, n[t])
                        act.copy(coef[:, s, t, :, K_], hq(kg_p[t][:, 0])).then_inc(k_cp, 1)
                        act.wait_ge(za_ok, n[t])
                        wait(act, b_ok, n[t] - TT)
                        wait(act, u_ok, n[t] - TT)
                        wait(act, w_ok, n[t] - TT)
                        act.activation(wa[:, t], za[:, t], ACT.Sigmoid).then_inc(wa_ok, 1)
                        act.wait_ge(rv, n[t])
                        act.copy(coef[:, s, t, :, R_], hq(rv_p[t][:, 0]))
                        act.copy(coef[:, s, t, :, V_], hq(rv_p[t][:, 1])).then_inc(rv_ok, 1)
                    if more:
                        leave_loras(b + 1, 1 - s)
                    for t in range(TT):
                        act.wait_ge(wa_ok, n[t])
                        act.mul(coef[:, s, t, :, W_], hq(wa[:, t, 0:C]), EXP_HALF).then_inc(w_ok, 1)
                    for t in range(TT):
                        act.wait_ge(kk_ok, n[t])
                        act.mul(coef[:, s, t, :, A_], hq(kk[:, t]), -1.0).then_inc(neg_ok, 1)

                leave_x(0, 0)
                leave_loras(0, 0)
                batches(act, rows)

            @block.sync
            def _(sp):
                for n, name in enumerate(("W_r", "W_k", "W_v")):
                    sp.dma_start(w_rkv[:, n], d["L0_attn_" + name].rearrange("(c p) n -> p c n", p=P)).then_inc(wld, 16)
                sp.dma_start(lora_raw[:, :, 0:RL], d["L0_attn_w_lora_a"].rearrange("(c p) n -> p c n", p=P)).then_inc(wld, 16)
                sp.dma_start(lora_raw[:, :, RL:], d["L0_attn_a_lora_a"].rearrange("(c p) n -> p c n", p=P)).then_inc(wld, 16)
                sp.dma_start(ga[:], d["L0_attn_g_lora_a"].rearrange("(c p) n -> p c n", p=P)).then_inc(wld, 16)
                sp.dma_start(g_b[:], d["L0_attn_g_lora_b"]).then_inc(wld, 16)
                for n, m in enumerate(MIX):
                    sp.dma_start(mix_w[:, n], vec("x_" + m).rearrange("(c p) -> p c", p=P), allow_slow_non_contiguous=True).then_inc(wld, 16)
                for t, name in ((bias_wa[:, 0], "w_lora_bias"), (bias_wa[:, 1], "a_lora_bias"), (bias_g[:], "g_lora_bias"),
                                (kk_row[:], "k_k"), (ka_row[:], "k_a"), (rk_row[:], "r_k")):
                    sp.dma_start(t, vec(name).unsqueeze(0).broadcast_to([P, C])).then_inc(wld, 16)
                sp.wait_ge(zeroed, 1)
                sp.dma_start(wa_b[0:RL, 0:C], d["L0_attn_w_lora_b"]).then_inc(wld, 16)
                sp.dma_start(wa_b[RL:2 * RL, C:], d["L0_attn_a_lora_b"]).then_inc(wld, 16)
                sp.wait_ge(wld, 16 * 20)
                sp.sem_inc(wload, 1)

                def load_x(b, s):
                    wait(sp, xt, b - 1)
                    sp.dma_start(x_in[:, s], d["x"][bass.ds(b, 1)].rearrange("o (t p) c -> p (o t) c", p=P)).then_inc(x_ld[s], 16)

                def store_bg(b, s):
                    for t in range(TT):
                        n1 = b * TT + t + 1
                        sp.wait_ge(g_ok, n1)
                        sp.wait_ge(bonus_ok, n1)
                        sp.dma_start(bg_d[bass.ds((b * TT + t) * P, P)], bg[:, s, t].rearrange("p k c -> p (k c)")).then_inc(stored[s], 16)

                def store(b, s, i, more):
                    if not (isinstance(b, int) and b + 2 >= B):
                        load_x(b + 2, s)
                    if not (isinstance(b, int) and b == 0):
                        store_bg(b - 1, 1 - s)
                    for t in range(TT):
                        n1 = b * TT + t + 1
                        sp.wait_ge(neg_ok, n1)
                        sp.wait_ge(k_ok, n1)
                        sp.wait_ge(b_ok, n1)
                        sp.dma_start(coef_d[bass.ds(b, 1), :, t * P:(t + 1) * P].rearrange("o q t f -> t (o q) f"),
                                     coef[:, s, t].rearrange("p q n g -> p q (n g)")).then_inc(stored[s], 16)

                load_x(0, 0)
                load_x(1, 1)
                batches(sp, store)
                store_bg(B - 1, (B - 1) % 2)
                for s in range(2):
                    sp.wait_ge(stored[s], 64 * (B // 2 + 1))

            @block.vector
            def _(dve):
                dve.memset(wa_b[:], 0.0).then_inc(zeroed, 1)
                dve.memset(x_t[:, :, :, 0:1], 0.0).then_inc(zeroed, 1)
                for s in range(2):
                    dve.sem_inc(stored[s], 64)
                dve.wait_ge(wload, 1)
                dve.tensor_scalar(omx[:], mix_w[:], -1.0, 1.0, ALU.mult, ALU.add).then_inc(omx_ok, 1)
                dve.tensor_scalar(oma_row[:], ka_row[:], -1.0, 1.0, ALU.mult, ALU.add)
                dve.wait_ge(omx_ok, 1)
                for c in range(CC):
                    for n, col in ((3, slice(0, RL)), (4, slice(RL, 2 * RL))):
                        dve.tensor_scalar(w_lora[:, 0, c, col], lora_raw[:, c, col], omx[:, n, c:c + 1], None, ALU.mult)
                        last = dve.tensor_scalar(w_lora[:, 1, c, col], lora_raw[:, c, col], mix_w[:, n, c:c + 1], None, ALU.mult)
                last.then_inc(prep, 1)

                def mix(b, s):
                    dve.wait_ge(xt_ok, b + 1)
                    wait(dve, mix_ok, b)
                    dve.tensor_tensor(delta[:], x_t[:, s, :, 0:T], x_t[:, s, :, 1:1 + T], ALU.subtract).then_inc(dlt, 1)
                    dve.wait_ge(dlt, b + 1)
                    wait(dve, rv, (b - 1) * TT)
                    for n in range(3):
                        for c in range(CC):
                            last = dve.scalar_tensor_tensor(mixed[:, s, n, c], delta[:, c], mix_w[:, n, c:c + 1],
                                                            x_t[:, s, c, 1:1 + T], ALU.mult, ALU.add)
                    last.then_inc(mix_ok, 1)

                def bonus(b):
                    wait(dve, bonus_ok, b * TT)
                    for t in range(TT):
                        dve.wait_ge(rr_ok, b * TT + t + 1)
                        dve.tensor_reduce(bs[:, t], heads(rr[:, t]), AX.X, ALU.add).then_inc(bs_ok, 1)

                def rows(b, s, i, more):
                    if more:
                        mix(b + 1, 1 - s)
                    if not (isinstance(b, int) and b == 0):
                        bonus(b - 1)
                    b1 = b + 1
                    n = [b * TT + t + 1 for t in range(TT)]
                    dve.wait_ge(stored[s], (i + 1) * 64)
                    for t in range(TT):
                        dve.wait_ge(g_m, n[t])
                        wait(dve, kk_ok, n[t] - TT)
                        dve.tensor_tensor(kk0[:, t], kg_p[t][:, 0], kk_row[:], ALU.mult).then_inc(kk0_ok, 1)
                        dve.tensor_tensor(bg[:, s, t, 1], kg_p[t][:, 1], bias_g[:], ALU.add).then_inc(g_ok, 1)
                        dve.wait_ge(wa_m, n[t])
                        wait(dve, wa_ok, n[t] - TT)
                        dve.tensor_tensor(za[:, t], wa_p[t][:], bias_wa[:].rearrange("p k c -> p (k c)"), ALU.add).then_inc(za_ok, 1)
                    wait(dve, newton, b * NEWTON)
                    for t in range(TT):
                        dve.wait_ge(sq_ok, n[t])
                        dve.tensor_reduce(ss[:, t], heads(sq[:, t]), AX.X, ALU.add).then_inc(ss_ok, 1)
                    dve.wait_ge(ss_ok, b * TT + TT)
                    dve.tensor_scalar(ss[:], ss[:], 1e-24, None, ALU.max).then_inc(newton, 1)
                    dve.wait_ge(newton, b * NEWTON + 1)
                    dve.tensor_scalar(inv[:].bitcast(I32), ss[:].bitcast(I32), 1, None, ALU.arith_shift_right).then_inc(newton, 1)
                    dve.wait_ge(newton, b * NEWTON + 2)
                    dve.tensor_scalar(inv[:].bitcast(I32), inv[:].bitcast(I32), -1.0, float(0x5f3759df), ALU.mult, ALU.add).then_inc(newton, 1)
                    for k in range(3):
                        dve.wait_ge(newton, b * NEWTON + 3 * k + 3)
                        dve.tensor_tensor(nt[:], inv[:], inv[:], ALU.mult).then_inc(newton, 1)
                        dve.wait_ge(newton, b * NEWTON + 3 * k + 4)
                        dve.scalar_tensor_tensor(nt[:], nt[:], -0.5, ss[:], ALU.mult, ALU.mult).then_inc(newton, 1)
                        dve.wait_ge(newton, b * NEWTON + 3 * k + 5)
                        dve.scalar_tensor_tensor(inv[:], nt[:], 1.5, inv[:], ALU.add, ALU.mult).then_inc(newton, 1)
                    dve.wait_ge(newton, b1 * NEWTON)
                    wait(dve, b_ok, b * TT)
                    wait(dve, neg_ok, b * TT)
                    for t in range(TT):
                        dve.tensor_tensor(heads(kk[:, t]), heads(kk0[:, t]), over(inv[:, t]), ALU.mult).then_inc(kk_ok, 1)
                    for t in range(TT):
                        dve.wait_ge(u_ok, n[t])
                        dve.wait_ge(k_cp, n[t])
                        dve.tensor_tensor(coef[:, s, t, :, K_], coef[:, s, t, :, K_], hq(u[:, t]), ALU.mult).then_inc(k_ok, 1)
                mix(0, 0)
                batches(dve, rows)
                bonus(B - 1)

            @block.gpsimd
            def _(pool):
                pool.wait_ge(prep, 1)

                def bonus(b, s):
                    for t in range(TT):
                        pool.wait_ge(bs_ok, b * TT + t + 1)
                        pool.tensor_tensor(bg[:, s, t, 0].rearrange("p (q h e) -> p q h e", q=Q, h=HQ),
                                           coef[:, s, t, :, V_].rearrange("p q (h e) -> p q h e", h=HQ),
                                           bs[:, t].rearrange("p (q h) -> p q h", q=Q).unsqueeze(3).broadcast_to([P, Q, HQ, D]),
                                           ALU.mult).then_inc(bonus_ok, 1)

                def rows(b, s, i, more):
                    n = [b * TT + t + 1 for t in range(TT)]
                    a = [wa[:, t, C:2 * C] for t in range(TT)]
                    if not (isinstance(b, int) and b == 0):
                        bonus(b - 1, 1 - s)
                    for t in range(TT):
                        pool.wait_ge(wa_ok, n[t])
                        pool.tensor_tensor(u[:, t], a[t], ka_row[:], ALU.mult).then_inc(u0_ok, 1)
                    for t in range(TT):
                        pool.wait_ge(u0_ok, n[t])
                        pool.tensor_tensor(u[:, t], u[:, t], oma_row[:], ALU.add).then_inc(u_ok, 1)
                    for t in range(TT):
                        pool.wait_ge(rv_ok, n[t])
                        pool.tensor_tensor(hq(rr[:, t]), coef[:, s, t, :, R_], hq(rk_row[:]), ALU.mult).then_inc(rr0_ok, 1)
                    for t in range(TT):
                        pool.wait_ge(kk_ok, n[t])
                        pool.tensor_tensor(coef[:, s, t, :, B_], hq(kk[:, t]), hq(a[t]), ALU.mult).then_inc(b_ok, 1)
                    for t in range(TT):
                        pool.wait_ge(rr0_ok, n[t])
                        pool.wait_ge(k_ok, n[t])
                        pool.tensor_tensor(hq(rr[:, t]), hq(rr[:, t]), coef[:, s, t, :, K_], ALU.mult).then_inc(rr_ok, 1)
                batches(pool, rows)
                bonus(B - 1, (B - 1) % 2)


def scan(nc, d, ident, zero, coef_d, o_d, w13, xs_d, s_w13, s_xs0):
    ctx = ExitStack()
    with ctx:
        def sb(name, shape, dt=F32):
            return ctx.enter_context(nc.sbuf_tensor(name, shape, dt))

        def sem(name):
            return nc.alloc_semaphore(name)

        NBK = T // TB
        coef = sb("sc_coef", [P, 2, TB, NC6, G])
        state = sb("sc_state", [P, 2, D, G])
        ta = sb("sc_ta", [P, D, G])
        sa = sb("sc_sa", [P, G])
        y = sb("sc_y", [P, 2, D, G])
        x = sb("sc_x", [P, 2, D, G])
        z = sb("sc_z", [P, D, G])
        r = sb("sc_r", [P, 2, D, G])
        JD = 13
        LAG = 2
        OUT = 6
        JP = 4
        part = sb("sc_part", [P, 2, TB, JP, G])
        o_sb = sb("sc_o", [P, 2, TB, G])
        xy_p = [ctx.enter_context(nc.psum_tensor(f"sc_xy_p{i}", [P, D, G], F32)) for i in range(2)]
        r_p = [ctx.enter_context(nc.psum_tensor(f"sc_r_p{i}", [P, 512], F32)) for i in range(2)]
        o_p = [ctx.enter_context(nc.psum_tensor(f"sc_o_p{i}", [P, TB, G], F32)) for i in range(2)]
        ld = [sem(f"c_ld{i}") for i in range(2)]
        stored = [sem(f"c_stored{i}") for i in range(2)]
        used, used2, r2_ok = sem("c_used"), sem("c_used2"), sem("c_r2")
        ta_ok, sa_ok, y_ok, x_ok, xy_ok, z_ok, s_ok, r_ok, r_sum, part_ok, o_m, o_ok = (
            sem("c_" + n) for n in ("ta", "sa", "y", "x", "xy", "z", "s", "r", "r_sum", "part", "o_m", "o"))
        w13_v = d["L0_ffn_moe_w13"].rearrange("e k n -> (e k) n")
        xs_v = xs_d.rearrange("(n p) c -> p n c", p=P)
        ZN = SLOTT // (NBK // 2)
        assert NE * CC == NBK // 2 and 0 < SLOTT - ZN * NBK // 2
        coef_v = coef_d.rearrange("b q t f -> (b q) t f")
        o_v = o_d.rearrange("b q t g -> (b q) t g")

        def heads(ap):
            return ap.rearrange("p j (h i) -> p j h i", h=HQ)

        def by_j(s, k, c, j0=0, j1=D):
            return coef[:, s, k, c].rearrange("p (h j) -> p j h", j=D)[:, j0:j1].unsqueeze(3).broadcast_to([P, j1 - j0, HQ, D])

        def by_i(ap):
            return ap.rearrange("p (h i) -> p h i", h=HQ).unsqueeze(1).broadcast_to([P, D, HQ, D])

        with nc.Block() as block:
            @block.sync
            def _(sp):
                with sp.Fori(0, NBK // 2) as i:
                    for s in range(2):
                        blk = i * 2 + s
                        sp.wait_ge(used, blk + 1)
                        sp.wait_ge(used2, blk + 1)
                        sp.dma_start(coef[:, s].rearrange("p t n g -> p t (n g)"), coef_v[:, bass.ds(blk * TB, TB)]).then_inc(ld[s], 16)
                    sp.dma_start(w13[:, bass.ds(i * (2 * MD), 2 * MD)], w13_v[bass.ds(i * P, P)]).then_inc(s_w13, 16)
                    sp.dma_start(xs_v[:, bass.ds(i * ZN, ZN)], zero[:].unsqueeze(1).broadcast_to([P, ZN, C])).then_inc(s_xs0, 16)
                sp.dma_start(xs_v[:, ZN * NBK // 2:], zero[:].unsqueeze(1).broadcast_to([P, SLOTT - ZN * NBK // 2, C])).then_inc(s_xs0, 16)

            @block.gpsimd
            def _(pool):
                def read_out(s, k, t1):
                    pool.wait_ge(r_sum, t1)
                    pool.tensor_tensor(heads(r[:, k % 2, 0:JD]), heads(state[:, k % 2, 0:JD]), by_j(s, k, R_, 0, JD), ALU.mult).then_inc(r_ok, 1)

                def steps(blk, s, first):
                    pool.wait_ge(ld[s], (blk // 2 + 1) * 16 if first else (blk + 1) * 16)
                    for k in range(TB):
                        p = k % 2
                        t = k + s * TB if first else pool.snap((blk * 2 + s) * TB + k)
                        t1 = t + 1 if first else pool.snap(t + 1)
                        pool.wait_ge(xy_ok, t1)
                        pool.tensor_tensor(heads(x[:, p]), by_i(coef[:, s, k, V_]), by_j(s, k, K_), ALU.mult).then_inc(x_ok, 1)
                        pool.wait_ge(s_ok, t1)
                        pool.tensor_tensor(heads(y[:, p]), heads(state[:, 1 - p]), by_j(s, k, W_), ALU.mult).then_inc(y_ok, 1)
                        if not (first and s == 0 and k == 0):
                            read_out(s if k else 1 - s, (k - 1) % TB, t)
                            if k == 0:
                                pool.wait_ge(r_ok, t)
                                pool.sem_inc(used, 1)

                pool.sem_inc(used, 2)
                pool.sem_inc(xy_ok, 2)
                pool.sem_inc(r_sum, 2)
                for s in range(2):
                    steps(s, s, True)
                with pool.Fori(1, NBK // 2) as i:
                    for s in range(2):
                        steps(i, s, False)
                pool.wait_ge(s_ok, T + 1)
                read_out(1, TB - 1, T)

            @block.vector
            def _(dve):
                dve.memset(state[:], 0.0).then_inc(s_ok, 1)

                def read_out(s, k, t1):
                    dve.wait_ge(r_sum, t1)
                    dve.tensor_tensor(heads(r[:, k % 2, JD:]), heads(state[:, k % 2, JD:]), by_j(s, k, R_, JD, D), ALU.mult).then_inc(r2_ok, 1)

                def steps(i, s, first):
                    dve.wait_ge(ld[s], (i + 1) * 16)
                    for k in range(TB):
                        p = k % 2
                        t = s * TB + k if first else dve.snap((i * 2 + s) * TB + k)
                        t1 = t + 1 if first else dve.snap(t + 1)
                        dve.wait_ge(s_ok, t1)
                        dve.tensor_tensor(heads(ta[:]), heads(state[:, 1 - p]), by_j(s, k, A_), ALU.mult).then_inc(ta_ok, 1)
                        dve.wait_ge(ta_ok, t1)
                        dve.tensor_reduce(sa[:], ta[:].rearrange("p j g -> p g j"), AX.X, ALU.add).then_inc(sa_ok, 1)
                        if not (first and s == 0 and k == 0):
                            read_out(s if k else 1 - s, (k - 1) % TB, t)
                            if k == 0:
                                dve.wait_ge(r2_ok, t)
                                dve.sem_inc(used2, 1)
                        dve.wait_ge(sa_ok, t1)
                        dve.tensor_tensor(heads(z[:]), by_i(sa[:]), by_j(s, k, B_), ALU.mult).then_inc(z_ok, 1)
                        dve.wait_ge(z_ok, t1)
                        dve.wait_ge(xy_ok, t + 3)
                        dve.tensor_tensor(state[:, p], xy_p[p][:], z[:], ALU.add).then_inc(s_ok, 1)

                dve.sem_inc(used2, 2)
                for s in range(2):
                    steps(0, s, True)
                with dve.Fori(1, NBK // 2) as i:
                    for s in range(2):
                        steps(i, s, False)
                dve.wait_ge(s_ok, T + 1)
                read_out(1, TB - 1, T)

            @block.tensor
            def _(pe):
                HJ = D // 2

                def add(src, p, start):
                    for h in range(2):
                        last = pe.matmul(xy_p[p][:, h * HJ:(h + 1) * HJ].rearrange("p j g -> p (j g)"), ident[:],
                                         src[:, p, h * HJ:(h + 1) * HJ].rearrange("p j g -> p (j g)"), start=start, stop=not start)
                    return last

                def sum_r(p, t1):
                    pe.wait_ge(r_ok, t1)
                    pe.wait_ge(r2_ok, t1)
                    pe.wait_ge(part_ok, t1)
                    for j in range(D // JP):
                        last = pe.matmul(r_p[p][:, 0:JP * G], ident[:], r[:, p, j * JP:(j + 1) * JP].rearrange("p j g -> p (j g)"),
                                         start=j == 0, stop=j == D // JP - 1)
                    last.then_inc(r_sum, 1)

                def sum_parts(s, blk1, js):
                    for j in js:
                        if j == 0:
                            pe.wait_ge(part_ok, blk1 * TB + 2)
                            pe.wait_ge(o_ok, blk1)
                        last = pe.matmul(o_p[s][:], ident[:], part[:, s, :, j], start=j == 0, stop=j == JP - 1)
                    if j == JP - 1:
                        last.then_inc(o_m, 1)

                def steps(i, s, first):
                    for k in range(TB):
                        p = k % 2
                        t = s * TB + k if first else pe.snap((i * 2 + s) * TB + k)
                        t1 = t + 1 if first else pe.snap(t + 1)
                        pe.wait_ge(x_ok, t1)
                        if not (first and s == 0 and k == 0):
                            pe.wait_ge(s_ok, t)
                        add(x, p, True)
                        pe.wait_ge(y_ok, t1)
                        add(y, p, False).then_inc(xy_ok, 1)
                        if not (first and s == 0 and k == 0):
                            sum_r(1 - p, t)
                        if 0 <= k - LAG < JP and not (first and s == 0):
                            sum_parts(1 - s, i * 2 + s, [k - LAG])

                for s in range(2):
                    steps(0, s, True)
                with pe.Fori(1, NBK // 2) as i:
                    for s in range(2):
                        steps(i, s, False)
                sum_r(1, T)
                sum_parts(1, NBK, range(JP))

            @block.scalar
            def _(act):
                for s in range(2):
                    act.sem_inc(stored[s], 16)
                act.sem_inc(part_ok, 2)
                act.sem_inc(o_ok, 2)

                def steps(i, s, ks):
                    for k in ks:
                        t = act.snap((i * 2 + s) * TB + k)
                        act.wait_ge(r_sum, t + 3)
                        act.copy(part[:, s, k].rearrange("p j g -> p (j g)"), r_p[k % 2][:, 0:JP * G]).then_inc(part_ok, 1)

                def leave(s, blk1):
                    act.wait_ge(o_m, blk1)
                    act.wait_ge(stored[s], (blk1 + 1) // 2 * 16 if isinstance(blk1, int) else (i + 1 - s) * 16)
                    act.copy(o_sb[:, s], o_p[s][:]).then_inc(o_ok, 1)
                    act.wait_ge(o_ok, blk1 + 2)
                    act.dma_start(o_v[:, bass.ds((blk1 - 1) * TB, TB)], o_sb[:, s]).then_inc(stored[s], 16)

                steps(0, 0, range(TB))
                steps(0, 1, range(OUT))
                leave(0, 1)
                steps(0, 1, range(OUT, TB))
                with act.Fori(1, NBK // 2) as i:
                    for s in range(2):
                        steps(i, s, range(OUT))
                        leave(1 - s, act.snap(i * 2 + s))
                        steps(i, s, range(OUT, TB))
                leave(1, NBK)
                for s in range(2):
                    act.wait_ge(stored[s], 16 * (NBK // 2 + 1))


def attend(nc, d, ident, o_d, bg_d, x2_d, logits):
    ctx = ExitStack()
    with ctx:
        def sb(name, shape, dt=F32):
            return ctx.enter_context(nc.sbuf_tensor(name, shape, dt))

        def ps(name, shape):
            return ctx.enter_context(nc.psum_tensor(name, shape, F32))

        HC = H // CC
        HB = HC // 2
        HV = HB * D
        SG = H // HB
        NU = TT * SG
        assert HB * LKV <= 512 and 2 * HV == P
        w_o = sb("w_o", [P, CC, C])
        w_q = sb("w_q", [P, CC, C])
        w_k = sb("w_k", [CD, C])
        w_v = sb("w_v", [CD, C])
        w_xo = sb("w_xo", [P, CC, C])
        router = sb("router", [P, CC, NE])
        b_q = sb("b_q", [P, CC])
        b_k = sb("b_k", [P, CC])
        bv_row = sb("bv_row", [P, C])
        bo_row = sb("bo_row", [P, C])
        gw_row = sb("gw_row", [P, C])
        gb_row = sb("gb_row", [P, C])
        own = sb("own", [P, HC])
        eps = sb("eps", [P, 1])

        o_in = sb("o_in", [P, TT, Q, G])
        bg_in = sb("bg_in", [P, TT, 2, C])
        x_in = sb("a_x_in", [P, TT, C])
        ctx_in = sb("ctx_in", [LKV, CD])
        mu = sb("mu", [P, TT * H])
        oc = sb("oc", [P, TT, C])
        sq = sb("a_sq", [P, TT, C])
        ss = sb("a_ss", [P, TT * H])
        sd = sb("sd", [P, TT * H])
        rs = sb("rs", [P, TT * H])
        zz = sb("zz", [P, TT, C])
        z_t = sb("z_t", [P, CC, T])
        y1 = sb("y1", [P, TT, C])
        x1 = sb("x1", [P, TT, C])
        x1b = sb("x1b", [P, 2, TT, C])
        x1_t = sb("x1_t", [P, CC, T])
        q_t = sb("q_t", [P, CC, T])
        ctx_t = sb("ctx_t", [CD, LKV])
        k_t = sb("k_t", [P, CC, LKV])
        k_own = sb("k_own", [P, CC, HC, LKV])
        v_own = sb("v_own", [LKV, 2, H, P])
        mx = sb("mx", [P, TT, SG, HB])
        pr = sb("pr", [P, TT, CC, HC, LKV])
        p_t = sb("p_t", [LKV, H, T])
        num_t = sb("num_t", [P, CC, T])
        den_t = sb("den_t", [P, CC, T])
        rden_h = sb("rden_h", [P, TT * H])
        rden = sb("rden", [P, CC, TT, HC, D])
        at_t = sb("at_t", [P, CC, T])
        y2 = sb("y2", [P, TT, C])
        x2 = sb("x2", [P, TT, C])
        x2_t = sb("x2_t", [P, CC, T])
        norms = {n: [sb(f"{n}_{k}", [P, TT, w]) for k, w in (("bn6", 6), ("mv", 2), ("std", 1), ("rstd", 1))] for n in ("n1", "n2")}

        a_p = ps("a_p", [P, 512])
        c_p = ps("c_p", [P, 512])
        sc_p = [ps(f"sc_p{i}", [P, 512]) for i in range(2)]
        pt_p = [ps(f"pt_p{i}", [P, HB, P]) for i in range(2)]
        pv_p = ps("pv_p", [P, CC, 2 * T])

        names = ("wld zeroed own wload consts ld_o ld_bg ld_x ld_ctx x2_st mu oc sq ss sd rs zz z1 z2 z3 z zt zt_ok y y1 bn1 mv1 std1 "
                 "rstd1 x1 x1b x1t x1t_ok q q_ok ctx ctx_ok kv k_ok v_ok k_own sc mx sub ex pt pt_ok pv pv_ok dt rden_h rden rt at y2 y2_ok "
                 "bn2 mv2 std2 rstd2 x2 x2t x2t_ok lg lg_ok passed")
        S = {n: nc.alloc_semaphore("a_" + n) for n in names.split()}

        def wait(eng, name, value):
            if not (isinstance(value, int) and value <= 0):
                eng.wait_ge(S[name], value)

        def row(name):
            return d[name].unsqueeze(0).broadcast_to([P, C])

        def flat(ap):
            return ap.rearrange("p a b -> p (a b)")

        def heads(ap):
            return ap.rearrange("p t (h e) -> p (t h) e", h=H)

        def over(ap):
            return ap.unsqueeze(2).broadcast_to([P, TT * H, D])

        def rounds(eng, round_):
            for j in range(4):
                round_(j, j % 2, True, j >= 1, j >= 2, j >= 3, j >= 4)
            with eng.Fori(2, B // 2) as i:
                for par in range(2):
                    round_(eng.snap(i * 2 + par), par, True, True, True, True, True)
            for j in range(B, B + 4):
                round_(j, j % 2, False, j < B + 1, j < B + 2, j < B + 3, True)

        loads = [(w_o[:], d["L0_attn_W_o"].rearrange("(c p) n -> p c n", p=P)),
                 (w_q[:], d["L0_xattn_Wq"].rearrange("(c p) n -> p c n", p=P)),
                 (w_k[:], d["L0_xattn_Wk"]), (w_v[:], d["L0_xattn_Wv"]),
                 (w_xo[:], d["L0_xattn_Wo"].rearrange("(c p) n -> p c n", p=P)),
                 (router[:], d["L0_ffn_moe_router"].rearrange("(c p) n -> p c n", p=P)),
                 (bv_row[:], row("L0_xattn_bv")), (bo_row[:], row("L0_xattn_bo")),
                 (gw_row[:], row("L0_attn_gn_weight")), (gb_row[:], row("L0_attn_gn_bias")),
                 (b_q[:], d["L0_xattn_bq"].rearrange("(c p) -> p c", p=P)),
                 (b_k[:], d["L0_xattn_bk"].rearrange("(c p) -> p c", p=P))]

        with nc.Block() as block:
            @block.sync
            def _(sp):
                for dst, src in loads:
                    sp.dma_start(dst, src, allow_slow_non_contiguous=True).then_inc(S["wld"], 16)
                sp.wait_ge(S["wld"], 16 * len(loads))
                sp.sem_inc(S["wload"], 1)

                def load(j, par, g, a, b, c, r):
                    if g:
                        wait(sp, "oc", j)
                        for t in range(TT):
                            sp.dma_start(o_in[:, t], o_d[bass.ds(j, 1), :, t * P:(t + 1) * P].rearrange("o q p g -> p (o q) g")).then_inc(S["ld_o"], 16)
                    if a:
                        wait(sp, "y1", j - 1)
                        sp.dma_start(x_in[:], d["x"][bass.ds(j - 1, 1)].rearrange("o (t p) c -> p (o t) c", p=P)).then_inc(S["ld_x"], 16)
                        wait(sp, "ctx", j - 1)
                        sp.dma_start(ctx_in[:], d["ctx_512"][bass.ds(j - 1, 1)].rearrange("o k c -> (o k) c")).then_inc(S["ld_ctx"], 16)
                    if g:
                        wait(sp, "z", j)
                        sp.dma_start(bg_in[:].rearrange("p t k c -> p t (k c)"),
                                     bg_d[bass.ds(j * T, T)].rearrange("(t p) f -> p t f", p=P)).then_inc(S["ld_bg"], 16)
                rounds(sp, load)

            @block.tensor
            def _(pe):
                pe.wait_ge(S["wload"], 1)
                pe.wait_ge(S["consts"], 2)

                def turn(dst, src):
                    for t in range(TT):
                        for c in range(CC):
                            last = pe.transpose(dst[:, c * T + t * P:c * T + (t + 1) * P], src[:, t, c * P:(c + 1) * P], ident[:])
                    return last

                def turn_back(src_t):
                    for c in range(CC):
                        for t in range(TT):
                            last = pe.transpose(c_p[:, c * T + t * P:c * T + (t + 1) * P], src_t[:, c, t * P:(t + 1) * P], ident[:])
                    return last

                def times(dst, src_t, w, cols, ts=range(TT)):
                    for t in ts:
                        for c in range(CC):
                            last = pe.matmul(dst[:, t * cols:(t + 1) * cols], src_t[:, c, t * P:(t + 1) * P], w[:, c],
                                             start=c == 0, stop=c == CC - 1)
                    return last

                def scores(b, u):
                    t, g = divmod(u, SG)
                    if u == 0:
                        wait(pe, "q_ok", b + 1)
                        wait(pe, "k_own", b + 1)
                    wait(pe, "sub", b * NU + u - 1)
                    pe.matmul(sc_p[u % 2][:, 0:HB * LKV], q_t[:, g // 2, t * P:(t + 1) * P],
                              k_own[:, g // 2, (g % 2) * HB:(g % 2 + 1) * HB].rearrange("p h k -> p (h k)"),
                              start=True, stop=True).then_inc(S["sc"], 1)

                def turn_probs(b, t):
                    for g in range(SG):
                        n = b * (TT * SG) + t * SG + g
                        if g % 2 == 0:
                            wait(pe, "ex", b * (TT * CC) + t * CC + g // 2 + 1)
                        wait(pe, "pt_ok", n - 1)
                        for h in range(HB):
                            last = pe.transpose(pt_p[g % 2][0:LKV, h], pr[:, t, g // 2, (g % 2) * HB + h], ident[:])
                        last.then_inc(S["pt"], 1)

                def queries(j):
                    wait(pe, "x1t_ok", j)
                    for m in range(CC):
                        for k in range(CC):
                            last = pe.matmul(a_p[:, m * T:(m + 1) * T], w_q[:, k, m * P:(m + 1) * P], x1_t[:, k],
                                             start=k == 0, stop=k == CC - 1)
                    last.then_inc(S["q"], 1)

                def values(j, slot, g):
                    f, e = divmod(g, 2)
                    if g == 0:
                        wait(pe, "pt_ok", (j - 2) * NU)
                    if e == 0:
                        wait(pe, "pv_ok", (j - 4) * CC + f + 1)
                    for h in range(HB):
                        last = pe.matmul(pv_p[:, f, e * T:(e + 1) * T], v_own[:, slot, g * HB + h], p_t[:, g * HB + h],
                                         start=h == 0, stop=h == HB - 1)
                    if e == 1:
                        last.then_inc(S["pv"], 1)

                def round_(j, par, g, a, b, c, r):
                    if b:
                        scores(j - 2, 0)
                        scores(j - 2, 1)
                    if r:
                        wait(pe, "x2", j - 3)
                        turn(c_p, x2).then_inc(S["x2t"], 1)
                    if a:
                        wait(pe, "z", j)
                        wait(pe, "q_ok", j - 1)
                        turn(a_p, zz).then_inc(S["zt"], 1)
                    for n in range(SG):
                        if c:
                            values(j, 1 - par, n)
                        if r and n == 1:
                            wait(pe, "x2t_ok", j - 3)
                            times(c_p, x2_t, router, NE).then_inc(S["lg"], 1)
                        if b:
                            scores(j - 2, 2 + n)
                        if a and n == 1:
                            wait(pe, "zt_ok", j)
                            times(a_p, z_t, w_o, C).then_inc(S["y"], 1)
                    if a:
                        wait(pe, "y1", j)
                        wait(pe, "ld_ctx", j * 16)
                        pe.transpose(a_p[:, 0:LKV], ctx_in[:], ident[0:LKV, 0:LKV]).then_inc(S["ctx"], 1)
                    if b:
                        scores(j - 2, 6)
                    if c:
                        wait(pe, "pv_ok", (j - 2) * CC)
                        wait(pe, "lg_ok", j - 3)
                        turn_back(den_t).then_inc(S["dt"], 1)
                    if b:
                        turn_probs(j - 2, 0)
                    if b:
                        scores(j - 2, 7)
                    if a:
                        wait(pe, "ctx_ok", j)
                        for m in range(CC):
                            pe.matmul(a_p[:, m * LKV:(m + 1) * LKV], w_k[:, m * P:(m + 1) * P], ctx_t[:], start=True, stop=True)
                        pe.matmul(a_p[0:LKV, CC * LKV:CC * LKV + C], ctx_t[:], w_v[:], start=True, stop=True).then_inc(S["kv"], 1)
                    if c:
                        wait(pe, "rden", j - 2)
                        for f in range(CC):
                            for t in range(TT):
                                last = pe.transpose(c_p[:, f * T + t * P:f * T + (t + 1) * P],
                                                    rden[:, f, t].rearrange("p h e -> p (h e)"), ident[:])
                        last.then_inc(S["rt"], 1)
                    if b:
                        turn_probs(j - 2, 1)
                    if c:
                        wait(pe, "at", j - 2)
                        times(c_p, at_t, w_xo, C, [0])
                    if a:
                        wait(pe, "x1", j)
                        wait(pe, "k_ok", j)
                        wait(pe, "v_ok", j)
                        turn(a_p, x1).then_inc(S["x1t"], 1)
                    if c:
                        times(c_p, at_t, w_xo, C, [1]).then_inc(S["y2"], 1)
                    if a:
                        queries(j)
                rounds(pe, round_)

            @block.scalar
            def _(act):
                act.wait_ge(S["wload"], 1)
                act.wait_ge(S["consts"], 2)

                def leave_probs(b, t):
                    for g in range(SG):
                        wait(act, "pt", b * (TT * SG) + t * SG + g + 1)
                        if t == 0 and g == 0:
                            wait(act, "pv", b * 2)
                        act.copy(p_t[:, g * HB:(g + 1) * HB, t * P:(t + 1) * P], pt_p[g % 2][0:LKV]).then_inc(S["pt_ok"], 1)

                def exp(b, t, c):
                    wait(act, "sub", b * NU + t * SG + c * 2 + 2)
                    act.activation(pr[:, t, c], pr[:, t, c], ACT.Exp).then_inc(S["ex"], 1)

                def leave_values(j, f):
                    wait(act, "pv", (j - 3) * CC + f + 1)
                    if f == 0:
                        wait(act, "at", j - 3)
                    for e in range(2):
                        half = slice(e * HV, (e + 1) * HV)
                        act.copy(num_t[half, f], pv_p[0:HV, f, e * T:(e + 1) * T])
                        last = act.copy(den_t[half, f], pv_p[HV:2 * HV, f, e * T:(e + 1) * T])
                    last.then_inc(S["pv_ok"], 1)

                def round_(j, par, g, a, b, c, r):
                    if g:
                        wait(act, "oc", j + 1)
                        act.activation(flat(sq[:]), flat(oc[:]), ACT.Square).then_inc(S["sq"], 1)
                    if a:
                        wait(act, "zt", j)
                        act.copy(flat(z_t[:]), a_p[:]).then_inc(S["zt_ok"], 1)
                    if r:
                        wait(act, "x2t", j - 3)
                        act.copy(flat(x2_t[:]), c_p[:]).then_inc(S["x2t_ok"], 1)
                    if b:
                        exp(j - 2, 0, 0)
                    if r:
                        act.dma_start(x2_d[bass.ds((j - 4) * T, T)].rearrange("(t p) c -> p t c", p=P), x2[:]).then_inc(S["x2_st"], 16)
                        wait(act, "lg", j - 3)
                        act.copy(logits[:, bass.ds((j - 4) * TT, TT)].rearrange("p t e -> p (t e)"), c_p[:, 0:TT * NE]).then_inc(S["lg_ok"], 1)
                    if c:
                        leave_values(j, 0)
                    if b:
                        exp(j - 2, 0, 1)
                    if c:
                        leave_values(j, 1)
                    if a:
                        wait(act, "ctx", j)
                        act.copy(ctx_t[:], a_p[:, 0:LKV]).then_inc(S["ctx_ok"], 1)
                    if b:
                        leave_probs(j - 2, 0)
                        exp(j - 2, 1, 0)
                        exp(j - 2, 1, 1)
                    if b:
                        leave_probs(j - 2, 1)
                    if g:
                        wait(act, "ss", j + 1)
                        act.activation(sd[:], ss[:], ACT.Sqrt, bias=eps[:], scale=1.0 / D).then_inc(S["sd"], 1)
                    if a:
                        wait(act, "mv1", j)
                        act.activation(norms["n1"][2][:], norms["n1"][1][:, :, 1:2], ACT.Sqrt, bias=eps[:]).then_inc(S["std1"], 1)
                    if a:
                        wait(act, "x1t", j)
                        act.copy(flat(x1_t[:]), a_p[:]).then_inc(S["x1t_ok"], 1)
                    if c:
                        wait(act, "mv2", j - 2)
                        act.activation(norms["n2"][2][:], norms["n2"][1][:, :, 1:2], ACT.Sqrt, bias=eps[:]).then_inc(S["std2"], 1)
                    if a:
                        wait(act, "q", j)
                        wait(act, "sc", (j - 1) * NU)
                        for m in range(CC):
                            last = act.activation(q_t[:, m], a_p[:, m * T:(m + 1) * T], ACT.Identity, bias=b_q[:, m:m + 1])
                        last.then_inc(S["q_ok"], 1)
                rounds(act, round_)
                act.wait_ge(S["x2_st"], B * 16)

            @block.vector
            def _(dve):
                dve.memset(v_own[:], 0.0).then_inc(S["zeroed"], 1)
                dve.wait_ge(S["zeroed"], 1)
                for h in range(HB):
                    for s in range(2):
                        dve.memset(v_own[:, s].rearrange("p (g h) n -> p g h n", h=HB)[:, :, h, HV + h * D:HV + (h + 1) * D], 1.0)
                dve.memset(eps[:], EPS).then_inc(S["consts"], 1)
                dve.wait_ge(S["wload"], 1)

                def moments(n, src, bn_s, mv_s, value):
                    bn6, mv, std, rstd = norms[n]
                    for t in range(TT):
                        last = dve.bn_stats(bn6[:, t], src[:, t])
                    last.then_inc(S[bn_s], 1)
                    wait(dve, bn_s, value)
                    dve.sem_inc(S["passed"], 1)
                    for t in range(TT):
                        last = dve.bn_aggr(mv[:, t], bn6[:, t])
                    last.then_inc(S[mv_s], 1)

                def normalise(n, dst, src, std_s, rstd_s, done, value):
                    bn6, mv, std, rstd = norms[n]
                    wait(dve, std_s, value)
                    dve.reciprocal(rstd[:], std[:]).then_inc(S[rstd_s], 1)
                    wait(dve, rstd_s, value)
                    for t in range(TT):
                        last = dve.tensor_scalar(dst[:, t], src[:, t], mv[:, t, 0:1], rstd[:, t], ALU.subtract, ALU.mult)
                    last.then_inc(S[done], 1)

                def shift(b, u):
                    t, g = divmod(u, SG)
                    n = b * NU + u + 1
                    wait(dve, "sc", n)
                    view = sc_p[u % 2][:, 0:HB * LKV].rearrange("p (h k) -> p h k", h=HB)
                    m = mx[:, t, g]
                    wait(dve, "sub", n - NU)
                    dve.tensor_reduce(m, view, AX.X, ALU.max).then_inc(S["mx"], 1)
                    wait(dve, "mx", n)
                    if g == 0:
                        wait(dve, "pt", (b - 1) * NU + (t + 1) * SG)
                    dve.tensor_tensor(pr[:, t, g // 2, (g % 2) * HB:(g % 2 + 1) * HB], view,
                                      m.unsqueeze(2).broadcast_to([P, HB, LKV]), ALU.subtract).then_inc(S["sub"], 1)

                def round_(j, par, g, a, b, c, r):
                    if g:
                        src = o_in[:].rearrange("p t q (h e) -> p (t q h) e", e=D)
                        wait(dve, "ld_o", (j + 1) * (16 * TT))
                        dve.tensor_reduce(mu[:], src, AX.X, ALU.add).then_inc(S["mu"], 1)
                    if b:
                        shift(j - 2, 0)
                    if g:
                        wait(dve, "mu", j + 1)
                        wait(dve, "zz", j)
                        dve.scalar_tensor_tensor(heads(oc[:]), over(mu[:]), -1.0 / D, src, ALU.mult, ALU.add).then_inc(S["oc"], 1)
                    if b:
                        for u in range(1, 4):
                            shift(j - 2, u)
                    if g:
                        wait(dve, "sq", j + 1)
                        wait(dve, "sd", j)
                        dve.tensor_reduce(ss[:], heads(sq[:]), AX.X, ALU.add).then_inc(S["ss"], 1)
                    if b:
                        shift(j - 2, 4)
                    if a:
                        wait(dve, "y", j)
                        wait(dve, "ld_x", j * 16)
                        wait(dve, "x1", j - 1)
                        dve.tensor_tensor(flat(y1[:]), a_p[:], flat(x_in[:]), ALU.add).then_inc(S["y1"], 1)
                        wait(dve, "y1", j)
                        moments("n1", y1, "bn1", "mv1", j)
                    if b:
                        shift(j - 2, 5)
                        shift(j - 2, 6)
                    if c:
                        wait(dve, "dt", j - 2)
                        wait(dve, "rt", j - 3)
                        dve.reciprocal(rden_h[:], c_p[:].rearrange("p (n e) -> p n e", e=D)[:, :, 0]).then_inc(S["rden_h"], 1)
                        wait(dve, "rden_h", j - 2)
                        dve.tensor_copy(rden[:].rearrange("p c t h e -> p (c t h) e"),
                                        rden_h[:].unsqueeze(2).broadcast_to([P, TT * H, D])).then_inc(S["rden"], 1)
                    if b:
                        shift(j - 2, 7)
                    if a:
                        wait(dve, "kv", j)
                        wait(dve, "k_own", j - 1)
                        for m in range(CC):
                            last = dve.tensor_scalar(k_t[:, m], a_p[:, m * LKV:(m + 1) * LKV], b_k[:, m:m + 1], 0.25, ALU.add, ALU.mult)
                        last.then_inc(S["k_ok"], 1)
                        wait(dve, "pv", (j - 2) * CC)
                        for h in range(HB):
                            last = dve.tensor_tensor(
                                v_own[:, 1 - par].rearrange("p (g h) n -> p g h n", h=HB)[:, :, h, h * D:(h + 1) * D],
                                a_p[0:LKV, CC * LKV:CC * LKV + C].rearrange("p (g h e) -> p g h e", h=HB, e=D)[:, :, h],
                                bv_row[0:LKV].rearrange("p (g h e) -> p g h e", h=HB, e=D)[:, :, h], ALU.add)
                        last.then_inc(S["v_ok"], 1)
                    if c:
                        wait(dve, "rt", j - 2)
                        wait(dve, "y2", j - 3)
                        dve.tensor_tensor(flat(at_t[:]), c_p[:], flat(num_t[:]), ALU.mult).then_inc(S["at"], 1)
                    if a:
                        wait(dve, "x1b", j - 1)
                        wait(dve, "x1t", j - 1)
                        normalise("n1", x1, y1, "std1", "rstd1", "x1", j)
                    if g:
                        wait(dve, "sd", j + 1)
                        wait(dve, "zz", j)
                        dve.reciprocal(rs[:], sd[:]).then_inc(S["rs"], 1)
                    if g:
                        wait(dve, "rs", j + 1)
                        wait(dve, "zt", j)
                        dve.tensor_tensor(heads(zz[:]), heads(oc[:]), over(rs[:]), ALU.mult).then_inc(S["zz"], 1)
                    if c:
                        wait(dve, "y2", j - 2)
                        wait(dve, "x1b", j - 2)
                        wait(dve, "x2", j - 3)
                        dve.tensor_tensor(flat(y2[:]), c_p[:], flat(x1b[:, 1 - par]), ALU.add).then_inc(S["y2_ok"], 1)
                        wait(dve, "y2_ok", j - 2)
                        moments("n2", y2, "bn2", "mv2", j - 2)
                        wait(dve, "x2_st", (j - 3) * 16)
                        wait(dve, "x2t", j - 3)
                        normalise("n2", x2, y2, "std2", "rstd2", "x2", j - 2)
                rounds(dve, round_)

            @block.gpsimd
            def _(pool):
                pool.memset(own[:], 1.0).then_inc(S["own"], 1)
                pool.wait_ge(S["own"], 1)
                pool.affine_select(out=own[:], in_=own[:], compare_op=ALU.is_ge, fill=0.0, base=0,
                                   pattern=[[-D, HC]], channel_multiplier=1).then_inc(S["own"], 1)
                pool.wait_ge(S["own"], 2)
                pool.affine_select(out=own[:], in_=own[:], compare_op=ALU.is_ge, fill=0.0, base=D - 1,
                                   pattern=[[D, HC]], channel_multiplier=-1).then_inc(S["consts"], 1)
                pool.wait_ge(S["consts"], 2)
                pool.wait_ge(S["wload"], 1)

                def round_(j, par, g, a, b, c, r):
                    def tiles(ap):
                        return ap.unsqueeze(1).broadcast_to([P, TT, C])
                    if a:
                        wait(pool, "k_ok", j)
                        wait(pool, "sc", (j - 1) * NU)
                        for m in range(CC):
                            last = pool.tensor_tensor(k_own[:, m], k_t[:, m].unsqueeze(1).broadcast_to([P, HC, LKV]),
                                                      own[:].unsqueeze(2).broadcast_to([P, HC, LKV]), ALU.mult)
                        last.then_inc(S["k_own"], 1)
                    if g:
                        wait(pool, "zz", j + 1)
                        pool.tensor_tensor(zz[:], zz[:], tiles(gw_row[:]), ALU.mult).then_inc(S["z1"], 1)
                        wait(pool, "z1", j + 1)
                        pool.tensor_tensor(zz[:], zz[:], tiles(gb_row[:]), ALU.add).then_inc(S["z2"], 1)
                        wait(pool, "z2", j + 1)
                        wait(pool, "ld_bg", (j + 1) * 16)
                        pool.tensor_tensor(zz[:], zz[:], bg_in[:, :, 0], ALU.add).then_inc(S["z3"], 1)
                        wait(pool, "z3", j + 1)
                        pool.tensor_tensor(zz[:], zz[:], bg_in[:, :, 1], ALU.mult).then_inc(S["z"], 1)
                    if a:
                        wait(pool, "x1", j)
                        wait(pool, "y2_ok", j - 2)
                        pool.tensor_tensor(x1b[:, 1 - par], x1[:], tiles(bo_row[:]), ALU.add).then_inc(S["x1b"], 1)
                rounds(pool, round_)


def dispatch(nc, d, logits, slots, gates, pair_experts, w2, s_w2):
    ctx = ExitStack()
    with ctx:
        def sb(name, shape, dt=F32):
            return ctx.enter_context(nc.sbuf_tensor(name, shape, dt))

        def sem(name):
            return nc.alloc_semaphore(name)

        FULL = [P, NT, NE]
        e_int = sb("e_int", [P, NE], I32)
        j_int = sb("j_int", [1, SLOTT], I32)
        e_row, e8_row = sb("e_row", [P, NE]), sb("e8_row", [P, NE])
        j_row = sb("j_row", [1, SLOTT])
        before = sb("before", [P, P])
        ones = sb("ones", [P, P])
        top = [sb(f"top{k}", [P, NT]) for k in range(2)]
        idx = [sb(f"idx{k}", [P, NT]) for k in range(2)]
        mask = [sb(f"mask{k}", FULL) for k in range(2)]
        eq, cand, l2 = sb("eq", FULL), sb("cand", FULL), sb("l2", FULL)
        gap, ex, den = sb("gap", [P, NT]), sb("ex", [P, NT]), sb("den", [P, NT])
        both, tot = sb("both", FULL), sb("tot", FULL)
        run = [sb(f"run{k}", FULL) for k in range(2)]
        cnt, padded, cum0, cum1, off = (sb("d_" + n, [P, NE]) for n in ("cnt", "padded", "cum0", "cum1", "off"))
        cnt_i = sb("cnt_i", [P, NE], I32)
        slot_f = sb("slot_f", [P, NT])
        past = sb("past", [1, SLOTT, NE])
        te, te_pair, te_before = sb("te", [1, SLOTT]), sb("te_pair", [1, SLOTT // 2]), sb("te_before", [1, SLOTT // 2])
        pre_p = ctx.enter_context(nc.psum_tensor("pre_p", [P, 512], F32))
        tot_p = ctx.enter_context(nc.psum_tensor("tot_p", [P, 512], F32))
        consts, step, gap_ok, ex_ok, both_ok, ranks = (sem("d_" + n) for n in ("consts", "step", "gap_ok", "ex_ok", "both_ok", "ranks"))

        def per_tile(ap):
            return ap.unsqueeze(2).broadcast_to(FULL)

        def per_expert(ap):
            return ap.unsqueeze(1).broadcast_to(FULL)

        w2_v = d["L0_ffn_moe_w2"].rearrange("e (m p) n -> p (e m) n", p=P)
        with nc.Block() as block:
            @block.sync
            def _(sp):
                for n in range(4):
                    part = slice(n * (NE * MD // P // 4), (n + 1) * (NE * MD // P // 4))
                    sp.dma_start(w2[:, part], w2_v[:, part]).then_inc(s_w2, 16)

            @block.gpsimd
            def _(pool):
                pool.iota(e_int[:], pattern=[[1, NE]], base=0, channel_multiplier=0).then_inc(consts, 1)
                pool.iota(j_int[:], pattern=[[P, SLOTT]], base=0, channel_multiplier=0).then_inc(consts, 1)
                pool.memset(ones[:], 1.0).then_inc(consts, 1)
                pool.wait_ge(consts, 3)
                pool.affine_select(out=before[:], in_=ones[:], compare_op=ALU.is_gt, fill=0.0, base=0,
                                   pattern=[[1, P]], channel_multiplier=-1).then_inc(consts, 1)

            @block.tensor
            def _(pe):
                pe.wait_ge(consts, 4)
                pe.wait_ge(both_ok, 1)
                rhs = both[:].rearrange("p n e -> p (n e)")
                pe.matmul(pre_p[:], before[:], rhs, start=True, stop=True)
                pe.matmul(tot_p[:], ones[:], rhs, start=True, stop=True).then_inc(ranks, 1)

            @block.scalar
            def _(act):
                act.wait_ge(gap_ok, 1)
                act.activation(ex[:], gap[:], ACT.Exp).then_inc(ex_ok, 1)

            @block.vector
            def _(dve):
                count = [0]

                def then(ins):
                    count[0] += 1
                    ins.then_inc(step, 1)
                    dve.wait_ge(step, count[0])

                dve.wait_ge(consts, 2)
                dve.tensor_copy(j_row[:], j_int[:])
                then(dve.tensor_copy(e_row[:], e_int[:]))
                then(dve.tensor_scalar(e8_row[:], e_row[:], float(NE), None, ALU.add))
                values = logits[:]
                for k in range(2):
                    then(dve.tensor_reduce(top[k][:], values, AX.X, ALU.max))
                    then(dve.tensor_tensor(eq[:], values, per_tile(top[k][:]), ALU.is_equal))
                    then(dve.scalar_tensor_tensor(cand[:], eq[:], -float(NE), per_expert(e8_row[:]), ALU.mult, ALU.add))
                    then(dve.tensor_reduce(idx[k][:], cand[:], AX.X, ALU.min))
                    then(dve.tensor_tensor(mask[k][:], per_expert(e_row[:]), per_tile(idx[k][:]), ALU.is_equal))
                    if k == 0:
                        then(dve.scalar_tensor_tensor(l2[:], mask[0][:], -3e38, logits[:], ALU.mult, ALU.add))
                        values = l2[:]
                dve.tensor_tensor(gap[:], top[1][:], top[0][:], ALU.subtract).then_inc(gap_ok, 1)
                dve.tensor_tensor(both[:], mask[0][:], mask[1][:], ALU.add).then_inc(both_ok, 1)
                dve.wait_ge(ex_ok, 1)
                then(dve.tensor_scalar(den[:], ex[:], 1.0, None, ALU.add))
                then(dve.reciprocal(gates[:, 0], den[:]))
                then(dve.tensor_tensor(gates[:, 1], ex[:], gates[:, 0], ALU.mult))
                dve.wait_ge(ranks, 1)
                then(dve.tensor_copy(tot[:].rearrange("p n e -> p (n e)"), tot_p[:]))
                src, k, s = tot, 0, 1
                while s < NT:
                    dst = run[k]
                    dve.tensor_copy(dst[:, 0:s], src[:, 0:s])
                    then(dve.tensor_tensor(dst[:, s:], src[:, s:], src[:, 0:NT - s], ALU.add))
                    src, k, s = dst, 1 - k, 2 * s
                incl = src
                then(dve.tensor_scalar(cnt[:], incl[:, NT - 1], float(P - 1), None, ALU.add))
                then(dve.tensor_copy(cnt_i[:], cnt[:]))
                then(dve.tensor_scalar(cnt_i[:], cnt_i[:], -P, None, ALU.bitwise_and))
                then(dve.tensor_copy(padded[:], cnt_i[:]))
                a, k, s = padded, 0, 1
                while s < NE:
                    c = (cum0, cum1)[k]
                    dve.tensor_copy(c[:, 0:s], a[:, 0:s])
                    then(dve.tensor_tensor(c[:, s:], a[:, s:], a[:, 0:NE - s], ALU.add))
                    a, k, s = c, 1 - k, 2 * s
                then(dve.tensor_tensor(off[:], a[:], padded[:], ALU.subtract))
                base = run[0] if incl is run[1] else run[1]
                then(dve.tensor_tensor(base[:], incl[:], tot[:], ALU.subtract))
                then(dve.tensor_tensor(base[:], base[:], per_expert(off[:]), ALU.add))
                then(dve.tensor_tensor(base[:].rearrange("p n e -> p (n e)"), pre_p[:], base[:].rearrange("p n e -> p (n e)"), ALU.add))
                for k in range(2):
                    then(dve.tensor_tensor(eq[:], mask[k][:], base[:], ALU.mult))
                    then(dve.tensor_reduce(slot_f[:], eq[:], AX.X, ALU.add))
                    then(dve.tensor_copy(slots[:, k], slot_f[:]))
                wide = [1, SLOTT, NE]
                then(dve.tensor_tensor(past[:], j_row[:].unsqueeze(2).broadcast_to(wide), a[0:1].unsqueeze(1).broadcast_to(wide), ALU.is_ge))
                then(dve.tensor_reduce(te[:], past[:], AX.X, ALU.add))
                then(dve.tensor_scalar(te[:], te[:], float(NE - 1), None, ALU.min))
                pair = te[:].rearrange("p (n k) -> p n k", k=2)
                dve.tensor_copy(te_before[:, 0:1], te[:, 0:1])
                dve.tensor_copy(te_before[:, 1:], pair[:, 0:SLOTT // 2 - 1, 1])
                then(dve.tensor_scalar(te_pair[:], pair[:, :, 1], float(NE), None, ALU.mult))
                then(dve.tensor_tensor(te_pair[:], te_pair[:], pair[:, :, 0], ALU.add))
                then(dve.scalar_tensor_tensor(te_pair[:], te_pair[:], float(NE), te_before[:], ALU.mult, ALU.add))
                then(dve.tensor_copy(pair_experts[:], te_pair[:]))


def scatter(nc, x2_d, slots, xs_d, s_xs0):
    ctx = ExitStack()
    with ctx:
        SL = 4
        row = ctx.enter_context(nc.sbuf_tensor("sx_row", [P, SL, C], F32))
        at = ctx.enter_context(nc.sbuf_tensor("sx_at", [P, SL, 2, 1], U32))
        sem = nc.alloc_semaphore
        at_ok, passed = sem("x_at_ok"), sem("x_passed")
        row_ld = [sem(f"x_row_ld{s}") for s in range(SL)]
        sent = [sem(f"x_sent{s}") for s in range(SL)]

        def rounds(eng, body):
            body(0, 0)
            with eng.Fori(1, NT // SL) as i:
                body(eng.snap(i * SL), i)

        def free(eng, s, i):
            if not (isinstance(i, int) and i == 0):
                eng.wait_ge(sent[s], i * 32)

        with nc.Block() as block:
            @block.sync
            def _(sp):
                def load(n, i):
                    for s in range(SL):
                        free(sp, s, i)
                        sp.dma_start(row[:, s], x2_d[bass.ds((n + s) * P, P)]).then_inc(row_ld[s], 16)
                rounds(sp, load)

            @block.vector
            def _(dve):
                def pick(n, i):
                    for s in range(SL):
                        free(dve, s, i)
                        dve.tensor_copy(at[:, s], slots[:, :, bass.ds(n + s, 1)]).then_inc(at_ok, 1)
                rounds(dve, pick)

            @block.gpsimd
            def _(pool):
                pool.wait_ge(s_xs0, 16 * (T // TB // 2 + 1))

                def send(n, i):
                    for s in range(SL):
                        pool.wait_ge(at_ok, n + s + 1)
                        pool.wait_ge(row_ld[s], (i + 1) * 16)
                        pool.sem_inc(passed, 1)
                        for k in range(2):
                            pool.indirect_dma_start(xs_d, bass.IndirectOffsetOnAxis(at[:, s, k], 0), row[:, s], None).then_inc(sent[s], 16)
                rounds(pool, send)
                for s in range(SL):
                    pool.wait_ge(sent[s], NT // SL * 32)


def experts(nc, ident, w13, w2, s_w13, s_w2, pair_experts, xs_d, ys_d):
    ctx = ExitStack()
    with ctx:
        def sb(name, shape, dt=F32):
            return ctx.enter_context(nc.sbuf_tensor(name, shape, dt))

        def ps(name, shape):
            return ctx.enter_context(nc.psum_tensor(name, shape, F32))

        def sem(name):
            return nc.alloc_semaphore(name)

        MC = MD // P
        x = sb("e_x", [P, 2, C])
        x_t = sb("e_x_t", [P, 2, CC, P])
        h = sb("e_h", [P, 2, MD])
        h_t = sb("e_h_t", [P, 2, MC, P])
        y = sb("e_y", [P, 2, C])
        xt_p = ps("e_xt_p", [P, 512])
        ht_p = ps("e_ht_p", [P, MC, P])
        gate_p = [ps(f"e_gate_p{i}", [P, MD]) for i in range(2)]
        up_p = [ps(f"e_up_p{i}", [P, MD]) for i in range(2)]
        y_p = [ps(f"e_y_p{i}", [P, 512]) for i in range(2)]
        ld = [sem(f"e_ld{i}") for i in range(2)]
        stored = [sem(f"e_stored{i}") for i in range(2)]
        xt, xt_ok, gate_m, up_m, silu_ok, h_ok, ht, ht_ok, y_m, y_ok = (
            sem("e_" + n) for n in "xt xt_ok gate_m up_m silu_ok h_ok ht ht_ok y_m y_ok".split())

        def wait(eng, sem_, value):
            if not (isinstance(value, int) and value <= 0):
                eng.wait_ge(sem_, value)

        def tiles(eng, body, experts_of=lambda i: None):
            def pair(i, before, after):
                j = [eng.snap(i * 2 + s) if not isinstance(i, int) else i * 2 + s for s in range(2)]
                e = experts_of(i)
                for s in range(2):
                    body(j[s], s, i, before or s == 1, after or s == 0, e)
            pair(0, False, True)
            with eng.Fori(1, SLOTT // 2 - 1) as i:
                pair(i, True, True)
            pair(SLOTT // 2 - 1, True, False)

        with nc.Block() as block:
            @block.sync
            def _(sp):
                def load(j, s, i, before, after, e):
                    wait(sp, xt, j - 1)
                    sp.dma_start(x[:, s], xs_d[bass.ds(j * P, P)]).then_inc(ld[s], 16)
                tiles(sp, load)

            @block.tensor
            def _(pe):
                pe.wait_ge(s_w13, 16 * NE * CC)
                pe.wait_ge(s_w2, 16 * 4)

                def experts_of(i):
                    packed = pe.value_load(pair_experts[0:1, bass.ds(i, 1)], min_val=0, max_val=NE ** 3 - 1)
                    return [pe.snap(packed % NE, min_val=0, max_val=NE - 1),
                            pe.snap(packed // NE % NE, min_val=0, max_val=NE - 1),
                            pe.snap(packed // (NE * NE), min_val=0, max_val=NE - 1)]

                def turn_x(j, s, k):
                    pe.wait_ge(ld[s], (k + 1) * 16)
                    wait(pe, xt_ok, j)
                    for c in range(CC):
                        last = pe.transpose(xt_p[:, c * P:(c + 1) * P], x[:, s, c * P:(c + 1) * P], ident[:])
                    last.then_inc(xt, 1)

                def up_or_gate(bank, s, half, e):
                    for c in range(CC):
                        last = pe.matmul(bank[:], x_t[:, s, c], w13[:, bass.ds(e * (CC * 2 * MD) + (c * 2 + half) * MD, MD)],
                                         start=c == 0, stop=c == CC - 1)
                    return last

                def turn_hidden(j, s):
                    wait(pe, h_ok, j + 1)
                    wait(pe, ht_ok, j)
                    for m in range(MC):
                        last = pe.transpose(ht_p[:, m], h[:, s, m * P:(m + 1) * P], ident[:])
                    last.then_inc(ht, 1)

                def down(j, s, e):
                    wait(pe, ht_ok, j + 1)
                    wait(pe, y_ok, j - 1)
                    for m in range(MC):
                        last = pe.matmul(y_p[s][:, 0:C], h_t[:, s, m], w2[:, bass.ds(e * MC + m, 1)].rearrange("p o n -> p (o n)"),
                                         start=m == 0, stop=m == MC - 1)
                    last.then_inc(y_m, 1)

                def tile(j, s, i, before, after, e):
                    wait(pe, xt_ok, j + 1)
                    wait(pe, h_ok, j - 1)
                    up_or_gate(gate_p[s], s, 0, e[s + 1]).then_inc(gate_m, 1)
                    if before:
                        turn_hidden(j - 1, 1 - s)
                    up_or_gate(up_p[s], s, 1, e[s + 1]).then_inc(up_m, 1)
                    if after:
                        turn_x(j + 1, 1 - s, i + s)
                    if before:
                        down(j - 1, 1 - s, e[s])

                turn_x(0, 0, 0)
                tiles(pe, tile, experts_of)
                turn_hidden(SLOTT - 1, 1)
                down(SLOTT - 1, 1, experts_of(SLOTT // 2 - 1)[2])

            @block.scalar
            def _(act):
                for s in range(2):
                    act.sem_inc(stored[s], 16)

                def leave(j, s, k):
                    act.wait_ge(y_m, j + 1)
                    act.wait_ge(stored[s], (k + 1) * 16)
                    act.copy(y[:, s], y_p[s][:, 0:C]).then_inc(y_ok, 1)
                    act.wait_ge(y_ok, j + 1)
                    act.dma_start(ys_d[bass.ds(j * P, P)], y[:, s]).then_inc(stored[s], 16)

                def tile(j, s, i, before, after, e):
                    act.wait_ge(gate_m, j + 1)
                    wait(act, ht, j - 1)
                    act.activation(h[:, s], gate_p[s][:], ACT.Silu).then_inc(silu_ok, 1)
                    if before:
                        leave(j - 1, 1 - s, i + s - 1)

                tiles(act, tile)
                leave(SLOTT - 1, 1, SLOTT // 2 - 1)
                for s in range(2):
                    act.wait_ge(stored[s], 16 * (SLOTT // 2 + 1))

            @block.vector
            def _(dve):
                def copy_x(j, s):
                    dve.wait_ge(xt, j + 1)
                    wait(dve, up_m, j - 1)
                    dve.tensor_copy(x_t[:, s].rearrange("p c n -> p (c n)"), xt_p[:, 0:C]).then_inc(xt_ok, 1)

                def copy_hidden(j, s):
                    dve.wait_ge(ht, j + 1)
                    wait(dve, y_m, j - 1)
                    dve.tensor_copy(h_t[:, s], ht_p[:]).then_inc(ht_ok, 1)

                def tile(j, s, i, before, after, e):
                    if before:
                        copy_hidden(j - 1, 1 - s)
                    dve.wait_ge(silu_ok, j + 1)
                    dve.wait_ge(up_m, j + 1)
                    dve.tensor_tensor(h[:, s], up_p[s][:], h[:, s], ALU.mult).then_inc(h_ok, 1)
                    if after:
                        copy_x(j + 1, 1 - s)

                copy_x(0, 0)
                tiles(dve, tile)
                copy_hidden(SLOTT - 1, 1)


def combine(nc, x2_d, slots, gates, ys_d, out):
    ctx = ExitStack()
    with ctx:
        def sb(name, shape, dt=F32):
            return ctx.enter_context(nc.sbuf_tensor(name, shape, dt))

        def sem(name):
            return nc.alloc_semaphore(name)

        SL = 4
        at = sb("f_at", [P, SL, 2, 1], U32)
        ya = [[sb(f"f_y{s}{k}", [P, C]) for k in range(2)] for s in range(SL)]
        x2 = sb("f_x2", [P, SL, C])
        acc = sb("f_acc", [P, SL, C])
        bn6 = sb("f_bn6", [P, SL, 6])
        mv = sb("f_mv", [P, SL, 2])
        rstd = sb("f_rstd", [P, SL, 1])
        std = sb("f_std", [P, SL, 1])
        eps = sb("f_eps", [P, 1])
        res = sb("f_res", [P, SL, C])
        got = [sem(f"f_got{i}") for i in range(SL)]
        ld = [sem(f"f_ld{i}") for i in range(SL)]
        stored = [sem(f"f_stored{i}") for i in range(SL)]
        passed, at_go = sem("f_passed"), sem("f_at_go")
        at_ok, acc0, acc1, bn_ok, mv_ok, std_ok, rstd_ok, res_ok, eps_ok = (
            sem("f_" + n) for n in "at_ok acc0 acc1 bn_ok mv_ok std_ok rstd_ok res_ok eps_ok".split())
        out_v = out.rearrange("b t c -> (b t) c")

        def wait(eng, sem_, value):
            if not (isinstance(value, int) and value <= 0):
                eng.wait_ge(sem_, value)

        def rounds(eng, body):
            body(0, 0, True)
            with eng.Fori(1, NT // SL - 1) as i:
                body(eng.snap(i * SL), i, True)
            body(NT - SL, NT // SL - 1, False)

        with nc.Block() as block:
            @block.gpsimd
            def _(pool):
                def gather(n, i, more):
                    for s in range(SL):
                        wait(pool, acc1, n + s + 1 - SL)
                        pool.wait_ge(at_ok, n + s + 1)
                        pool.sem_inc(at_go, 1)
                        for k in range(2):
                            pool.indirect_dma_start(ya[s][k][:], None, ys_d, bass.IndirectOffsetOnAxis(at[:, s, k], 0)).then_inc(got[s], 16)
                rounds(pool, gather)

            @block.vector
            def _(dve):
                dve.memset(eps[:], EPS).then_inc(eps_ok, 1)

                def pick(n, s):
                    dve.tensor_copy(at[:, s], slots[:, :, bass.ds(n + s, 1)]).then_inc(at_ok, 1)

                def add(n, i, more):
                    for s in range(SL):
                        dve.wait_ge(got[s], (i + 1) * 32)
                        if more:
                            pick(n + SL, s)
                        dve.wait_ge(ld[s], (i + 1) * 16)
                        wait(dve, res_ok, n + s + 1 - SL)
                        dve.scalar_tensor_tensor(acc[:, s], ya[s][0][:], gates[:, 0, bass.ds(n + s, 1)], x2[:, s], ALU.mult, ALU.add).then_inc(acc0, 1)
                        dve.wait_ge(acc0, n + s + 1)
                        dve.scalar_tensor_tensor(acc[:, s], ya[s][1][:], gates[:, 1, bass.ds(n + s, 1)], acc[:, s], ALU.mult, ALU.add).then_inc(acc1, 1)
                        if s % 2:
                            for r in (s - 1, s):
                                dve.wait_ge(acc1, n + r + 1)
                                dve.bn_stats(bn6[:, r], acc[:, r]).then_inc(bn_ok, 1)
                            for r in (s - 1, s):
                                dve.wait_ge(bn_ok, n + r + 1)
                                dve.sem_inc(passed, 1)
                                dve.bn_aggr(mv[:, r], bn6[:, r]).then_inc(mv_ok, 1)
                            for r in (s - 1, s):
                                dve.wait_ge(std_ok, n + r + 1)
                                dve.reciprocal(rstd[:, r], std[:, r]).then_inc(rstd_ok, 1)
                            for r in (s - 1, s):
                                dve.wait_ge(rstd_ok, n + r + 1)
                                wait(dve, stored[r], i * 16)
                                dve.tensor_scalar(res[:, r], acc[:, r], mv[:, r, 0:1], rstd[:, r], ALU.subtract, ALU.mult).then_inc(res_ok, 1)
                for s in range(SL):
                    pick(0, s)
                rounds(dve, add)

            @block.scalar
            def _(act):
                act.wait_ge(eps_ok, 1)

                def std_of(n, i, more):
                    for s in range(SL):
                        act.wait_ge(mv_ok, n + s + 1)
                        act.activation(std[:, s], mv[:, s, 1:2], ACT.Sqrt, bias=eps[:]).then_inc(std_ok, 1)
                rounds(act, std_of)

            @block.sync
            def _(sp):
                def load(n, s):
                    wait(sp, acc0, n + s + 1 - SL)
                    sp.dma_start(x2[:, s], x2_d[bass.ds((n + s) * P, P)]).then_inc(ld[s], 16)

                def store(n, i, more):
                    for s in range(SL):
                        if more:
                            load(n + SL, s)
                        sp.wait_ge(res_ok, n + s + 1)
                        sp.dma_start(out_v[bass.ds((n + s) * P, P)], res[:, s]).then_inc(stored[s], 16)
                for s in range(SL):
                    load(0, s)
                rounds(sp, store)
                for s in range(SL):
                    sp.wait_ge(stored[s], NT // SL * 16)


_INS = ["x", "ctx_512"] + ["L0_attn_" + n for n in (
    "x_r x_w x_k x_v x_a x_g k_k k_a r_k W_r W_k W_v W_o w_lora_a w_lora_b w_lora_bias a_lora_a a_lora_b "
    "a_lora_bias g_lora_a g_lora_b g_lora_bias gn_weight gn_bias").split()] + [
    "L0_xattn_" + n for n in "Wq bq Wk bk Wv bv Wo bo".split()] + [
    "L0_ffn_" + n for n in "moe_router moe_w13 moe_w2".split()]
_UNUSED = {"L0_attn_x_g"}


def kernel(**inputs):
    import numpy as _np
    import concourse.bacc as _bacc
    from concourse import mybir as _mybir
    from concourse.bass_utils import run_bass_kernel_spmd as _run

    nc = _bacc.Bacc("TRN2", target_bir_lowering=False, num_devices=1)
    arrays, aps = {}, {}
    for name in _INS:
        if name in _UNUSED:
            continue
        a = _np.ascontiguousarray(inputs[name])
        arrays[f"in_{name}_dram"] = a
        aps[name] = nc.dram_tensor(f"in_{name}_dram", a.shape, _mybir.dt.from_np(a.dtype), kind="ExternalInput").ap()
    out = nc.dram_tensor("out_0_dram", (B, T, C), F32, kind="ExternalOutput").ap()
    decoder_kernel(nc, aps, out)
    r = _run(nc, [arrays], core_ids=[0])
    return r.results[0]["out_0_dram"]
```
